# Optimizing a Trainium2 kernel written in Bass

```python
import numpy as np
import jax
import jax.numpy as jnp

def _softmax(x, axis=-1):
    return jax.nn.softmax(x, axis=axis)

def _gelu(x):
    return jax.nn.gelu(x, approximate=True)

def _silu(x):
    return jax.nn.silu(x)

def _sigmoid(x):
    return jax.nn.sigmoid(x)

def _layernorm(x, axis=-1, eps=1e-05):
    m = jnp.mean(x, axis=axis, keepdims=True)
    v = jnp.var(x, axis=axis, keepdims=True)
    return (x - m) / jnp.sqrt(v + eps)

def _scatter_add(tgt, idx, src, axis=0):
    return tgt.at[idx].add(src)

def _segment_sum(src, seg, n):
    return jax.ops.segment_sum(src, seg, n)
kernel_name = 'mk_prb_d1_jaxref_r4_9bc277'

def setup_inputs(seed: int=0):
    np.random.seed(seed)
    _w = jnp.asarray

    def _L0_attn_setup():
        import jax, jax.numpy as jnp
        import numpy as np
        B, S, E = (4, 512, 256)
        HIDDEN = 256
        HEADS = 16
        key = jax.random.key(seed)
        k0, k1, k2, k3, k4 = jax.random.split(key, 5)
        inputs = jax.random.normal(k0, (B, S, E), dtype=jnp.float32)
        W_qkv = jax.random.normal(k1, (E, 3 * HIDDEN), dtype=jnp.float32) * 0.02
        b_qkv = jnp.zeros((3 * HIDDEN,), dtype=jnp.float32)
        W_out = jax.random.normal(k2, (HIDDEN, HIDDEN), dtype=jnp.float32) * 0.02
        b_out = jnp.zeros((HIDDEN,), dtype=jnp.float32)
        return {'inputs': inputs, 'W_qkv': W_qkv, 'b_qkv': b_qkv, 'W_out': W_out, 'b_out': b_out}
    _L0_attn_in = _L0_attn_setup()

    def _L0_ffn_setup():
        import jax, jax.numpy as jnp
        import numpy as np
        from functools import partial
        DIM = 256
        LIGHT_HID = 128
        HEAVY_HID = 1024
        NUM_HEAVY = 256
        N_ITERS = 50
        K_ROUTE = 8.0
        EPS = 0.1

        def rms_norm(x, gamma):
            norm = jnp.linalg.norm(x, axis=-1, keepdims=True)
            normed = x / jnp.maximum(norm, 1e-12)
            return normed * x.shape[-1] ** 0.5 * gamma

        def ffn(x, gamma, w1, b1, w2, b2):
            h = rms_norm(x, gamma)
            h = jax.nn.gelu(h @ w1 + b1, approximate=False)
            return h @ w2 + b2

        def coor_descent_route(x, routing_token, num_tokens):
            s = jnp.einsum('bnd,d->bn', x, routing_token)
            constant = EPS * jnp.log(jnp.asarray(K_ROUTE, dtype=s.dtype))
            b0 = -jax.nn.relu(s)
            a0 = jnp.zeros((s.shape[0], 1), dtype=s.dtype)

            def step(carry, _):
                a_prev, b = carry
                a = constant - EPS * jax.nn.logsumexp((s + b) / EPS, axis=-1, keepdims=True)
                b = -jax.nn.relu(s + a)
                return ((a, b), None)
            (a, b), _ = jax.lax.scan(step, (a0, b0), None, length=N_ITERS)
            scores = jnp.exp((s + a + b) / EPS)
            sel_scores, sel_idx = jax.lax.top_k(scores, num_tokens)
            sel_scores = sel_scores + jax.lax.stop_gradient(1.0 - sel_scores)
            return (sel_scores, sel_idx)
        key = jax.random.key(seed)
        ks = jax.random.split(key, 12)

        def lin(k, fan_in, fan_out):
            lim = 1.0 / np.sqrt(fan_in)
            kw, kb = jax.random.split(k)
            w = jax.random.uniform(kw, (fan_in, fan_out), jnp.float32, -lim, lim)
            b = jax.random.uniform(kb, (fan_out,), jnp.float32, -lim, lim)
            return (w, b)
        x = jax.random.normal(ks[0], (4, 2048, DIM), jnp.float32)
        routing_token = jax.random.normal(ks[1], (DIM,), jnp.float32)
        gamma_light = jnp.ones((DIM,), jnp.float32)
        w1_l, b1_l = lin(ks[2], DIM, LIGHT_HID)
        w2_l, b2_l = lin(ks[3], LIGHT_HID, DIM)
        gamma_heavy = jnp.ones((DIM,), jnp.float32)
        w1_h, b1_h = lin(ks[4], DIM, HEAVY_HID)
        w2_h, b2_h = lin(ks[5], HEAVY_HID, DIM)
        return dict(x=x, routing_token=routing_token, gamma_light=gamma_light, w1_light=w1_l, b1_light=b1_l, w2_light=w2_l, b2_light=b2_l, gamma_heavy=gamma_heavy, w1_heavy=w1_h, b1_heavy=b1_h, w2_heavy=w2_h, b2_heavy=b2_h)
    _L0_ffn_in = _L0_ffn_setup()
    _d = {'L0_attn_inputs': _L0_attn_in['inputs'], 'L0_attn_W_qkv': _L0_attn_in['W_qkv'], 'L0_attn_b_qkv': _L0_attn_in['b_qkv'], 'L0_attn_W_out': _L0_attn_in['W_out'], 'L0_attn_b_out': _L0_attn_in['b_out'], 'L0_ffn_routing_token': _L0_ffn_in['routing_token'], 'L0_ffn_gamma_light': _L0_ffn_in['gamma_light'], 'L0_ffn_w1_light': _L0_ffn_in['w1_light'], 'L0_ffn_b1_light': _L0_ffn_in['b1_light'], 'L0_ffn_w2_light': _L0_ffn_in['w2_light'], 'L0_ffn_b2_light': _L0_ffn_in['b2_light'], 'L0_ffn_gamma_heavy': _L0_ffn_in['gamma_heavy'], 'L0_ffn_w1_heavy': _L0_ffn_in['w1_heavy'], 'L0_ffn_b1_heavy': _L0_ffn_in['b1_heavy'], 'L0_ffn_w2_heavy': _L0_ffn_in['w2_heavy'], 'L0_ffn_b2_heavy': _L0_ffn_in['b2_heavy']}
    _x0 = _d['L0_attn_inputs']
    _d['L0_attn_inputs'] = jax.random.normal(jax.random.fold_in(jax.random.key(seed), 1), (4, 1024, 256), dtype=_x0.dtype)
    del _x0
    return _d

def reference(L0_attn_inputs, L0_attn_W_qkv, L0_attn_b_qkv, L0_attn_W_out, L0_attn_b_out, L0_ffn_routing_token, L0_ffn_gamma_light, L0_ffn_w1_light, L0_ffn_b1_light, L0_ffn_w2_light, L0_ffn_b2_light, L0_ffn_gamma_heavy, L0_ffn_w1_heavy, L0_ffn_b1_heavy, L0_ffn_w2_heavy, L0_ffn_b2_heavy):

    def _L0_attn_ref(inputs, W_qkv, b_qkv, W_out, b_out):
        import jax, jax.numpy as jnp
        import numpy as np
        B, S, E = (4, 512, 256)
        HIDDEN = 256
        HEADS = 16
        Bv, Sv, Ev = inputs.shape
        x = inputs @ W_qkv + b_qkv
        x = x.reshape(Bv, HEADS, Sv, -1)
        q, k, v = jnp.split(x, 3, axis=-1)
        scale = (2 * HIDDEN) ** (-0.5)
        qk = jnp.einsum('bhse,bhte->bhst', q, k) * scale
        mask = jnp.triu(jnp.full((Sv, Sv), -jnp.inf, dtype=qk.dtype), k=1)
        attn = jax.nn.softmax(qk + mask, axis=-1)
        sa = jnp.einsum('bhst,bhte->bhse', attn, v).reshape(Bv, Sv, -1)
        return sa @ W_out + b_out

    def _L0_ffn_ref(x, routing_token, gamma_light, w1_light, b1_light, w2_light, b2_light, gamma_heavy, w1_heavy, b1_heavy, w2_heavy, b2_heavy):
        import jax, jax.numpy as jnp
        import numpy as np
        from functools import partial
        DIM = 256
        LIGHT_HID = 128
        HEAVY_HID = 1024
        NUM_HEAVY = 256
        N_ITERS = 50
        K_ROUTE = 8.0
        EPS = 0.1

        def rms_norm(x, gamma):
            norm = jnp.linalg.norm(x, axis=-1, keepdims=True)
            normed = x / jnp.maximum(norm, 1e-12)
            return normed * x.shape[-1] ** 0.5 * gamma

        def ffn(x, gamma, w1, b1, w2, b2):
            h = rms_norm(x, gamma)
            h = jax.nn.gelu(h @ w1 + b1, approximate=False)
            return h @ w2 + b2

        def coor_descent_route(x, routing_token, num_tokens):
            s = jnp.einsum('bnd,d->bn', x, routing_token)
            constant = EPS * jnp.log(jnp.asarray(K_ROUTE, dtype=s.dtype))
            b0 = -jax.nn.relu(s)
            a0 = jnp.zeros((s.shape[0], 1), dtype=s.dtype)

            def step(carry, _):
                a_prev, b = carry
                a = constant - EPS * jax.nn.logsumexp((s + b) / EPS, axis=-1, keepdims=True)
                b = -jax.nn.relu(s + a)
                return ((a, b), None)
            (a, b), _ = jax.lax.scan(step, (a0, b0), None, length=N_ITERS)
            scores = jnp.exp((s + a + b) / EPS)
            sel_scores, sel_idx = jax.lax.top_k(scores, num_tokens)
            sel_scores = sel_scores + jax.lax.stop_gradient(1.0 - sel_scores)
            return (sel_scores, sel_idx)
        bsz = x.shape[0]
        light_out = ffn(x, gamma_light, w1_light, b1_light, w2_light, b2_light)
        sel_scores, sel_idx = coor_descent_route(x, routing_token, NUM_HEAVY)
        batch_range = jnp.arange(bsz)[:, None]
        routed = x[batch_range, sel_idx]
        routed_out = ffn(routed, gamma_heavy, w1_heavy, b1_heavy, w2_heavy, b2_heavy)
        routed_out = routed_out * sel_scores[..., None]
        heavy_out = jnp.zeros_like(x).at[batch_range, sel_idx].set(routed_out)
        return light_out + heavy_out
    x = L0_attn_inputs
    xn = _layernorm(x, axis=-1)
    x = x + _L0_attn_ref(xn, L0_attn_W_qkv, L0_attn_b_qkv, L0_attn_W_out, L0_attn_b_out) + _L0_ffn_ref(xn, L0_ffn_routing_token, L0_ffn_gamma_light, L0_ffn_w1_light, L0_ffn_b1_light, L0_ffn_w2_light, L0_ffn_b2_light, L0_ffn_gamma_heavy, L0_ffn_w1_heavy, L0_ffn_b1_heavy, L0_ffn_w2_heavy, L0_ffn_b2_heavy)
    return x

_drawn_inputs = setup_inputs


def setup_inputs(seed=0):
    import zlib

    import numpy as np

    out = dict(_drawn_inputs(seed))
    spreads = {'L0_attn_b_qkv': (0.0, 0.8),
     'L0_attn_b_out': (0.0, 0.1),
     'L0_ffn_gamma_light': (1.0, 0.2),
     'L0_ffn_gamma_heavy': (1.0, 0.6)}
    factors = {'L0_attn_W_qkv': 6.65,
     'L0_attn_W_out': 4.539,
     'L0_ffn_b1_light': 4.593,
     'L0_ffn_b1_heavy': 8.0,
     'L0_ffn_b2_heavy': 6.806}
    for name, (base, spread) in spreads.items():
        noise = np.random.default_rng([zlib.crc32(name.encode()), seed]).standard_normal(out[name].shape)
        drawn = base * np.exp(spread * noise) if base else spread * noise
        out[name] = jnp.asarray(drawn.astype(out[name].dtype))
    for name, factor in factors.items():
        out[name] = (out[name] * factor).astype(out[name].dtype)
    return out
```

```python
from contextlib import ExitStack
import math

import concourse.bass as bass
from concourse import mybir

F32 = mybir.dt.float32
BF16 = mybir.dt.bfloat16
I32 = mybir.dt.int32
ALU = mybir.AluOpType
ACT = mybir.ActivationFunctionType
AX = mybir.AxisListType

P = 128
EPS_LN = 1e-5
EPS_ROUTE = 0.1
K_ROUTE = 8.0
N_ITERS = 50
NUM_HEAVY = 256
EXP_FLOOR = -87.33654
MASKED = -3.0e38
VAR_FLOOR = 1e-36


def ring_orders():
    C = lambda c, a, b: [("C", c, k) for k in range(a, b)]
    T = lambda c: [("T", c, 0), ("T", c, 1)]
    first = (T(0) + T(1) + C(0, 0, 12) + T(2) + C(1, 0, 6) + [("MT", 0)] + C(1, 6, 12) + T(3)
             + C(2, 0, 6) + [("MT", 1)] + C(2, 6, 12) + C(3, 0, 6) + [("MT", 2)] + C(3, 6, 12))
    first += [("NOP",)] * (len(first) % 2)
    steady = (T(0) + [("MT", 3)] + T(1) + C(0, 0, 6) + [("OT", 0), ("OT", 1)] + C(0, 6, 10) + [("R", 0)]
              + C(0, 10, 12) + T(2) + C(1, 0, 6) + [("MT", 0)] + C(1, 6, 10) + [("R", 1)] + C(1, 10, 12) + T(3)
              + C(2, 0, 6) + [("MT", 1)] + C(2, 6, 10) + [("R", 2)] + C(2, 10, 12)
              + C(3, 0, 6) + [("MT", 2)] + C(3, 6, 12))
    last = [("MT", 3), ("OT", 0), ("OT", 1)] + [("R", k) for k in range(5)]
    return first, steady, last


CHUNKS = [(qb, k0, min(512, (qb + 1) * P - k0), k0 + 512 >= (qb + 1) * P)
          for qb in range(8) for k0 in range(0, (qb + 1) * P, 512)]
EXPS = ([(kb, (c,)) for kb in range(4) for c in range(4)] + [(4, (0, 1)), (4, (2, 3)), (5, (0, 1)), (5, (2, 3)),
        (6, (0, 1, 2, 3)), (7, (0, 1, 2, 3))])
EXPS_OF = [sum(1 for kb, _ in EXPS if kb <= k) for k in range(8)]


def merge(ring, back):
    ring_cost = {"T": 0.7, "C": 0.45, "MT": 0.25, "OT": 0.6, "R": 0.5, "NOP": 0}
    back_cost = {"E": 1.1, "PV": 0.0}
    tr = sum(ring_cost[i[0]] for i in ring)
    tb = sum(back_cost[i[0]] for i in back)
    out, a, b = [], 0.0, 0.0
    r, k = list(ring), list(back)
    while r or k:
        held = r and r[0][0] == "OT" and ("PV", 7, -1) in k
        if k and (not r or held or b / tb <= a / tr):
            b += back_cost[k[0][0]]
            out.append(k.pop(0))
        else:
            a += ring_cost[r[0][0]]
            out.append(r.pop(0))
    return out


def back_order(previous):
    out = []
    for j, (kb, heads) in enumerate(EXPS):
        if previous and j == 2:
            out += [("PV", 6, -1), ("PV", 7, -1)]
        out.append(("E", j))
        if kb >= 1 and EXPS_OF[kb] == j + 1:
            out.append(("PV", kb - 1, 0))
    return [i for i in out if not (i[0] == "PV" and i[1] >= 6 and i[2] == 0)]


def timeline(ring, late, load):
    order = merge(ring, back_order(late))
    out = [("MAX", 3)]
    exps = routes = 0
    subs = [("SUB", k) for k in range(5)] if load else []
    for item in order:
        if item[0] == "OT" and not late:
            item = ("SKIP", item[1])
        if item[0] == "R":
            at = len(out)
            n = 0
            while n < 2 and at > 1 and out[at - 1][0] != "RA":
                at -= 1
                n += out[at][0] == "E"
            out.insert(at, ("RX", item[1]))
            out += [item, ("RA", item[1])]
            continue
        out.append(item)
        if item == ("PV", 7, -1):
            out += [("OUT",), ("VALUES",)]
        if item == ("E", 1) and not late:
            out += [("VALUES",)]
        if item[0] == "C" and item[2] == 11 and item[1] < 3:
            out.append(("MAX", item[1]))
        if item[0] == "E":
            exps += 1
            if exps == 5 and load:
                out.append(("CAST",))
            if exps in EXPS_OF:
                out.append(("CAUSAL", EXPS_OF.index(exps)))
            if exps in (7, 9, 11, 13, 15) and subs:
                out.append(subs.pop(0))
    return out


def wait_apart(engine, semaphore, value):
    engine.wait_ge(semaphore, value)
    if not isinstance(value, int):
        engine.nop(nofuse=True)


def layer_kernel(nc, x, W_qkv, b_qkv, W_out, b_out, rtok, g_l, w1_l, b1_l, w2_l, b2_l, g_h, w1_h, b1_h, w2_h, b2_h, out):
    B, S, E = x.shape
    T = B * S
    NT = T // P
    QKV = W_qkv.shape[1]
    HEADS = 16
    D = QKV // HEADS // 3
    SLOTS = HEADS
    NQ = T // 256
    HID_L, HID_H = w1_l.shape[1], w1_h.shape[1]
    KE = E // P
    NHC = HID_H // P
    SCALE = float((2 * E) ** -0.5)
    C_ROUTE = EPS_ROUTE * math.log(K_ROUTE)
    NSLOT = B * NUM_HEAVY // P
    HW = QKV // 2
    W = 6 * D

    xf = x.rearrange("b s e -> (b s) e")
    of = out.rearrange("b s e -> (b s) e")

    ring_first, ring_steady, ring_last = ring_orders()
    L0, L = len(ring_first), len(ring_steady)

    def ring_at(step, item):
        if isinstance(step, int) and step == -1:
            at = ring_first.index(item)
            return at % 2, at // 2
        if isinstance(step, int):
            at = L0 + L * (NQ - 1) + ring_last.index(item)
            return at % 2, at // 2
        i, u = step
        at = L0 + L * u + ring_steady.index(item)
        return at % 2, L * i + at // 2

    NE = len(EXPS)
    ST = 10
    RK_AT = [0]
    for k in range(8):
        RK_AT.append(RK_AT[-1] + (3 if k else 2))
    RK = 2 + RK_AT[8] + 2
    N_DCONST, N_CONST, N_FOLD = 11, 13, 5

    def final_ot(h):
        at = L0 + L * (NQ - 1) + len(ring_last) + h
        return at % 2, at // 2

    with ExitStack() as ctx:
        def sb(name, shape, dt=F32):
            return ctx.enter_context(nc.sbuf_tensor(name, shape, dt))

        def sem(name):
            return ctx.enter_context(nc.semaphore(name))

        qkv_d = nc.dram_tensor("qkv_d", [T, QKV], F32).ap()
        sa_d = nc.dram_tensor("sa_d", [T, E], F32).ap()
        s_d = nc.dram_tensor("s_d", [T], F32).ap()
        na_d = nc.dram_tensor("na_d", [P], F32).ap()

        psM = ctx.enter_context(nc.psum_tensor("psM", [P, 2, 512], F32))
        psE = ctx.enter_context(nc.psum_tensor("psE", [P, 2, 2, 512], F32))
        psO = ctx.enter_context(nc.psum_tensor("psO", [P, 2, 512], F32))

        ident = sb("ident", [P, P])
        blockones = sb("blockones", [P, P])
        maskrow = sb("maskrow", [P, 512])
        below = sb("below", [P, P])
        iota256 = sb("iota256", [P, NUM_HEAVY])
        iota_i = sb("iota_i", [P, NUM_HEAVY], I32)
        tokid_i = sb("tokid_i", [P, 2, NT], I32)
        tokid = sb("tokid", [P, 2, NT], BF16)
        shared = sb("shared", [P, KE * (QKV + 1) + 3 * QKV])
        a0, a1 = KE * (QKV + 1), KE * (QKV + 1) + QKV
        w_qkv = shared[:, 0:a0].rearrange("p (k n) -> p k n", k=KE)
        bias_qkv = shared[:, a0:a1]
        qkvs = shared[:, a1:a1 + 2 * QKV].rearrange("p (b n) -> p b n", b=2)
        w2h = shared[:, 0:NHC * E].rearrange("p (c n) -> p c n", n=E)
        a2 = NHC * E
        wout = shared[:, a2:a2 + KE * E].rearrange("p (k n) -> p k n", n=E)
        w2l = shared[:, a2 + 2 * E:a2 + 3 * E]
        bias_o = shared[:, a2 + 3 * E:a2 + 5 * E].rearrange("p (k n) -> p k n", n=E)
        bias_h = shared[:, a2 + 5 * E:a2 + 6 * E]
        rt_row = shared[:, a2 + 6 * E:a2 + 7 * E]
        xrT = sb("xrT", [P, KE, T])
        xT = sb("xT", [P, 2, KE, P])
        gdot = sb("gdot", [P, NSLOT])
        gu = sb("gu", [P, NSLOT])
        gw = sb("gw", [P, NSLOT])
        gscore = sb("gscore", [P, NSLOT])
        skipped = sb("skipped", [24, 2])
        xr = sb("xr", [P, 2, E])
        bn6 = sb("bn6", [P, NT, 6])
        mv = sb("mv", [P, NT, 2])
        veps = sb("veps", [P, 2, NT])
        halfpow = sb("halfpow", [P, 2, NT])
        roots = sb("roots", [P, 2, NT])
        nrm = sb("nrm", [P, NT])
        rnrm = sb("rnrm", [P, NT])
        xscale = sb("xscale", [P, NT])
        xshift = sb("xshift", [P, NT])
        unscale = sb("unscale", [P, NT])
        s_tok = sb("s_tok", [P, NT])
        strips = sb("strips", [P, 10752])
        QT = sb("QT", [P, 2, 4096])
        parts = sb("parts", [P, 2, 32 * W])
        pm = sb("pm", [P, 2, 32, 3 * D])
        r1 = sb("r1", [P, 32, 2 * D])
        vext = sb("vext", [P, 2, 32, 32])
        osb = sb("osb", [P, 1024])
        rden = sb("rden", [P, 2, 4, 4])
        pmo = sb("pmo", [P, 2, 4, 8, D])
        mx = sb("mx", [P, 4, 8, 2])
        nm = sb("nm", [P, 4, 8])
        nmr = sb("nmr", [P, 4, 8])
        mW = sb("mW", [P, 4, 24])
        mT = sb("mT", [24, 4, P])
        rs = sb("rs", [P, 32])
        smax = sb("smax", [P, 1])
        rz = sb("rz", [P, 32])
        re = sb("re", [P, 32])
        rsum = sb("rsum", [P, 1])
        lns = sb("lns", [P, 1])
        rm = sb("rm", [P, 2])
        na = sb("na", [P, 1])
        na_all = sb("na_all", [P, B])
        nlo_all = sb("nlo_all", [P, B])
        w1l = sb("w1l", [P, KE, HID_L])
        w1h = sb("w1h", [P, KE, HID_H])
        b1l = sb("b1l", [P, 1])
        b1h = sb("b1h", [P, NHC])
        gl = sb("gl", [P, KE])
        gh = sb("gh", [P, KE])
        rank3 = sb("rank3", [P, 3, 8])
        rank = sb("rank", [P, 8])
        keyc = sb("keyc", [P, 8])
        idxf = sb("idxf", [P, NSLOT])
        idx = sb("idx", [P, NSLOT], I32)

        xs = strips[:, 0:NT * E].rearrange("p (t e) -> p t e", e=E)
        partsb = parts[:, :, :].rearrange("p b w -> p (b w)").bitcast(BF16).rearrange(
            "p (b n g e t) -> p b n g e t", b=2, n=32, g=6, t=2)
        QTb = QT[:, :, :].rearrange("p b w -> p (b w)").bitcast(BF16).rearrange("p (b w t) -> p b w t", b=2, t=2)
        mWb = mW[:, :, :].rearrange("p c w -> p (c w)").bitcast(BF16).rearrange(
            "p (c i n t) -> p c i n t", c=4, i=3, t=2)
        strip_at = {}
        for region, kbs in ((0, (0, 3, 6)), (4096, (1, 4, 7)), (4096 + 3584, (2, 5))):
            for kb in kbs:
                w = (8 - kb) * P
                strip_at[kb] = strips[:, region:region + 4 * w].rearrange("p (c w) -> p c w", c=4)

        sa_in = strips[:, 0:2048].rearrange("p (b t e) -> p b t e", b=2, e=E)
        x_in2 = strips[:, 2048:4096].rearrange("p (b t e) -> p b t e", b=2, e=E)
        saT = strips[:, 8192:8704].rearrange("p (b e) -> p b e", b=2)
        ob = QT[:, 0, 0:2048].rearrange("p (b t e) -> p b t e", b=2, e=E)
        hT = parts[:, 0, 0:1024].rearrange("p (b n) -> p b n", b=2)
        hotb = parts[:, :, :].rearrange("p b w -> p (b w)")[:, 2048:6144].bitcast(BF16).rearrange(
            "p (t n) -> p t n", n=NUM_HEAVY)
        keyr = osb
        junk = pmo[:, :, :, :, :].rearrange("p a c n d -> p (a c n d)")
        hidT = strips[:, 0:8192].rearrange("p (c n) -> p c n", n=NSLOT * P)
        xg = QT[:, 1, 0:2048].rearrange("p (t e) -> p t e", e=E)
        xgT = QT[:, 1, 2048:4096].rearrange("p (k n) -> p k n", k=KE)
        hv = vext[:, :, :, :].rearrange("p b n w -> p (b n w)").rearrange("p (t e) -> p t e", e=E)
        xgn = pm[:, :, :, :].rearrange("p b n w -> p (b n w)")[:, 0:2048].rearrange("p (t e) -> p t e", e=E)

        wd_in = sem("wd_in")
        x_in = [sem(f"x_in{g}") for g in range(4)]
        wa_in = sem("wa_in")
        wc_in = sem("wc_in")
        consts = sem("consts")
        dconst = sem("dconst")
        bn_done = sem("bn_done")
        stat_done = sem("stat_done")
        nrm_inv = sem("nrm_inv")
        xr_done = sem("xr_done")
        xT_ps = sem("xT_ps")
        xT_done = sem("xT_done")
        qkv_ps = sem("qkv_ps")
        qkv_done = sem("qkv_done")
        qkv_st = [sem(f"qkv_st{u}") for u in range(2)]
        s_st = sem("s_st")
        route_in = sem("route_in")
        smax_done = sem("smax_done")
        pm_in = [sem(f"pm_in{u}") for u in range(2)]
        cast_done = sem("cast_done")
        v_done = sem("v_done")
        split_done = sem("split_done")
        full = [sem(f"full{s}") for s in range(2)]
        free = [sem(f"free{s}") for s in range(2)]
        mx_done = sem("mx_done")
        nm_done = sem("nm_done")
        mw_done = sem("mw_done")
        m_in = [sem(f"m_in{c}") for c in range(4)]
        qk_ps = sem("qk_ps")
        exp_done = sem("exp_done")
        mask_done = sem("mask_done")
        pv_done = sem("pv_done")
        osb_done = sem("osb_done")
        rden_done = sem("rden_done")
        pmo_done = sem("pmo_done")
        sa_st = [sem(f"sa_st{u}") for u in range(2)]
        rz_done = sem("rz_done")
        re_done = sem("re_done")
        ln_done = sem("ln_done")
        fold_done = sem("fold_done")
        na_st = sem("na_st")
        na_in = sem("na_in")
        nlo_done = sem("nlo_done")
        c_in = [sem(f"c_in{u}") for u in range(2)]
        c_x = sem("c_x")
        h_ps = sem("h_ps")
        h_done = sem("h_done")
        saT_ps = sem("saT_ps")
        saT_done = sem("saT_done")
        o_ps = sem("o_ps")
        ob_done = sem("ob_done")
        out_st = [sem(f"out_st{u}") for u in range(2)]
        key_in = sem("key_in")
        rk = sem("rk")
        hot_done = sem("hot_done")
        idx_ps = sem("idx_ps")
        idx_done = sem("idx_done")
        g_in = [sem(f"g_in{t}") for t in range(NSLOT)]
        gx_done = sem("gx_done")
        gp_done = sem("gp_done")
        gs_done = sem("gs_done")
        gT_ps = sem("gT_ps")
        gT_done = sem("gT_done")
        hh_ps = sem("hh_ps")
        hh_done = sem("hh_done")
        ho_ps = sem("ho_ps")
        hv_half = sem("hv_half")
        hv_done = sem("hv_done")
        add_st = [sem(f"add_st{t}") for t in range(NSLOT)]
        group_of = sem("group_of")
        xc_st = [sem(f"xc_st{u}") for u in range(2)]
        c_x_in = [sem(f"c_x_in{u}") for u in range(2)]
        gn_done = sem("gn_done")
        gu_done = sem("gu_done")

        block = ctx.enter_context(nc.Block())

        @block.sync
        def _(sp):
            xt = xf.rearrange("(t p) e -> p t e", p=P)
            for g in range(4):
                sp.dma_start(xs[:, 8 * g:8 * g + 8, :], xt[:, 8 * g:8 * g + 8, :]).then_inc(x_in[g], 16)
                if g == 0:
                    sp.dma_start(w_qkv[:, :, 0:QKV], W_qkv.rearrange("(k p) n -> p k n", p=P)).then_inc(wa_in, 16)
                    sp.dma_start(w_qkv[:, :, QKV:QKV + 1], rtok.rearrange("(k p o) -> p k o", p=P, o=1), allow_slow_non_contiguous=True).then_inc(wa_in, 16)
                    sp.dma_start(bias_qkv, b_qkv.partition_broadcast(P)).then_inc(wa_in, 16)
            for dst, src in ((w1l[:, :, :], w1_l.rearrange("(k p) n -> p k n", p=P)),
                             (w1h[:, :, :], w1_h.rearrange("(k p) n -> p k n", p=P)),
                             (b1l[:, :], b1_l.rearrange("(p o) -> p o", o=1)),
                             (b1h[:, :], b1_h.rearrange("(k p) -> p k", p=P)),
                             (gl[:, :], g_l.rearrange("(k p) -> p k", p=P)),
                             (gh[:, :], g_h.rearrange("(k p) -> p k", p=P))):
                sp.dma_start(dst, src, allow_slow_non_contiguous=True).then_inc(wc_in, 16)

            def store_qkv(i, u):
                wait_apart(sp, xT_done, 2 * i + u + 1)
                sp.dma_start(xrT[:, :, bass.ds((2 * i + u) * P, P)], xT[:, u]).then_inc(xc_st[u], 16)
                wait_apart(sp, qkv_done, 2 * i + u + 1)
                sp.dma_start(qkv_d.rearrange("(t p) n -> p t n", p=P)[:, bass.ds(2 * i + u, 1), :],
                             qkvs[:, u:u + 1, :]).then_inc(qkv_st[u], 16)

            def load_pm(i, u):
                wait_apart(sp, qkv_st[0], 32 * i + 16 * u + 16)
                wait_apart(sp, qkv_st[1], 32 * i + 16 * u + 16)
                src = qkv_d.rearrange("(q n t) (j f) -> q (t j) n f", n=32, t=8, j=SLOTS)
                sp.dma_start(pm[:, u, :, :], src[bass.ds(2 * i + u, 1)].rearrange("a p n f -> (a p) n f")
                             ).then_inc(pm_in[u], 16)

            with sp.Fori(0, NT // 4) as i:
                for u in range(2):
                    store_qkv(i, u)
            load_pm(0, 0)
            load_pm(0, 1)
            with sp.Fori(NT // 4, NT // 2) as i:
                for u in range(2):
                    store_qkv(i, u)
            wait_apart(sp, qkv_done, NT)
            sp.dma_start(s_d.rearrange("(t p o) -> p t o", p=P, o=1), s_tok[:, :].unsqueeze(2), allow_slow_non_contiguous=True).then_inc(s_st, 16)
            wait_apart(sp, s_st, 16)
            sp.dma_start(rs[:, :], s_d.rearrange("(p n) -> p n", n=32)).then_inc(route_in, 16)
            for b in range(B):
                sp.dma_start(xs[32 * b:32 * b + 32, 0:4, :].rearrange("p t e -> p (t e)"),
                             s_d[b * S:(b + 1) * S].partition_broadcast(32)).then_inc(route_in, 16)

            wait_apart(sp, qkv_st[0], 16 * (NT // 2))
            wait_apart(sp, qkv_st[1], 16 * (NT // 2))
            for dst, src in ((w2l, w2_l), (wout, W_out.rearrange("(k p) n -> p k n", p=P)),
                             (w2h, w2_h.rearrange("(k p) n -> p k n", p=P)),
                             (bias_o[:, 0, :], b_out.partition_broadcast(P)), (bias_o[:, 1, :], b2_l.partition_broadcast(P)),
                             (bias_h, b2_h.partition_broadcast(P)), (rt_row, rtok.partition_broadcast(P))):
                sp.dma_start(dst, src).then_inc(wd_in, 16)

            def load_m(i, u, c):
                first = isinstance(i, int) and i == -1
                s, at = ring_at(-1 if first else (i, u), ("MT", c))
                wait_apart(sp, free[s], at + 1)
                fu = 0 if first else (u if c == 3 else 1 - u)
                sp.dma_start(QT[W:W + 3, fu, c * 1024:(c + 1) * 1024].rearrange("i (n p) -> i n p", p=P),
                             mT[:, c, :]).then_inc(m_in[c], 16)

            def store_sa(i, u, where):
                for h in range(2):
                    s, at = where(h)
                    wait_apart(sp, free[s], at + 1)
                dst = sa_d.rearrange("(q n t) (j f) -> q (t j) n f", n=32, t=8, j=SLOTS)
                sp.dma_start(dst[bass.ds(2 * i + u, 1)].rearrange("a p n f -> (a p) n f"),
                             pmo[:, u].rearrange("p c n f -> p (c n) f")).then_inc(sa_st[u], 16)

            wait_apart(sp, v_done, 1)
            wait_apart(sp, split_done, 5)
            load_pm(1, 0)
            for c in range(3):
                load_m(-1, 0, c)

            def step(i, u, late=True, load=True):
                load_m(i, u, 3)
                if late:
                    store_sa(i if u else i - 1, 1 - u, lambda h: ring_at((i, u), ("OT", h)))
                if load:
                    wait_apart(sp, v_done, 2 * i + u + 2)
                    wait_apart(sp, split_done, 5 * (2 * i + u + 2))
                    load_pm(i + 1 if u == 0 else i + 2, 1 - u)
                for c in range(3):
                    load_m(i, u, c)

            for u in range(2):
                sp.sem_inc(sa_st[u], 16)
            step(0, 0, late=False)
            step(0, 1)
            with sp.Fori(1, NQ // 2 - 2) as i:
                step(i, 0)
                step(i, 1)
            step(NQ // 2 - 2, 0)
            step(NQ // 2 - 2, 1, load=False)
            step(NQ // 2 - 1, 0, load=False)
            s, at = ring_at(NQ - 1, ("MT", 3))
            wait_apart(sp, free[s], at + 1)
            sp.dma_start(QT[W:W + 3, 1, 3 * 1024:4096].rearrange("i (n p) -> i n p", p=P), mT[:, 3, :]).then_inc(m_in[3], 16)
            store_sa(NQ // 2 - 1, 0, lambda h: ring_at(NQ - 1, ("OT", h)))
            wait_apart(sp, rz_done, N_ITERS * 4 + 1)
            sp.dma_start(na_d.rearrange("(p o) -> p o", o=1), na[:, :]).then_inc(na_st, 16)
            wait_apart(sp, na_st, 16)
            sp.dma_start(na_all[:, :], na_d.rearrange("(b g) -> g b", g=32)[0, :].partition_broadcast(P),
                         allow_slow_non_contiguous=True).then_inc(na_in, 16)
            store_sa(NQ // 2 - 1, 1, final_ot)

            wait_apart(sp, pv_done, 8 * NQ)
            for u in range(2):
                wait_apart(sp, sa_st[u], 16 * (NQ // 2 + 1))
            xb3 = xf.rearrange("(b t p) e -> b p t e", t=4, p=P)
            sb3 = sa_d.rearrange("(b t p) e -> b p t e", t=4, p=P)
            ob3 = of.rearrange("(b t p) e -> b p t e", t=4, p=P)

            def load_c(i, u):
                sp.dma_start(sa_in[:, u], sb3[bass.ds(2 * i + u, 1)].rearrange("a p t e -> (a p) t e")).then_inc(c_in[u], 16)
                sp.dma_start(x_in2[:, u], xb3[bass.ds(2 * i + u, 1)].rearrange("a p t e -> (a p) t e")).then_inc(c_x_in[u], 16)

            def load_key(i):
                sp.dma_start(keyr[:, :], s_d.rearrange("(b n) -> b n", n=S)[bass.ds(i, 1), :]
                             .rearrange("a n -> (a n)").partition_broadcast(P)).then_inc(key_in, 16)

            def unit(i, u, more=True):
                wait_apart(sp, ob_done, 8 * i + 4 * u + 4)
                sp.dma_start(ob3[bass.ds(2 * i + u, 1)].rearrange("a p t e -> (a p) t e"), ob[:, u]).then_inc(out_st[u], 16)
                if more:
                    wait_apart(sp, saT_ps, 8 * i + 4 * u + 4)
                    load_c(i + 1, u)
                    if u == 1:
                        wait_apart(sp, rk, RK * (i + 1))
                        load_key(i + 1)

            load_c(0, 0)
            load_c(0, 1)
            load_key(0)
            with sp.Fori(0, B - 1) as i:
                unit(i, 0)
                unit(i, 1)
            unit(B - 1, 0, more=False)
            unit(B - 1, 1, more=False)
            wait_apart(sp, out_st[0], 16 * B)
            wait_apart(sp, out_st[1], 16 * B)

        @block.scalar
        def _(act):
            def normalise(t, u):
                return nc.scalar.activation(xr[:, u, :], xs[:, bass.ds(t, 1), :].rearrange("p a e -> p (a e)"),
                                            ACT.Identity, bias=xshift[:, bass.ds(t, 1)], scale=xscale[:, bass.ds(t, 1)])

            def tile_a(i, u, more=True):
                t = 2 * i + u
                if more:
                    act.wait_ge(group_of, t + 2)
                    if not (isinstance(i, int) and t == 0):
                        act.wait_ge(xT_ps, t)
                    normalise(t + 1, 1 - u).then_inc(xr_done, 1)
                act.wait_ge(xT_ps, t + 1)
                if not (isinstance(i, int) and i == 0):
                    act.wait_ge(qkv_ps, t - 1)
                    act.wait_ge(xc_st[u], 16 * i)
                nc.scalar.activation(xT[:, u].rearrange("p k n -> p (k n)"), psM[:, u, 0:KE * P], ACT.Copy).then_inc(xT_done, 1)

            def cast(i, u):
                act.wait_ge(pm_in[u], 16 * (i + 1))
                for t, g0 in ((0, 0), (1, 2)):
                    src = pm[:, u, :, t * D:(t + 1) * D].unsqueeze(2).to_broadcast([P, 32, 3, D])
                    nc.scalar.activation(partsb[:, u, :, g0:g0 + 3, :, t], src, ACT.Copy).then_inc(cast_done, 1)

            def values(i, u):
                act.wait_ge(pm_in[u], 16 * (i + 1))
                nc.scalar.activation(vext[:, u, :, 0:D], pm[:, u, :, 2 * D:3 * D], ACT.Copy).then_inc(v_done, 1)

            act.wait_ge(group_of, 1)
            normalise(0, 0).then_inc(xr_done, 1)
            tile_a(0, 0)
            tile_a(0, 1)
            with act.Fori(1, NT // 4) as i:
                tile_a(i, 0)
                tile_a(i, 1)
            act.wait_ge(dconst, N_DCONST)
            cast(0, 0)
            with act.Fori(NT // 4, NT // 2 - 1) as i:
                tile_a(i, 0)
                tile_a(i, 1)
            tile_a(NT // 2 - 1, 0)
            tile_a(NT // 2 - 1, 1, more=False)
            values(0, 0)
            cast(0, 1)

            def exps(i, u, j):
                q = 2 * i + u
                kb, heads = EXPS[j]
                w = (8 - kb) * P
                act.wait_ge(qk_ps, NE * q + j + 1)
                if j == 0 or EXPS[j - 1][0] != kb:
                    if kb >= 3:
                        act.wait_ge(pv_done, 8 * q + kb - 2)
                    elif not (isinstance(i, int) and q == 0):
                        act.wait_ge(pv_done, 8 * (q - 1) + (7, 8, 6)[kb])
                slot = psE[:, j % 2]
                dst = strip_at[kb][:, heads[0]:heads[-1] + 1, :]
                if kb == 5:
                    src = slot[:, :, 0:w]
                else:
                    src = slot.rearrange("p b n -> p (b n)")[:, 0:len(heads) * w]
                    dst = dst.rearrange("p c w -> p (c w)")
                nc.scalar.activation(dst, src, ACT.Exp, scale=SCALE).then_inc(exp_done, 1)

            def outputs(i, u):
                q = 2 * i + u
                act.wait_ge(pv_done, 8 * q + 8)
                if not (isinstance(i, int) and q == 0):
                    s, at = ring_at((i, u), ("OT", 1))
                    act.wait_ge(full[s], at + 1)
                nc.scalar.activation(osb[:, :], psO[:, :, :].rearrange("p h n -> p (h n)"), ACT.Copy).then_inc(osb_done, 1)

            def route_exp(r):
                act.wait_ge(rz_done, 4 * r + 3)
                nc.scalar.activation(re[:, :], rz[:, :], ACT.Exp, scale=1.0 / EPS_ROUTE, accum_out=rsum[:, :]).then_inc(re_done, 1)

            def route_ln(step, k):
                s, at = ring_at(step, ("R", k))
                act.wait_ge(full[s], at + 1)
                nc.scalar.activation(lns[:, :], psM[:, s, 0:1], ACT.Ln).then_inc(free[s], 1)

            def step(ring, where, i, u, late=True, load=True, value=True):
                r = 6 * i + 3 * u
                for item in timeline(ring, late, load):
                    if item[0] == "E":
                        exps(i, u, item[1])
                    elif item[0] == "OUT":
                        outputs(i if u else i - 1, 1 - u)
                    elif item[0] == "VALUES" and value:
                        values(i if u == 0 else i + 1, 1 - u)
                    elif item[0] == "CAST":
                        cast(i + 1, u)
                    elif item[0] == "RX":
                        route_exp(r + item[1])
                    elif item[0] == "R":
                        route_ln(where, item[1])

            act.wait_ge(smax_done, 1)
            step(ring_steady, (0, 0), 0, 0, late=False)
            step(ring_steady, (0, 1), 0, 1)
            with act.Fori(1, NQ // 2 - 1) as i:
                step(ring_steady, (i, 0), i, 0)
                step(ring_steady, (i, 1), i, 1)
            li = NQ // 2 - 1
            step(ring_steady, (li, 0), li, 0, load=False)
            step(ring_last, NQ - 1, li, 1, load=False, value=False)
            act.wait_ge(pv_done, 8 * NQ)
            s, at = ring_at(NQ - 1, ("OT", 1))
            act.wait_ge(full[s], at + 1)
            nc.scalar.activation(osb[:, :], psO[:, :, :].rearrange("p h n -> p (h n)"), ACT.Copy).then_inc(osb_done, 1)

            def hidden(i, u):
                act.wait_ge(h_ps, 2 * i + u + 1)
                if not (isinstance(i, int) and i == 0):
                    act.wait_ge(o_ps, 8 * (i - 1) + 4 * u + 4)
                nc.scalar.activation(hT[:, u, :], psO[:, u, :], ACT.Gelu, bias=b1l[:, 0:1]).then_inc(h_done, 1)

            def unit(i, u, more=True):
                for t in range(4):
                    n = 8 * i + 4 * u + t
                    act.wait_ge(saT_ps, n + 1)
                    if not (isinstance(i, int) and n < 2):
                        act.wait_ge(o_ps, n - 1)
                    nc.scalar.activation(saT[:, t % 2, :], psM[:, t % 2, 0:KE * P], ACT.Copy).then_inc(saT_done, 1)
                    if t == 1 and more:
                        hidden(i if u == 0 else i + 1, 1 - u)

            hidden(0, 0)
            unit(0, 0)
            unit(0, 1)
            with act.Fori(1, B - 1) as i:
                unit(i, 0)
                unit(i, 1)
            unit(B - 1, 0)
            unit(B - 1, 1, more=False)

            act.wait_ge(ob_done, NT)
            for h in range(2):
                for t in range(4):
                    st = 4 * h + t
                    act.wait_ge(gT_ps, st + 1)
                    nc.scalar.activation(xgT[:, :, st * P:(st + 1) * P], psM[:, st % 2, 0:KE * P].rearrange(
                        "p (k n) -> p k n", k=KE), ACT.Copy).then_inc(gT_done, 1)
                for c in range(NHC):
                    m = NHC * h + c
                    act.wait_ge(hh_ps, m + 1)
                    nc.scalar.activation(hidT[:, c, h * 512:(h + 1) * 512], psO[:, m % 2, :], ACT.Gelu,
                                         bias=b1h[:, c:c + 1]).then_inc(hh_done, 1)
                if h == 0:
                    act.wait_ge(gu_done, 2 * NSLOT + 2)
                    nc.scalar.activation(gscore[:, :], gu[:, :], ACT.Exp, scale=1.0 / EPS_ROUTE).then_inc(gs_done, 1)

        @block.tensor
        def _(pe):
            pe.wait_ge(consts, 2)

            def transposes_a(i, u):
                t = 2 * i + u
                pe.wait_ge(xr_done, t + 1)
                if not (isinstance(i, int) and i == 0):
                    pe.wait_ge(xT_done, t - 1)
                for k in range(KE):
                    mm = pe.transpose(psM[:, u, k * P:(k + 1) * P], xr[:, u, k * P:(k + 1) * P], ident[:, :])
                mm.then_inc(xT_ps, 1)

            def project(i, u):
                t = 2 * i + u
                pe.wait_ge(xT_done, t + 1)
                if isinstance(i, int) and t == 0:
                    pe.wait_ge(wa_in, 48)
                if not (isinstance(i, int) and i == 0):
                    pe.wait_ge(qkv_done, t - 1)
                for h in range(2):
                    n = HW + h
                    for k in range(KE):
                        mm = pe.matmul(psE[:, u, h, 0:n], xT[:, u, k, :], w_qkv[:, k, HW * h:HW * h + n],
                                       start=(k == 0), stop=(k == KE - 1))
                mm.then_inc(qkv_ps, 1)

            def tile_a(i, u, more=True):
                if more:
                    transposes_a(i if u == 0 else i + 1, 1 - u)
                project(i, u)

            transposes_a(0, 0)
            tile_a(0, 0)
            tile_a(0, 1)
            with pe.Fori(1, NT // 2 - 1) as i:
                tile_a(i, 0)
                tile_a(i, 1)
            tile_a(NT // 2 - 1, 0)
            tile_a(NT // 2 - 1, 1, more=False)

            def ring_item(step, fi, fu, f, item, r=None):
                s, at = ring_at(step, ("OT", item[1]) if item[0] == "SKIP" else item)
                if not (isinstance(at, int) and at == 0):
                    pe.wait_ge(free[s], at)
                kind = item[0]
                if kind == "T":
                    _, c, h = item
                    if c == 0 and h == 0:
                        pe.wait_ge(split_done, 5 * f + 5)
                    for b in range(4):
                        n = 8 * c + 4 * h + b
                        mm = pe.transpose(psM[0:W, s, b * P:(b + 1) * P], parts[:, fu, n * W:(n + 1) * W], ident[:, :])
                elif kind == "C":
                    _, c, k = item
                    qb, k0, n, _d = CHUNKS[k]
                    if k in (0, 4):
                        ts, tat = ring_at(step, ("T", c, 0 if k == 0 else 1))
                        pe.wait_ge(free[ts], tat + 1)
                    mm = pe.matmul(psM[:, s, 0:n], QTb[0:W, fu, c * 1024 + qb * P:c * 1024 + (qb + 1) * P, 0],
                                   QTb[0:W, fu, c * 1024 + k0:c * 1024 + k0 + n, 1], start=True, stop=True)
                elif kind == "MT":
                    c = item[1]
                    pe.wait_ge(mw_done, 4 * (4 * (f - 1 if c == 3 else f) + c + 1))
                    mm = pe.transpose(psM[0:24, s, 0:P], mW[:, c, :], ident[:, :])
                elif kind == "OT":
                    h = item[1]
                    pe.wait_ge(osb_done, f - 1)
                    for b in range(4):
                        mm = pe.transpose(psM[:, s, b * P:(b + 1) * P], osb[:, (4 * h + b) * P:(4 * h + b + 1) * P], ident[:, :])
                elif kind == "R":
                    pe.wait_ge(re_done, r + 1)
                    mm = pe.matmul(psM[:, s, 0:1], blockones[:, :], rsum[:, :], start=True, stop=True)
                else:
                    mm = pe.transpose(psM[0:24, s, 0:P], mW[:, 3, :], ident[:, :])
                mm.then_inc(full[s], 1)

            def scores(i, u, j):
                q = 2 * i + u
                kb, heads = EXPS[j]
                w = (8 - kb) * P
                if not (isinstance(i, int) and q == 0 and j < 2):
                    pe.wait_ge(exp_done, NE * q + j - 1)
                if kb == 0:
                    pe.wait_ge(m_in[heads[0]], 16 * (q + 1))
                for n, c in enumerate(heads):
                    lhsT = QTb[0:W + 3, u, c * 1024 + kb * P:c * 1024 + (kb + 1) * P, 1]
                    if kb < 4:
                        spans = [(0, 0, 512), (1, 512, w)]
                    elif kb == 6:
                        spans = [(n // 2, 0, w)]
                    elif kb == 7:
                        spans = [(0, 0, w)]
                    else:
                        spans = [(n, 0, w)]
                    off = {6: (n % 2) * w, 7: n * w}.get(kb, 0)
                    for bank, a, b in spans:
                        if b > a:
                            q0 = c * 1024 + kb * P + a
                            mm = pe.matmul(psE[:, j % 2, bank, off:off + b - a], lhsT, QTb[0:W + 3, u, q0:q0 + b - a, 0],
                                           start=True, stop=True)
                mm.then_inc(qk_ps, 1)

            def product(i, u, kb):
                q = 2 * i + u
                w = (8 - kb) * P
                pe.wait_ge(mask_done, 8 * q + kb + 1)
                if kb == 0:
                    pe.wait_ge(v_done, q + 1)
                    if not (isinstance(i, int) and q == 0):
                        pe.wait_ge(osb_done, q)
                for h in range(kb // 4, 2):
                    q0 = max(kb * P, 512 * h)
                    n = 512 * (h + 1) - q0
                    for c in range(4):
                        mm = pe.matmul(psO[32 * c:32 * c + 32, h, q0 - 512 * h:512], vext[:, u, 8 * c + kb, :],
                                       strip_at[kb][:, c, q0 - kb * P:q0 - kb * P + n],
                                       start=(kb == 0), stop=(kb == 4 * h + 3), skip_group_check=True)
                mm.then_inc(pv_done, 1)

            pe.wait_ge(dconst, N_DCONST)
            for item in ring_first:
                ring_item(-1, 0, 0, 0, item)

            def step(ring, where, i, u, late=True, load=True):
                for item in timeline(ring, late, load):
                    if item[0] == "E":
                        scores(i, u, item[1])
                    elif item[0] == "PV" and item[2] == 0:
                        product(i, u, item[1])
                    elif item[0] == "PV":
                        product(i if u else i - 1, 1 - u, item[1])
                    elif item[0] in ("T", "C", "MT", "OT", "R", "SKIP"):
                        ring_item(where, i if u == 0 else i + 1, 1 - u, 2 * i + u + 1, item,
                                  6 * i + 3 * u + item[1] if item[0] == "R" else None)

            step(ring_steady, (0, 0), 0, 0, late=False)
            step(ring_steady, (0, 1), 0, 1)
            with pe.Fori(1, NQ // 2 - 1) as i:
                step(ring_steady, (i, 0), i, 0)
                step(ring_steady, (i, 1), i, 1)
            li = NQ // 2 - 1
            step(ring_steady, (li, 0), li, 0, load=False)
            step(ring_last, NQ - 1, li, 1, load=False)
            product(li, 1, 6)
            product(li, 1, 7)

            def light_hidden(i, u):
                if isinstance(i, int) and i == 0:
                    pe.wait_ge(osb_done, NQ)
                    pe.wait_ge(fold_done, N_FOLD - 1)
                    pe.wait_ge(wd_in, 16 * 7)
                    pe.wait_ge(xc_st[0], 16 * (NT // 2))
                    pe.wait_ge(xc_st[1], 16 * (NT // 2))
                else:
                    pe.wait_ge(h_done, 2 * (i - 1) + u + 1)
                for k in range(KE):
                    mm = pe.matmul(psO[:, u, :], w1l[:, k, :], xrT[:, k, bass.ds(1024 * i + 512 * u, 512)],
                                   start=(k == 0), stop=(k == KE - 1))
                mm.then_inc(h_ps, 1)

            light_hidden(0, 0)
            s0 = (L0 + L * (NQ - 1) + len(ring_last)) % 2
            base = (L0 + L * (NQ - 1) + len(ring_last)) // 2
            for h in range(2):
                s, at = final_ot(h)
                pe.wait_ge(free[s], at)
                for b in range(4):
                    mm = pe.transpose(psM[:, s, b * P:(b + 1) * P], osb[:, (4 * h + b) * P:(4 * h + b + 1) * P], ident[:, :])
                mm.then_inc(full[s], 1)
            light_hidden(0, 1)

            def transposes_c(i, u, t):
                n = 8 * i + 4 * u + t
                if t == 0:
                    pe.wait_ge(c_in[u], 16 * (i + 1))
                if not (isinstance(i, int) and n < 2):
                    pe.wait_ge(saT_done, n - 1)
                elif n == 0:
                    for h in range(2):
                        s, at = final_ot(h)
                        pe.wait_ge(free[s], at + 1)
                for k in range(KE):
                    mm = pe.transpose(psM[:, t % 2, k * P:(k + 1) * P], sa_in[:, u, t, k * P:(k + 1) * P], ident[:, :])
                mm.then_inc(saT_ps, 1)

            def project_c(i, u, t):
                n = 8 * i + 4 * u + t
                o = psE[:, t // 2, t % 2, 0:E]
                if t == 0:
                    pe.wait_ge(h_done, 2 * i + u + 1)
                if not (isinstance(i, int) and n < 4):
                    pe.wait_ge(ob_done, n - 3)
                pe.matmul(o, hT[:, u, t * P:(t + 1) * P], w2l, start=True, stop=False)
                pe.wait_ge(saT_done, n + 1)
                for k in range(KE):
                    mm = pe.matmul(o, saT[:, t % 2, k * P:(k + 1) * P], wout[:, k, :], start=False, stop=(k == KE - 1))
                mm.then_inc(o_ps, 1)

            def unit(i, u, more=True):
                for t in range(4):
                    if t < 3:
                        transposes_c(i, u, t + 1)
                    elif more:
                        transposes_c(i if u == 0 else i + 1, 1 - u, 0)
                    project_c(i, u, t)
                    if t == 0 and more and not (isinstance(i, int) and i == 0 and u == 0):
                        light_hidden(i if u == 0 else i + 1, 1 - u)

            transposes_c(0, 0, 0)
            unit(0, 0)
            unit(0, 1)
            with pe.Fori(1, B - 1) as i:
                unit(i, 0)
                unit(i, 1)
            unit(B - 1, 0)
            unit(B - 1, 1, more=False)

            for st in range(NSLOT):
                b, hh = st // 2, st % 2
                if hh == 0:
                    pe.wait_ge(hot_done, 8 * (b + 1))
                if st == 0:
                    pe.wait_ge(saT_done, NT)
                    pe.wait_ge(consts, N_CONST)
                for k in range(8):
                    mm = pe.matmul(psM[:, 0, 2 * st:2 * st + 2], hotb[:, 8 * b + k, hh * P:(hh + 1) * P],
                                   tokid[:, :, 8 * b + k], start=(k == 0), stop=(k == 7))
            mm.then_inc(idx_ps, 1)

            for h in range(2):
                for t in range(4):
                    st = 4 * h + t
                    pe.wait_ge(gn_done, st + 1)
                    if st >= 2:
                        pe.wait_ge(gT_done, st - 1)
                    elif st == 0:
                        pe.wait_ge(idx_done, 2)
                    for k in range(KE):
                        mm = pe.transpose(psM[:, st % 2, k * P:(k + 1) * P], xgn[:, st, k * P:(k + 1) * P], ident[:, :])
                    mm.then_inc(gT_ps, 1)
                pe.wait_ge(gT_done, 4 * h + 4)
                for c in range(NHC):
                    m = NHC * h + c
                    if m >= 2:
                        pe.wait_ge(hh_done, m - 1)
                    for k in range(KE):
                        mm = pe.matmul(psO[:, m % 2, :], w1h[:, k, c * P:(c + 1) * P], xgT[:, k, h * 512:(h + 1) * 512],
                                       start=(k == 0), stop=(k == KE - 1))
                    mm.then_inc(hh_ps, 1)
                for t in range(4):
                    st = 4 * h + t
                    o = psE[:, t // 2, t % 2, 0:E]
                    if st >= 4:
                        pe.wait_ge(hv_half, st - 3)
                    else:
                        pe.wait_ge(ob_done, NT)
                    for c in range(NHC):
                        pe.wait_ge(hh_done, NHC * h + c + 1)
                        mm = pe.matmul(o, hidT[:, c, st * P:(st + 1) * P], w2h[:, c, :], start=(c == 0), stop=(c == NHC - 1))
                    mm.then_inc(ho_ps, 1)

        @block.vector
        def _(dve):
            def const(ins):
                ins.then_inc(dconst, 1)

            const(dve.memset(vext[:, :, :, :], 0.0))
            const(dve.memset(blockones[:, :], 0.0))
            const(dve.memset(mWb[:, :, :, :, 1], 1.0))
            const(dve.memset(mx[:, :, :, :], MASKED))
            const(dve.memset(rank3[:, :, :], 0.0))
            dve.wait_ge(dconst, 2)
            const(dve.memset(vext[:, :, :, D:D + 1], 1.0))
            for b in range(4):
                const(dve.memset(blockones[32 * b:32 * b + 32, 32 * b:32 * b + 32], 1.0))
            const(dve.memset(mWb[:, :, :, :, 0], 0.0))

            def stats(g, t):
                n = 8 * g + t
                if t == 0:
                    dve.wait_ge(x_in[g], 16)
                nc.vector.bn_stats(bn6[:, n, :], xs[:, n, :]).then_inc(bn_done, 1)
                dve.wait_ge(bn_done, 2 * n + 1)
                nc.vector.bn_aggr(mv[:, n, :], bn6[:, n, :]).then_inc(bn_done, 1)

            def invert(g):
                dve.wait_ge(stat_done, ST * g + 5)
                nc.vector.reciprocal(rnrm[:, 8 * g:8 * g + 8], nrm[:, 8 * g:8 * g + 8]).then_inc(nrm_inv, 1)

            def evacuate(i, u):
                t = 2 * i + u
                dve.wait_ge(qkv_ps, t + 1)
                if not (isinstance(i, int) and i == 0):
                    dve.wait_ge(qkv_st[u], 16 * i)
                nc.vector.tensor_scalar(s_tok[:, bass.ds(t, 1)], psE[:, u, 1, HW:HW + 1], unscale[:, bass.ds(t, 1)], None,
                                        ALU.mult)
                nc.vector.scalar_tensor_tensor(out=qkvs[:, u, :].rearrange("p (h n) -> p h n", h=2), in0=psE[:, u, :, 0:HW],
                                               scalar=unscale[:, bass.ds(t, 1)],
                                               in1=bias_qkv.rearrange("p (h n) -> p h n", h=2),
                                               op0=ALU.mult, op1=ALU.add).then_inc(qkv_done, 1)

            for t in range(8):
                stats(0, t)
            invert(0)
            dve.wait_ge(wa_in, 48)
            for g in range(1, 4):
                for t in range(8):
                    stats(g, t)
                invert(g)
            dve.wait_ge(stat_done, ST * 4)
            evacuate(0, 0)
            evacuate(0, 1)
            with dve.Fori(1, NT // 2) as i:
                evacuate(i, 0)
                evacuate(i, 1)

            def ring_item(step, fu, f, late_m, late_u, item):
                s, at = ring_at(step, ("OT", item[1]) if item[0] == "SKIP" else item)
                kind = item[0]
                if kind == "C" and CHUNKS[item[2]][3]:
                    wait_apart(dve, full[s], at + 1)
                else:
                    dve.wait_ge(full[s], at + 1)
                if kind == "T":
                    _, c, h = item
                    q0 = c * 1024 + h * 512
                    nc.vector.tensor_copy(QT[0:W, fu, q0:q0 + 512], psM[0:W, s, :]).then_inc(free[s], 1)
                elif kind == "C":
                    _, c, k = item
                    qb, k0, n, diag = CHUNKS[k]
                    if k == 0 and not (isinstance(f, int) and f == 0):
                        wait_apart(dve, nm_done, 4 * (f - 1) + c + 1)
                    acc = mx[:, c, qb, k0 // 512:k0 // 512 + 1]
                    if diag:
                        nc.vector.tensor_tensor_reduce(psM[:, s, 0:n], psM[:, s, 0:n], maskrow[:, 512 - n:512], 1.0, MASKED,
                                                       ALU.add, ALU.max, acc).then_inc(free[s], 1)
                    else:
                        nc.vector.tensor_reduce(acc, psM[:, s, 0:n], AX.X, ALU.max).then_inc(free[s], 1)
                    if k == 11:
                        for kk in (10, 11):
                            ss, aa = ring_at(step, ("C", c, kk))
                            dve.wait_ge(free[ss], aa + 1)
                        nc.vector.tensor_reduce(nm[:, c, :], mx[:, c, :, :], AX.X, ALU.max, negate=True).then_inc(nm_done, 1)
                elif kind == "MT":
                    nc.vector.tensor_copy(mT[:, item[1], :], psM[0:24, s, 0:P]).then_inc(free[s], 1)
                elif kind == "OT":
                    normalise(late_m, late_u, item[1], s)
                else:
                    nc.vector.tensor_copy(skipped[:, s:s + 1], psM[0:24, s, 0:1]).then_inc(free[s], 1)

            def normalise(m, u, h, s):
                o = psM[:, s, :].rearrange("p (n c w) -> p n c w", n=4, c=4)
                nc.vector.reciprocal(rden[:, h], o[:, :, :, D]).then_inc(rden_done, 1)
                dve.wait_ge(rden_done, 4 * m + 2 * u + h + 1)
                if h == 0:
                    dve.wait_ge(sa_st[u], 16 * (m + 1))
                nc.vector.tensor_tensor(pmo[:, u, :, 4 * h:4 * h + 4, :].rearrange("p c n d -> p n c d"), o[:, :, :, 0:D],
                                        rden[:, h].unsqueeze(3).to_broadcast([P, 4, 4, D]), ALU.mult).then_inc(free[s], 1)

            for item in ring_first:
                ring_item(-1, 0, 0, None, None, item)
            dve.wait_ge(route_in, 16 * 5)
            nc.vector.tensor_reduce(smax[:, :], xs[:, 0:4, :].rearrange("p t e -> p (t e)"), AX.X, ALU.max).then_inc(smax_done, 1)

            def step(ring, where, i, u, late=True, load=True):
                for item in timeline(ring, late, load):
                    if item[0] in ("T", "C", "MT", "OT", "SKIP"):
                        ring_item(where, 1 - u, 2 * i + u + 1, i if u else i - 1, 1 - u, item)

            step(ring_steady, (0, 0), 0, 0, late=False)
            step(ring_steady, (0, 1), 0, 1)
            with dve.Fori(1, NQ // 2 - 1) as i:
                step(ring_steady, (i, 0), i, 0)
                step(ring_steady, (i, 1), i, 1)
            li = NQ // 2 - 1
            step(ring_steady, (li, 0), li, 0, load=False)
            step(ring_last, NQ - 1, li, 1, load=False)
            for h in range(2):
                s, at = final_ot(h)
                dve.wait_ge(full[s], at + 1)
                normalise(NQ // 2 - 1, 1, h, s)

            dve.wait_ge(na_in, 16)
            nc.vector.tensor_scalar(nlo_all[:, :], na_all[:, :], EPS_ROUTE * EXP_FLOOR, None, ALU.add).then_inc(nlo_done, 1)
            dve.wait_ge(nlo_done, 1)

            def ranking(i, u, t):
                k = 4 * u + t
                at = RK * i + 2 + RK_AT[k]
                kp = keyc[:, k:k + 1]
                dve.wait_ge(rk, at)
                if k > 0:
                    nc.vector.tensor_scalar(junk[:, 0:k * P], keyr[:, 0:k * P], kp, 0.0, ALU.is_ge, ALU.add,
                                            accum_out=rank3[:, 0, k:k + 1]).then_inc(rk, 1)
                    at += 1
                    dve.wait_ge(rk, at)
                nc.vector.tensor_scalar(junk[:, k * P:S], keyr[:, k * P:S], kp, 0.0, ALU.is_gt, ALU.add,
                                        accum_out=rank3[:, 1, k:k + 1]).then_inc(rk, 1)
                dve.wait_ge(rk, at + 1)
                nc.vector.scalar_tensor_tensor(out=junk[:, k * P:(k + 1) * P], in0=keyr[:, k * P:(k + 1) * P], scalar=kp,
                                               in1=below[:, :], op0=ALU.is_equal, op1=ALU.mult,
                                               accum_out=rank3[:, 2, k:k + 1]).then_inc(rk, 1)

            def unit(i, u):
                for t in range(4):
                    n = 8 * i + 4 * u + t
                    if t == 0:
                        dve.wait_ge(c_x, 2 * i + u + 1)
                        if not (isinstance(i, int) and i == 0):
                            dve.wait_ge(out_st[u], 16 * i)
                    dve.wait_ge(o_ps, n + 1)
                    nc.vector.tensor_tensor(ob[:, u, t, :], psE[:, t // 2, t % 2, 0:E], x_in2[:, u, t, :], ALU.add
                                            ).then_inc(ob_done, 1)
                    if u == 0 and t == 0:
                        dve.wait_ge(key_in, 16 * (i + 1))
                        lo, hi = nlo_all[:, bass.ds(i, 1)], na_all[:, bass.ds(i, 1)]
                        nc.vector.tensor_scalar(keyr[:, :], keyr[:, :], hi, lo, ALU.min, ALU.max).then_inc(rk, 1)
                        nc.vector.tensor_scalar(keyc[:, :], s_tok[:, bass.ds(8 * i, 8)], hi, lo, ALU.min, ALU.max).then_inc(rk, 1)
                    ranking(i, u, t)
                if u == 1:
                    at = RK * i + 2 + RK_AT[8]
                    dve.wait_ge(rk, at)
                    nc.vector.tensor_tensor(rank[:, :], rank3[:, 0, :], rank3[:, 1, :], ALU.add).then_inc(rk, 1)
                    dve.wait_ge(rk, at + 1)
                    nc.vector.tensor_tensor(rank[:, :], rank[:, :], rank3[:, 2, :], ALU.add).then_inc(rk, 1)
                    dve.wait_ge(rk, at + 2)
                    for k in range(8):
                        nc.vector.tensor_scalar(hotb[:, bass.ds(8 * i + k, 1), :].rearrange("p a n -> p (a n)"), iota256[:, :],
                                                rank[:, k:k + 1], None, ALU.is_equal).then_inc(hot_done, 1)

            dve.wait_ge(consts, N_CONST)
            unit(0, 0)
            unit(0, 1)
            with dve.Fori(1, B) as i:
                unit(i, 0)
                unit(i, 1)

            dve.wait_ge(idx_ps, 1)
            ip = psM[:, 0, 0:2 * NSLOT].rearrange("p (s w) -> p s w", w=2)
            nc.vector.tensor_scalar(idxf[:, :], ip[:, :, 0], float(P), None, ALU.mult).then_inc(idx_done, 1)
            dve.wait_ge(idx_done, 1)
            nc.vector.tensor_tensor(idx[:, :], idxf[:, :], ip[:, :, 1], ALU.add).then_inc(idx_done, 1)

            for h in range(2):
                for t in range(4):
                    st = 4 * h + t
                    dve.wait_ge(g_in[st], 16)
                    nc.vector.bn_stats(bn6[:, st, :], xg[:, st, :]).then_inc(gx_done, 1)
                    dve.wait_ge(gx_done, 9 * h + 2 * t + 1)
                    nc.vector.bn_aggr(mv[:, st, :], bn6[:, st, :]).then_inc(gx_done, 1)
                dve.wait_ge(gp_done, ST * h + 5)
                nc.vector.reciprocal(rnrm[:, 4 * h:4 * h + 4], nrm[:, 4 * h:4 * h + 4]).then_inc(gx_done, 1)
                dve.wait_ge(gp_done, ST * (h + 1))
                for t in range(4):
                    st = 4 * h + t
                    nc.vector.tensor_scalar(xgn[:, st, :], xg[:, st, :], xscale[:, st:st + 1], xshift[:, st:st + 1],
                                            ALU.mult, ALU.add).then_inc(gn_done, 1)
            for st in range(NSLOT):
                dve.wait_ge(gn_done, st + 1)
                nc.vector.tensor_tensor_reduce(xg[:, st, :], xgn[:, st, :], rt_row, 1.0, 0.0, ALU.mult, ALU.add,
                                               gdot[:, st:st + 1]).then_inc(gu_done, 1)
            dve.wait_ge(gu_done, NSLOT)
            for st in range(NSLOT):
                nc.vector.tensor_scalar(gu[:, st:st + 1], gdot[:, st:st + 1], unscale[:, st:st + 1],
                                        na_all[:, st // 2:st // 2 + 1], ALU.mult, ALU.subtract).then_inc(gu_done, 1)
            dve.wait_ge(gu_done, 2 * NSLOT)
            nc.vector.tensor_scalar(gu[:, :], gu[:, :], 0.0, None, ALU.min).then_inc(gu_done, 1)
            dve.wait_ge(gu_done, 2 * NSLOT + 1)
            nc.vector.tensor_scalar(gu[:, :], gu[:, :], 1.0, None, ALU.mult).then_inc(gu_done, 1)
            dve.wait_ge(gs_done, 1)
            nc.vector.tensor_scalar(gw[:, :], gscore[:, :], -1.0, 1.0, ALU.mult, ALU.add).then_inc(gu_done, 1)
            dve.wait_ge(gu_done, 2 * NSLOT + 3)
            nc.vector.tensor_tensor(gw[:, :], gw[:, :], gscore[:, :], ALU.add).then_inc(gu_done, 1)
            dve.wait_ge(gu_done, 2 * NSLOT + 4)
            for st in range(NSLOT):
                t = st % 4
                dve.wait_ge(ho_ps, st + 1)
                nc.vector.tensor_tensor(hv[:, st, :], psE[:, t // 2, t % 2, 0:E], bias_h, ALU.add).then_inc(hv_half, 1)
                dve.wait_ge(hv_half, st + 1)
                nc.vector.tensor_scalar(hv[:, st, :], hv[:, st, :], gw[:, st:st + 1], None, ALU.mult).then_inc(hv_done, 1)

        @block.gpsimd
        def _(pool):
            def const(ins, n=[0]):
                ins.then_inc(consts, 1)
                n[0] += 1
                return n[0]

            const(pool.memset(ident[:, :], 1.0))
            pool.wait_ge(consts, 1)
            const(pool.affine_select(out=ident[:, :], in_=ident[:, :], pattern=[[-1, P]], compare_op=ALU.is_equal,
                                     fill=0.0, base=0, channel_multiplier=1))
            const(pool.memset(halfpow[:, 0, :], -0.5))
            const(pool.memset(halfpow[:, 1, :], 0.5))
            pool.wait_ge(consts, 4)

            def factors(a, n, base, done, size):
                var, mean = mv[:, a:a + n, 1], mv[:, a:a + n, 0]
                c = slice(a, a + n)

                def then(ins, k):
                    ins.then_inc(done, 1)
                    pool.wait_ge(done, base + k)

                pool.tensor_scalar(veps[:, 0, c], var, EPS_LN, None, ALU.add).then_inc(done, 1)
                then(pool.tensor_scalar(veps[:, 1, c], var, VAR_FLOOR, None, ALU.max), 2)
                then(pool.tensor_tensor(roots[:, :, c], veps[:, :, c], halfpow[:, :, c], ALU.pow), 3)
                then(pool.tensor_tensor(nrm[:, c], roots[:, 0, c], roots[:, 1, c], ALU.mult), 4)
                then(pool.tensor_scalar(nrm[:, c], nrm[:, c], float(E) ** 0.5, 1e-12, ALU.mult, ALU.max), 5)
                pool.tensor_scalar(unscale[:, c], nrm[:, c], float(E) ** -0.5, None, ALU.mult).then_inc(done, 1)
                pool.wait_ge(*size)
                then(pool.tensor_tensor(xscale[:, c], roots[:, 0, c], rnrm[:, c], ALU.mult), 7)
                then(pool.tensor_scalar(xscale[:, c], xscale[:, c], float(E) ** 0.5, None, ALU.mult), 8)
                then(pool.tensor_tensor(xshift[:, c], mean, xscale[:, c], ALU.mult), 9)
                then(pool.tensor_scalar(xshift[:, c], xshift[:, c], -1.0, None, ALU.mult), 10)

            for g in range(4):
                pool.wait_ge(bn_done, 16 * (g + 1))
                factors(8 * g, 8, ST * g, stat_done, (nrm_inv, g + 1))
                pool.sem_inc(group_of, 8)

            const(pool.memset(maskrow[:, :], 0.0))
            const(pool.memset(below[:, :], 1.0))
            pool.wait_ge(consts, 6)
            const(pool.affine_select(out=maskrow[:, 512 - P:512], in_=maskrow[:, 512 - P:512], pattern=[[-1, P]],
                                     compare_op=ALU.is_ge, fill=MASKED, base=0, channel_multiplier=1))
            const(pool.affine_select(out=below[:, :], in_=below[:, :], pattern=[[-1, P]], compare_op=ALU.is_gt,
                                     fill=0.0, base=0, channel_multiplier=1))
            const(pool.iota(iota_i[:, :], pattern=[[1, NUM_HEAVY]], base=0, channel_multiplier=0))
            const(pool.iota(tokid_i[:, 0, :], pattern=[[1, NT]], base=0, channel_multiplier=0))
            const(pool.iota(tokid_i[:, 1, :], pattern=[[0, NT]], base=0, channel_multiplier=1))
            pool.wait_ge(consts, 11)
            const(pool.tensor_copy(iota256[:, :], iota_i[:, :]))
            const(pool.tensor_copy(tokid[:, :, :], tokid_i[:, :, :]))

            pool.wait_ge(wc_in, 16 * 6)
            for k in range(KE):
                pool.tensor_scalar(w1l[:, k, :], w1l[:, k, :], gl[:, k:k + 1], None, ALU.mult).then_inc(fold_done, 1)
                pool.tensor_scalar(w1h[:, k, :], w1h[:, k, :], gh[:, k:k + 1], None, ALU.mult).then_inc(fold_done, 1)

            def second(i, u, t):
                q = 2 * i + u
                pool.wait_ge(cast_done, 2 * q + 1 + t)
                x_ = pm[:, u, :, t * D:(t + 1) * D].unsqueeze(2).to_broadcast([P, 32, 2, D])
                p1 = partsb[:, u, :, 2:3, :, t].to_broadcast([P, 32, 2, D])
                dst = partsb[:, u, :, 3:6:2, :, t] if t == 0 else partsb[:, u, :, 1:6:4, :, t]
                pool.tensor_tensor(dst, x_, p1, ALU.subtract).then_inc(split_done, 1)

            def rest(i, u):
                pool.tensor_tensor(r1[:, :, :].rearrange("p n (t e) -> p n t e", t=2),
                                   pm[:, u, :, 0:2 * D].rearrange("p n (t e) -> p n t e", t=2),
                                   partsb[:, u, :, 2, :, :].rearrange("p n e t -> p n t e"), ALU.subtract).then_inc(split_done, 1)

            def third(i, u, t):
                pool.wait_ge(split_done, 5 * (2 * i + u) + 3)
                pool.tensor_tensor(partsb[:, u, :, 4 if t == 0 else 0, :, t], r1[:, :, t * D:(t + 1) * D],
                                   partsb[:, u, :, 5, :, t], ALU.subtract).then_inc(split_done, 1)

            for u in range(2):
                second(0, u, 0)
                second(0, u, 1)
                if u == 1:
                    pool.wait_ge(split_done, 5)
                rest(0, u)
                third(0, u, 0)
                third(0, u, 1)

            def maxima(f, c):
                wait_apart(pool, nm_done, 4 * f + c + 1)
                at = 4 * (4 * f + c)
                p = [mWb[:, c, k, :, 0] for k in range(3)]
                pool.tensor_copy(p[0], nm[:, c, :]).then_inc(mw_done, 1)
                pool.wait_ge(mw_done, at + 1)
                pool.tensor_tensor(p[1], nm[:, c, :], p[0], ALU.subtract).then_inc(mw_done, 1)
                pool.tensor_tensor(nmr[:, c, :], nm[:, c, :], p[0], ALU.subtract).then_inc(mw_done, 1)
                pool.wait_ge(mw_done, at + 3)
                pool.tensor_tensor(p[2], nmr[:, c, :], p[1], ALU.subtract).then_inc(mw_done, 1)

            pool.wait_ge(dconst, N_DCONST)
            for c in range(3):
                maxima(0, c)
            pool.wait_ge(smax_done, 1)
            pool.memset(na[:, :], 0.0).then_inc(rz_done, 1)

            def route_z(r):
                wait_apart(pool, rz_done, 4 * r + 1)
                pool.tensor_scalar(rm[:, 0:1], na[:, :], smax[:, :], None, ALU.min).then_inc(rz_done, 1)
                wait_apart(pool, rz_done, 4 * r + 2)
                pool.tensor_scalar(rz[:, :], rs[:, :], na[:, :], rm[:, 0:1], ALU.min, ALU.subtract).then_inc(rz_done, 1)
                pool.tensor_scalar(rm[:, 1:2], rm[:, 0:1], C_ROUTE, None, ALU.subtract).then_inc(rz_done, 1)

            def route_a(step_, k, r):
                s, at = ring_at(step_, ("R", k))
                pool.wait_ge(free[s], at + 1)
                wait_apart(pool, rz_done, 4 * r + 4)
                pool.tensor_scalar(na[:, :], lns[:, :], EPS_ROUTE, rm[:, 1:2], ALU.mult, ALU.add).then_inc(rz_done, 1)

            route_z(0)

            def causal(i, u, kb):
                wait_apart(pool, exp_done, NE * (2 * i + u) + EXPS_OF[kb])
                diag = strip_at[kb][:, :, 0:P]
                pool.affine_select(out=diag, in_=diag, pattern=[[0, 4], [1, P]], compare_op=ALU.is_ge, fill=0.0,
                                   base=0, channel_multiplier=-1).then_inc(mask_done, 1)

            def sub(i, u, k):
                if k < 2:
                    second(i, u, k)
                elif k == 2:
                    pool.wait_ge(split_done, 5 * (2 * i + u) + 2)
                    rest(i, u)
                else:
                    third(i, u, k - 3)

            def step(ring, where, i, u, late=True, load=True):
                f, r = 2 * i + u + 1, 6 * i + 3 * u
                for item in timeline(ring, late, load):
                    if item[0] == "MAX":
                        maxima(f - 1 if item[1] == 3 else f, item[1])
                    elif item[0] == "CAUSAL":
                        causal(i, u, item[1])
                    elif item[0] == "SUB":
                        sub(i + 1, u, item[1])
                    elif item[0] == "RA":
                        route_a(where, item[1], r + item[1])
                        if not (isinstance(i, int) and r + item[1] == N_ITERS - 1):
                            route_z(r + item[1] + 1)

            step(ring_steady, (0, 0), 0, 0, late=False)
            step(ring_steady, (0, 1), 0, 1)
            with pool.Fori(1, NQ // 2 - 1) as i:
                step(ring_steady, (i, 0), i, 0)
                step(ring_steady, (i, 1), i, 1)
            li = NQ // 2 - 1
            step(ring_steady, (li, 0), li, 0, load=False)
            step(ring_last, NQ - 1, li, 1, load=False)

            def unit(i, u):
                pool.wait_ge(c_x_in[u], 16 * (i + 1))
                pool.tensor_tensor(x_in2[:, u], x_in2[:, u], bias_o[:, 0:1, :].to_broadcast([P, 4, E]), ALU.add).then_inc(c_x, 1)

            pool.wait_ge(wd_in, 16 * 7)
            pool.tensor_tensor(bias_o[:, 0, :], bias_o[:, 0, :], bias_o[:, 1, :], ALU.add).then_inc(fold_done, 1)
            pool.wait_ge(fold_done, N_FOLD)
            with pool.Fori(0, B) as i:
                unit(i, 0)
                unit(i, 1)
            pool.wait_ge(idx_done, 2)
            for st in range(NSLOT):
                pool.indirect_dma_start(out=xg[:, st, :], out_offset=None, in_=xf,
                                        in_offset=bass.IndirectOffsetOnAxis(ap=idx[:, st:st + 1], axis=0)).then_inc(g_in[st], 16)
            for h in range(2):
                pool.wait_ge(gx_done, 9 * h + 8)
                factors(4 * h, 4, ST * h, gp_done, (gx_done, 9 * h + 9))
            pool.wait_ge(out_st[0], 16 * B)
            pool.wait_ge(out_st[1], 16 * B)
            for st in range(NSLOT):
                pool.wait_ge(hv_done, st + 1)
                pool.indirect_dma_start(out=of, out_offset=bass.IndirectOffsetOnAxis(ap=idx[:, st:st + 1], axis=0),
                                        in_=hv[:, st, :], in_offset=None, compute_op=ALU.add).then_inc(add_st[st], 16)
            for st in range(NSLOT):
                pool.wait_ge(add_st[st], 16)


_INS = ['L0_attn_inputs', 'L0_attn_W_qkv', 'L0_attn_b_qkv', 'L0_attn_W_out', 'L0_attn_b_out', 'L0_ffn_routing_token',
        'L0_ffn_gamma_light', 'L0_ffn_w1_light', 'L0_ffn_b1_light', 'L0_ffn_w2_light', 'L0_ffn_b2_light',
        'L0_ffn_gamma_heavy', 'L0_ffn_w1_heavy', 'L0_ffn_b1_heavy', 'L0_ffn_w2_heavy', 'L0_ffn_b2_heavy']
_OUTS = [((4, 1024, 256), 'float32')]


def kernel(**inputs):
    import numpy as _np
    import concourse.bacc as _bacc
    from concourse import mybir as _mybir
    from concourse.bass_utils import run_bass_kernel_spmd as _run

    nc = _bacc.Bacc("TRN2", target_bir_lowering=False, num_devices=1)
    arrays, args = {}, []
    for name in _INS:
        a = _np.ascontiguousarray(inputs[name])
        arrays[f"in_{name}"] = a
        args.append(nc.dram_tensor(f"in_{name}", a.shape, _mybir.dt.from_np(a.dtype), kind="ExternalInput").ap())
    for i, (shape, dtype) in enumerate(_OUTS):
        dt = _mybir.dt.from_np(_np.dtype(dtype))
        args.append(nc.dram_tensor(f"out_{i}", shape, dt, kind="ExternalOutput").ap())
    layer_kernel(nc, *args)
    r = _run(nc, [arrays], core_ids=[0])
    return r.results[0]["out_0"]
```

```python
from contextlib import ExitStack
import math

import concourse.bass as bass
from concourse import mybir

F32 = mybir.dt.float32
BF16 = mybir.dt.bfloat16
I32 = mybir.dt.int32
ALU = mybir.AluOpType
ACT = mybir.ActivationFunctionType
AX = mybir.AxisListType

P = 128
EPS_LN = 1e-5
EPS_ROUTE = 0.1
K_ROUTE = 8.0
N_ITERS = 50
NUM_HEAVY = 256
EXP_FLOOR = -87.33654
MASKED = -3.0e38
VAR_FLOOR = 1e-36


MS = 3
ES = 3


def ring_orders():
    C = lambda c, a, b: [("C", c, k) for k in range(a, b)]
    T = lambda c: [("T", c, 0), ("T", c, 1)]
    first = (T(0) + T(1) + C(0, 0, 12) + T(2) + C(1, 0, 6) + [("MT", 0)] + C(1, 6, 12) + T(3)
             + C(2, 0, 6) + [("MT", 1)] + C(2, 6, 12) + C(3, 0, 6) + [("MT", 2)] + C(3, 6, 12))
    steady = (T(0) + [("MT", 3)] + T(1) + C(0, 0, 6) + [("OT", 0), ("OT", 1)] + C(0, 6, 10) + [("R", 0)]
              + C(0, 10, 12) + T(2) + C(1, 0, 6) + [("MT", 0)] + C(1, 6, 10) + [("R", 1)] + C(1, 10, 12) + T(3)
              + C(2, 0, 6) + [("MT", 1)] + C(2, 6, 10) + [("R", 2)] + C(2, 10, 12)
              + C(3, 0, 6) + [("MT", 2)] + C(3, 6, 12))
    steady += [("NOP",)] * (-len(steady) % MS)
    last = [("MT", 3), ("OT", 0), ("OT", 1)] + [("R", k) for k in range(5)]
    return first, steady, last


CHUNKS = [(qb, k0, min(512, (qb + 1) * P - k0), k0 + 512 >= (qb + 1) * P)
          for qb in range(8) for k0 in range(0, (qb + 1) * P, 512)]
EXPS = ([(kb, (c,), h * 512, 512 - h * kb * P) for kb in range(2) for c in range(4) for h in range(2)]
        + [(2, (0,), 0, 512), (2, (1,), 0, 512), (2, (0, 1), 512, 256)]
        + [(2, (2,), 0, 512), (2, (3,), 0, 512), (2, (2, 3), 512, 256)]
        + [(3, (0,), 0, 512), (3, (1,), 0, 512), (3, (0, 1), 512, 128)]
        + [(3, (2,), 0, 512), (3, (3,), 0, 512), (3, (2, 3), 512, 128)]
        + [(kb, (c,), 0, (8 - kb) * P) for kb in (4, 5) for c in range(4)]
        + [(6, (0, 1), 0, 256), (6, (2, 3), 0, 256), (7, (0, 1, 2, 3), 0, 128)])
EXPS_OF = [sum(1 for task in EXPS if task[0] <= k) for k in range(8)]


SUB_AFTER = (9, 13, 15, 19, 21)
CAST_COST = 3.2
PACE, PVB = 3.0, 0.4
PVS = [(kb, h) for kb in range(8) for h in range(kb // 4, 2)]
PVS_OF = [sum(1 for kb, _ in PVS if kb <= k) for k in range(8)]
NPV = len(PVS)


def merge(ring, late, load):
    LAG = 0.3
    pe = act = dve = pool = 0.0
    m_free, e_free = [0.0] * MS, [0.0] * ES
    copied, nm_at, mw_at, psum_at, mask_at, m_at = {}, {}, {3: 1.5}, {}, {}, {}
    strip_used = {}
    r = list(ring)
    e = list(range(len(EXPS)))
    late_pv = [(6, 1, -1), (7, 1, -1)] if late else []
    p = late_pv + [(kb, h, 0) for kb, h in PVS if kb < 6]
    for kb, h, w in late_pv:
        mask_at[kb, w] = 1.5
    out, nr, osb_at, subs = [], 0, 0.0 if not late else None, 5 if load else 0
    if load:
        act = CAST_COST
    total = (len(r), len(e), len(p))
    while r or e or p:
        choice = []
        if p:
            kb, h, w = p[0]
            if (kb, w) in mask_at and not (kb == 0 and osb_at is None):
                t = max(pe, mask_at[kb, w], osb_at + LAG if (kb, w) == (0, 0) else 0)
                choice.append((t, 2, p[0]))
        if e:
            j = e[0]
            kb, heads, a0_, n_ = EXPS[j]
            before = {0: (6, -1), 1: (7, -1), 3: (0, 0), 4: (1, 0), 5: (2, 0), 6: (3, 0), 7: (4, 0)}.get(kb)
            if not (before and any((a, w) == before for a, _, w in p)):
                choice.append((max(pe, e_free[j % ES], m_at.get(3, 0) if (kb, heads) == (0, (3,)) else 0),
                               0 if act < dve else 1, ("E", j)))
        if r:
            x = r[0]
            t = max(pe, m_free[nr % MS])
            if x[0] == "C" and x[2] in (0, 4):
                t = max(t, copied[x[1], 0 if x[2] == 0 else 1] if (x[1], 0) in copied else t)
            if x[0] == "MT":
                t = max(t, mw_at.get(x[1], t))
            if not (x[0] == "OT" and late and osb_at is None):
                if x[0] == "OT" and late:
                    t = max(t, osb_at + LAG)
                choice.append((t, 0 if dve <= act else 1, x))
        def key(c):
            x = c[2]
            if isinstance(x[0], int):
                share = 1 - len(p) / total[2]
            elif x[0] == "E":
                share = 1 - len(e) / total[1]
            else:
                share = 1 - len(r) / total[0]
            return max(c[0], pe) + PACE * share + (PVB if isinstance(x[0], int) else 0), c[1]
        t, _, x = min(choice, key=key)
        if isinstance(x[0], int):
            kb, h, w = p.pop(0)
            out.append(("PV",) + x)
            q0 = max(kb * P, 512 * h)
            pe = t + 0.00185 * (512 * (h + 1) - q0)
            strip_used[kb, w] = pe
            if x == (7, 1, -1):
                act = max(act, pe + LAG) + 1.1
                osb_at = act
                act += 0.6
        elif x[0] == "E":
            e.pop(0)
            kb, heads, _, n_ = EXPS[x[1]]
            cols = len(heads) * n_
            pe = t + 0.00045 * cols
            before = {0: (6, -1), 1: (7, -1), 3: (0, 0), 4: (1, 0), 5: (2, 0), 6: (3, 0), 7: (4, 0)}.get(kb)
            act = max(act, pe + LAG, strip_used.get(before, 0) + LAG) + 0.2 + 0.00083 * cols
            e_free[x[1] % ES] = act + LAG
            out.append(x)
            if x[1] + 1 in EXPS_OF:
                pool = max(pool, act + LAG) + 0.7
                mask_at[EXPS_OF.index(x[1] + 1), 0] = pool + LAG
            if x[1] + 1 in SUB_AFTER and subs:
                subs -= 1
                pool = pool + 2.2
        else:
            r.pop(0)
            out.append(x)
            s = nr % MS
            nr += 1
            width = CHUNKS[x[2]][2] if x[0] == "C" else 0
            pe = t + {"T": 0.45, "C": 0.00045 * width, "MT": 0.1, "OT": 0.45, "R": 0.06, "NOP": 0.06}[x[0]]
            if x[0] == "R":
                act = max(act, pe + LAG) + 0.5
                m_free[s] = act + LAG
                pool += 1.2
            else:
                dve = max(dve, pe + LAG) + {"T": 0.6, "C": 0.1 + 0.00105 * width, "MT": 0.25, "OT": 0.75, "NOP": 0.1}[x[0]]
                m_free[s] = dve + LAG
            if x[0] == "T":
                copied[x[1], x[2]] = dve + LAG
            if x[0] == "C" and x[2] == 11:
                dve += 0.3
                pool = max(pool, dve + LAG) + 0.9
                mw_at[x[1]] = pool + LAG
            if x[0] == "MT":
                m_at[x[1]] = dve + 2.2
    return out


def timeline(ring, late, load):
    order = merge(ring, late, load)
    out = ([("CAST",)] if load else []) + [("MAX", 3)]
    exps = routes = 0
    subs = [("SUB", k) for k in range(5)] if load else []
    for item in order:
        if item[0] == "OT" and not late:
            item = ("SKIP", item[1])
        if item[0] == "R":
            at = len(out)
            n = 0
            while n < 2 and at > 1 and out[at - 1][0] != "RA":
                at -= 1
                n += out[at][0] == "E"
            out.insert(at, ("RX", item[1]))
            out += [item, ("RA", item[1])]
            continue
        out.append(item)
        if item == ("PV", 7, 1, -1):
            out += [("OUT",), ("VALUES",)]
        if item == ("E", 1) and not late:
            out += [("VALUES",)]
        if item[0] == "C" and item[2] == 11 and item[1] < 3:
            out.append(("MAX", item[1]))
        if item[0] == "E":
            exps += 1
            if exps in EXPS_OF:
                out.append(("CAUSAL", EXPS_OF.index(exps)))
            if exps in SUB_AFTER and subs:
                out.append(subs.pop(0))
    return out


def wait_apart(engine, semaphore, value):
    engine.wait_ge(semaphore, value)
    if not isinstance(value, int):
        engine.nop(nofuse=True)


def layer_kernel(nc, x, W_qkv, b_qkv, W_out, b_out, rtok, g_l, w1_l, b1_l, w2_l, b2_l, g_h, w1_h, b1_h, w2_h, b2_h, out):
    B, S, E = x.shape
    T = B * S
    NT = T // P
    QKV = W_qkv.shape[1]
    HEADS = 16
    D = QKV // HEADS // 3
    SLOTS = HEADS
    NQ = T // 256
    HID_L, HID_H = w1_l.shape[1], w1_h.shape[1]
    KE = E // P
    NHC = HID_H // P
    SCALE = float((2 * E) ** -0.5)
    C_ROUTE = EPS_ROUTE * math.log(K_ROUTE)
    NSLOT = B * NUM_HEAVY // P
    HW = QKV // 2
    W = 6 * D

    xf = x.rearrange("b s e -> (b s) e")
    of = out.rearrange("b s e -> (b s) e")

    ring_first, ring_steady, ring_last = ring_orders()
    L0, L = len(ring_first), len(ring_steady)

    def ring_at(step, item):
        if isinstance(step, int) and step == -1:
            at = ring_first.index(item)
            return at % MS, at // MS
        if isinstance(step, int):
            at = L0 + L * (NQ - 1) + ring_last.index(item)
            return at % MS, at // MS
        i, u = step
        at = L0 + L * u + ring_steady.index(item)
        return at % MS, 2 * L // MS * i + at // MS

    NE = len(EXPS)
    ST = 10
    GROUPS = [(0, 2), (2, 6), (8, 12), (20, 12)]
    RK_AT = [0]
    for k in range(8):
        RK_AT.append(RK_AT[-1] + (3 if k else 2))
    RK = 2 + RK_AT[8] + 2
    N_DCONST, N_CONST, N_FOLD = 11, 13, 5

    def final_ot(h):
        at = L0 + L * (NQ - 1) + len(ring_last) + h
        return at % MS, at // MS

    with ExitStack() as ctx:
        def sb(name, shape, dt=F32):
            return ctx.enter_context(nc.sbuf_tensor(name, shape, dt))

        def sem(name):
            return ctx.enter_context(nc.semaphore(name))

        qkv_d = nc.dram_tensor("qkv_d", [T, QKV], F32).ap()
        sa_d = nc.dram_tensor("sa_d", [T, E], F32).ap()
        s_d = nc.dram_tensor("s_d", [T], F32).ap()
        na_d = nc.dram_tensor("na_d", [P], F32).ap()

        ps = ctx.enter_context(nc.psum_tensor("ps", [P, 8, 512], F32))
        psM = ps[:, 0:MS]
        psE = ps[:, MS:MS + ES]
        psO = ps[:, 6:8]
        psA = [ps[:, 4 + 2 * u:6 + 2 * u] for u in range(2)]
        psC = ps[:, 2:6]

        ident = sb("ident", [P, P])
        blockones = sb("blockones", [P, P])
        maskrow = sb("maskrow", [P, 512])
        below = sb("below", [P, P])
        iota256 = sb("iota256", [P, NUM_HEAVY])
        iota_i = sb("iota_i", [P, NUM_HEAVY], I32)
        tokid_i = sb("tokid_i", [P, 2, NT], I32)
        tokid = sb("tokid", [P, 2, NT], BF16)
        shared = sb("shared", [P, KE * (QKV + 1) + 3 * QKV])
        a0, a1 = KE * (QKV + 1), KE * (QKV + 1) + QKV
        w_qkv = shared[:, 0:a0].rearrange("p (k n) -> p k n", k=KE)
        bias_qkv = shared[:, a0:a1]
        qkvs = shared[:, a1:a1 + 2 * QKV].rearrange("p (b n) -> p b n", b=2)
        w2h = shared[:, 0:NHC * E].rearrange("p (c n) -> p c n", n=E)
        a2 = NHC * E
        wout = shared[:, a2:a2 + KE * E].rearrange("p (k n) -> p k n", n=E)
        w2l = shared[:, a2 + 2 * E:a2 + 3 * E]
        bias_o = shared[:, a2 + 3 * E:a2 + 5 * E].rearrange("p (k n) -> p k n", n=E)
        bias_h = shared[:, a2 + 5 * E:a2 + 6 * E]
        rt_row = shared[:, a2 + 6 * E:a2 + 7 * E]
        xrT = sb("xrT", [P, KE, T])
        xT = sb("xT", [P, 2, KE, P])
        gdot = sb("gdot", [P, NSLOT])
        gu = sb("gu", [P, NSLOT])
        gw = sb("gw", [P, NSLOT])
        gscore = sb("gscore", [P, NSLOT])
        skipped = sb("skipped", [24, 3])
        xr = sb("xr", [P, 2, E])
        bn6 = sb("bn6", [P, NT, 6])
        mv = sb("mv", [P, NT, 2])
        veps = sb("veps", [P, 2, NT])
        halfpow = sb("halfpow", [P, 2, NT])
        roots = sb("roots", [P, 2, NT])
        nrm = sb("nrm", [P, NT])
        rnrm = sb("rnrm", [P, NT])
        xscale = sb("xscale", [P, NT])
        xshift = sb("xshift", [P, NT])
        unscale = sb("unscale", [P, NT])
        s_tok = sb("s_tok", [P, NT])
        strips = sb("strips", [P, 10752])
        QT = sb("QT", [P, 2, 4096])
        parts = sb("parts", [P, 2, 32 * W])
        pm = sb("pm", [P, 2, 32, 3 * D])
        r1 = sb("r1", [P, 32, 2 * D])
        vext = sb("vext", [P, 2, 32, 32])
        osb = sb("osb", [P, 1024])
        rden = sb("rden", [P, 2, 4, 4])
        pmo = sb("pmo", [P, 2, 4, 8, D])
        mx = sb("mx", [P, 4, 8, 2])
        nm = sb("nm", [P, 4, 8])
        nmr = sb("nmr", [P, 4, 8])
        mW = sb("mW", [P, 4, 24])
        mT = sb("mT", [24, 4, P])
        rs = sb("rs", [P, 32])
        smax = sb("smax", [P, 1])
        rz = sb("rz", [P, 32])
        re = sb("re", [P, 32])
        rsum = sb("rsum", [P, 1])
        lns = sb("lns", [P, 1])
        rm = sb("rm", [P, 2])
        na = sb("na", [P, 1])
        na_all = sb("na_all", [P, B])
        nlo_all = sb("nlo_all", [P, B])
        w1l = sb("w1l", [P, KE, HID_L])
        w1h = sb("w1h", [P, KE, HID_H])
        b1l = sb("b1l", [P, 1])
        b1h = sb("b1h", [P, NHC])
        gl = sb("gl", [P, KE])
        gh = sb("gh", [P, KE])
        rank3 = sb("rank3", [P, 3, 8])
        rank = sb("rank", [P, 8])
        keyc = sb("keyc", [P, 8])
        idxf = sb("idxf", [P, NSLOT])
        idx = sb("idx", [P, NSLOT], I32)

        xs = strips[:, 0:NT * E].rearrange("p (t e) -> p t e", e=E)
        partsb = parts[:, :, :].rearrange("p b w -> p (b w)").bitcast(BF16).rearrange(
            "p (b n g e t) -> p b n g e t", b=2, n=32, g=6, t=2)
        QTb = QT[:, :, :].rearrange("p b w -> p (b w)").bitcast(BF16).rearrange("p (b w t) -> p b w t", b=2, t=2)
        mWb = mW[:, :, :].rearrange("p c w -> p (c w)").bitcast(BF16).rearrange(
            "p (c i n t) -> p c i n t", c=4, i=3, t=2)
        strip_at = {}
        for region, kbs in ((0, (0, 3, 6)), (4096, (1, 4, 7)), (4096 + 3584, (2, 5))):
            for kb in kbs:
                w = (8 - kb) * P
                strip_at[kb] = strips[:, region:region + 4 * w].rearrange("p (c w) -> p c w", c=4)

        sa_in = strips[:, 0:2048].rearrange("p (b t e) -> p b t e", b=2, e=E)
        x_in2 = strips[:, 2048:4096].rearrange("p (b t e) -> p b t e", b=2, e=E)
        saT = strips[:, 8192:8704].rearrange("p (b e) -> p b e", b=2)
        ob = QT[:, 0, 0:2048].rearrange("p (b t e) -> p b t e", b=2, e=E)
        hT = parts[:, 0, 0:1024].rearrange("p (b n) -> p b n", b=2)
        hotb = parts[:, :, :].rearrange("p b w -> p (b w)")[:, 2048:6144].bitcast(BF16).rearrange(
            "p (t n) -> p t n", n=NUM_HEAVY)
        keyr = osb
        junk = pmo[:, :, :, :, :].rearrange("p a c n d -> p (a c n d)")
        hidT = strips[:, 0:8192].rearrange("p (c n) -> p c n", n=NSLOT * P)
        xg = QT[:, 1, 0:2048].rearrange("p (t e) -> p t e", e=E)
        xgT = QT[:, 1, 2048:4096].rearrange("p (k n) -> p k n", k=KE)
        hv = vext[:, :, :, :].rearrange("p b n w -> p (b n w)").rearrange("p (t e) -> p t e", e=E)
        xgn = pm[:, :, :, :].rearrange("p b n w -> p (b n w)")[:, 0:2048].rearrange("p (t e) -> p t e", e=E)

        wd_in = sem("wd_in")
        x_in = [sem(f"x_in{g}") for g in range(len(GROUPS))]
        wa_in = sem("wa_in")
        wc_in = sem("wc_in")
        consts = sem("consts")
        dconst = sem("dconst")
        bn_done = sem("bn_done")
        stat_done = sem("stat_done")
        nrm_inv = sem("nrm_inv")
        xr_done = sem("xr_done")
        xT_ps = sem("xT_ps")
        xT_done = sem("xT_done")
        qkv_ps = sem("qkv_ps")
        qkv_done = sem("qkv_done")
        qkv_st = [sem(f"qkv_st{u}") for u in range(2)]
        s_st = sem("s_st")
        route_in = sem("route_in")
        smax_done = sem("smax_done")
        pm_in = [sem(f"pm_in{u}") for u in range(2)]
        cast_done = sem("cast_done")
        v_done = sem("v_done")
        split_done = sem("split_done")
        full = [sem(f"full{s}") for s in range(MS)]
        free = [sem(f"free{s}") for s in range(MS)]
        mx_done = sem("mx_done")
        nm_done = sem("nm_done")
        mw_done = sem("mw_done")
        m_in = [sem(f"m_in{c}") for c in range(4)]
        qk_ps = sem("qk_ps")
        exp_done = sem("exp_done")
        mask_done = sem("mask_done")
        pv_done = sem("pv_done")
        osb_done = sem("osb_done")
        rden_done = sem("rden_done")
        pmo_done = sem("pmo_done")
        sa_st = [sem(f"sa_st{u}") for u in range(2)]
        rz_done = sem("rz_done")
        re_done = sem("re_done")
        ln_done = sem("ln_done")
        fold_done = sem("fold_done")
        na_st = sem("na_st")
        na_in = sem("na_in")
        nlo_done = sem("nlo_done")
        c_in = [sem(f"c_in{u}") for u in range(2)]
        c_x = sem("c_x")
        h_ps = sem("h_ps")
        h_done = sem("h_done")
        saT_ps = sem("saT_ps")
        saT_done = sem("saT_done")
        o_ps = sem("o_ps")
        ob_done = sem("ob_done")
        out_st = [sem(f"out_st{u}") for u in range(2)]
        key_in = sem("key_in")
        rk = sem("rk")
        hot_done = sem("hot_done")
        idx_ps = sem("idx_ps")
        idx_done = sem("idx_done")
        g_in = [sem(f"g_in{t}") for t in range(NSLOT)]
        gx_done = sem("gx_done")
        gp_done = sem("gp_done")
        gs_done = sem("gs_done")
        gT_ps = sem("gT_ps")
        gT_done = sem("gT_done")
        hh_ps = sem("hh_ps")
        hh_done = sem("hh_done")
        ho_ps = sem("ho_ps")
        hv_half = sem("hv_half")
        hv_done = sem("hv_done")
        add_st = [sem(f"add_st{t}") for t in range(NSLOT)]
        group_of = sem("group_of")
        xc_st = [sem(f"xc_st{u}") for u in range(2)]
        c_x_in = [sem(f"c_x_in{u}") for u in range(2)]
        gn_done = sem("gn_done")
        gu_done = sem("gu_done")

        pm_rows = qkv_d.rearrange("(q n t) (j f) -> q (t j) n f", n=32, t=8, j=SLOTS)

        block = ctx.enter_context(nc.Block())

        @block.sync
        def _(sp):
            xt = xf.rearrange("(t p) e -> p t e", p=P)
            for g, (a, n) in enumerate(GROUPS):
                sp.dma_start(xs[:, a:a + n, :], xt[:, a:a + n, :]).then_inc(x_in[g], 16)
                if g == 0:
                    sp.dma_start(w_qkv[:, :, 0:QKV], W_qkv.rearrange("(k p) n -> p k n", p=P)).then_inc(wa_in, 16)
                    sp.dma_start(w_qkv[:, :, QKV:QKV + 1], rtok.rearrange("(k p o) -> p k o", p=P, o=1), allow_slow_non_contiguous=True).then_inc(wa_in, 16)
                    sp.dma_start(bias_qkv, b_qkv.partition_broadcast(P)).then_inc(wa_in, 16)
            for dst, src in ((w1l[:, :, :], w1_l.rearrange("(k p) n -> p k n", p=P)),
                             (w1h[:, :, :], w1_h.rearrange("(k p) n -> p k n", p=P)),
                             (b1l[:, :], b1_l.rearrange("(p o) -> p o", o=1)),
                             (b1h[:, :], b1_h.rearrange("(k p) -> p k", p=P)),
                             (gl[:, :], g_l.rearrange("(k p) -> p k", p=P)),
                             (gh[:, :], g_h.rearrange("(k p) -> p k", p=P))):
                sp.dma_start(dst, src, allow_slow_non_contiguous=True).then_inc(wc_in, 16)

            def store_qkv(i, u):
                wait_apart(sp, xT_done, 2 * i + u + 1)
                sp.dma_start(xrT[:, :, bass.ds((2 * i + u) * P, P)], xT[:, u]).then_inc(xc_st[u], 16)
                wait_apart(sp, qkv_done, 2 * i + u + 1)
                sp.dma_start(qkv_d.rearrange("(t p) n -> p t n", p=P)[:, bass.ds(2 * i + u, 1), :],
                             qkvs[:, u:u + 1, :]).then_inc(qkv_st[u], 16)

            def load_pm(i, u):
                wait_apart(sp, qkv_st[0], 32 * i + 16 * u + 16)
                wait_apart(sp, qkv_st[1], 32 * i + 16 * u + 16)
                sp.dma_start(pm[:, u, :, :], pm_rows[bass.ds(2 * i + u, 1)].rearrange("a p n f -> (a p) n f")
                             ).then_inc(pm_in[u], 16)

            with sp.Fori(0, NT // 2) as i:
                for u in range(2):
                    store_qkv(i, u)
            wait_apart(sp, qkv_done, NT)
            sp.dma_start(s_d.rearrange("(t p o) -> p t o", p=P, o=1), s_tok[:, :].unsqueeze(2), allow_slow_non_contiguous=True).then_inc(s_st, 16)
            wait_apart(sp, s_st, 16)
            sp.dma_start(rs[:, :], s_d.rearrange("(p n) -> p n", n=32)).then_inc(route_in, 16)
            for b in range(B):
                sp.dma_start(xs[32 * b:32 * b + 32, 0:4, :].rearrange("p t e -> p (t e)"),
                             s_d[b * S:(b + 1) * S].partition_broadcast(32)).then_inc(route_in, 16)

            wait_apart(sp, qkv_st[0], 16 * (NT // 2))
            wait_apart(sp, qkv_st[1], 16 * (NT // 2))
            for dst, src in ((w2l, w2_l), (wout, W_out.rearrange("(k p) n -> p k n", p=P)),
                             (w2h, w2_h.rearrange("(k p) n -> p k n", p=P)),
                             (bias_o[:, 0, :], b_out.partition_broadcast(P)), (bias_o[:, 1, :], b2_l.partition_broadcast(P)),
                             (bias_h, b2_h.partition_broadcast(P)), (rt_row, rtok.partition_broadcast(P))):
                sp.dma_start(dst, src).then_inc(wd_in, 16)

            def load_m(i, u, c):
                first = isinstance(i, int) and i == -1
                s, at = ring_at(-1 if first else (i, u), ("MT", c))
                wait_apart(sp, free[s], at + 1)
                fu = 0 if first else (u if c == 3 else 1 - u)
                sp.dma_start(QT[W:W + 3, fu, c * 1024:(c + 1) * 1024].rearrange("i (n p) -> i n p", p=P),
                             mT[:, c, :]).then_inc(m_in[c], 16)

            def store_sa(i, u, where):
                for h in range(2):
                    s, at = where(h)
                    wait_apart(sp, free[s], at + 1)
                dst = sa_d.rearrange("(q n t) (j f) -> q (t j) n f", n=32, t=8, j=SLOTS)
                sp.dma_start(dst[bass.ds(2 * i + u, 1)].rearrange("a p n f -> (a p) n f"),
                             pmo[:, u].rearrange("p c n f -> p (c n) f")).then_inc(sa_st[u], 16)

            wait_apart(sp, v_done, 1)
            wait_apart(sp, split_done, 5)
            load_pm(1, 0)
            for c in range(3):
                load_m(-1, 0, c)

            def step(i, u, late=True, load=True):
                load_m(i, u, 3)
                if late:
                    store_sa(i if u else i - 1, 1 - u, lambda h: ring_at((i, u), ("OT", h)))
                if load:
                    wait_apart(sp, v_done, 2 * i + u + 2)
                    wait_apart(sp, split_done, 5 * (2 * i + u + 2))
                    load_pm(i + 1 if u == 0 else i + 2, 1 - u)
                for c in range(3):
                    load_m(i, u, c)

            for u in range(2):
                sp.sem_inc(sa_st[u], 16)
            step(0, 0, late=False)
            step(0, 1)
            with sp.Fori(1, NQ // 2 - 2) as i:
                step(i, 0)
                step(i, 1)
            step(NQ // 2 - 2, 0)
            step(NQ // 2 - 2, 1, load=False)
            step(NQ // 2 - 1, 0, load=False)
            s, at = ring_at(NQ - 1, ("MT", 3))
            wait_apart(sp, free[s], at + 1)
            sp.dma_start(QT[W:W + 3, 1, 3 * 1024:4096].rearrange("i (n p) -> i n p", p=P), mT[:, 3, :]).then_inc(m_in[3], 16)
            store_sa(NQ // 2 - 1, 0, lambda h: ring_at(NQ - 1, ("OT", h)))
            wait_apart(sp, rz_done, N_ITERS * 4 + 1)
            sp.dma_start(na_d.rearrange("(p o) -> p o", o=1), na[:, :]).then_inc(na_st, 16)
            wait_apart(sp, na_st, 16)
            sp.dma_start(na_all[:, :], na_d.rearrange("(b g) -> g b", g=32)[0, :].partition_broadcast(P),
                         allow_slow_non_contiguous=True).then_inc(na_in, 16)
            store_sa(NQ // 2 - 1, 1, final_ot)

            wait_apart(sp, pv_done, NPV * NQ)
            for u in range(2):
                wait_apart(sp, sa_st[u], 16 * (NQ // 2 + 1))
            xb3 = xf.rearrange("(b t p) e -> b p t e", t=4, p=P)
            sb3 = sa_d.rearrange("(b t p) e -> b p t e", t=4, p=P)
            ob3 = of.rearrange("(b t p) e -> b p t e", t=4, p=P)

            def load_c(i, u):
                sp.dma_start(sa_in[:, u], sb3[bass.ds(2 * i + u, 1)].rearrange("a p t e -> (a p) t e")).then_inc(c_in[u], 16)
                sp.dma_start(x_in2[:, u], xb3[bass.ds(2 * i + u, 1)].rearrange("a p t e -> (a p) t e")).then_inc(c_x_in[u], 16)

            def load_key(i):
                sp.dma_start(keyr[:, :], s_d.rearrange("(b n) -> b n", n=S)[bass.ds(i, 1), :]
                             .rearrange("a n -> (a n)").partition_broadcast(P)).then_inc(key_in, 16)

            def unit(i, u, more=True):
                wait_apart(sp, ob_done, 8 * i + 4 * u + 4)
                sp.dma_start(ob3[bass.ds(2 * i + u, 1)].rearrange("a p t e -> (a p) t e"), ob[:, u]).then_inc(out_st[u], 16)
                if more:
                    wait_apart(sp, saT_ps, 8 * i + 4 * u + 4)
                    load_c(i + 1, u)
                    if u == 1:
                        wait_apart(sp, rk, RK * (i + 1))
                        load_key(i + 1)

            load_c(0, 0)
            load_c(0, 1)
            load_key(0)
            with sp.Fori(0, B - 1) as i:
                unit(i, 0)
                unit(i, 1)
            unit(B - 1, 0, more=False)
            unit(B - 1, 1, more=False)
            wait_apart(sp, out_st[0], 16 * B)
            wait_apart(sp, out_st[1], 16 * B)

        @block.scalar
        def _(act):
            def normalise(t, u):
                return nc.scalar.activation(xr[:, u, :], xs[:, bass.ds(t, 1), :].rearrange("p a e -> p (a e)"),
                                            ACT.Identity, bias=xshift[:, bass.ds(t, 1)], scale=xscale[:, bass.ds(t, 1)])

            def tile_a(i, u, more=True):
                t = 2 * i + u
                if more:
                    act.wait_ge(group_of, t + 2)
                    if not (isinstance(i, int) and t == 0):
                        act.wait_ge(xT_ps, t)
                    normalise(t + 1, 1 - u).then_inc(xr_done, 1)
                act.wait_ge(xT_ps, t + 1)
                if not (isinstance(i, int) and i == 0):
                    act.wait_ge(qkv_ps, t - 1)
                    act.wait_ge(xc_st[u], 16 * i)
                nc.scalar.activation(xT[:, u].rearrange("p k n -> p (k n)"), psM[:, u, 0:KE * P], ACT.Copy).then_inc(xT_done, 1)

            def cast(i, u):
                act.wait_ge(pm_in[u], 16 * (i + 1))
                for t, g0 in ((0, 0), (1, 2)):
                    src = pm[:, u, :, t * D:(t + 1) * D].unsqueeze(2).to_broadcast([P, 32, 3, D])
                    nc.scalar.activation(partsb[:, u, :, g0:g0 + 3, :, t], src, ACT.Copy).then_inc(cast_done, 1)

            def values(i, u):
                act.wait_ge(pm_in[u], 16 * (i + 1))
                nc.scalar.activation(vext[:, u, :, 0:D], pm[:, u, :, 2 * D:3 * D], ACT.Copy).then_inc(v_done, 1)

            act.wait_ge(group_of, 1)
            normalise(0, 0).then_inc(xr_done, 1)
            tile_a(0, 0)
            tile_a(0, 1)
            with act.Fori(1, NT // 8) as i:
                tile_a(i, 0)
                tile_a(i, 1)
            for u in range(2):
                act.wait_ge(qkv_st[0], 16 * (u + 1))
                act.wait_ge(qkv_st[1], 16 * (u + 1))
                act.dma_start(pm[:, u, :, :], pm_rows[u:u + 1].rearrange("a p n f -> (a p) n f")).then_inc(pm_in[u], 16)
            with act.Fori(NT // 8, NT // 4) as i:
                tile_a(i, 0)
                tile_a(i, 1)
            act.wait_ge(dconst, N_DCONST)
            cast(0, 0)
            with act.Fori(NT // 4, NT // 2 - 1) as i:
                tile_a(i, 0)
                tile_a(i, 1)
            tile_a(NT // 2 - 1, 0)
            tile_a(NT // 2 - 1, 1, more=False)
            values(0, 0)
            cast(0, 1)

            def exps(i, u, j):
                q = 2 * i + u
                kb, heads, a, n = EXPS[j]
                act.wait_ge(qk_ps, NE * q + j + 1)
                if j == 0 or EXPS[j - 1][0] != kb:
                    if kb >= 3:
                        act.wait_ge(pv_done, NPV * q + PVS_OF[kb - 3])
                    elif not (isinstance(i, int) and q == 0):
                        act.wait_ge(pv_done, NPV * (q - 1) + PVS_OF[(6, 7, 5)[kb]])
                src = psE[:, (NE * u + j) % ES, 0:len(heads) * n].rearrange("p (c n) -> p c n", n=n)
                dst = strip_at[kb][:, heads[0]:heads[-1] + 1, a:a + n]
                nc.scalar.activation(dst, src, ACT.Exp, scale=SCALE).then_inc(exp_done, 1)

            def outputs(i, u):
                q = 2 * i + u
                act.wait_ge(pv_done, NPV * (q + 1))
                if not (isinstance(i, int) and q == 0):
                    s, at = ring_at((i, u), ("OT", 1))
                    act.wait_ge(full[s], at + 1)
                nc.scalar.activation(osb[:, :], psO[:, :, :].rearrange("p h n -> p (h n)"), ACT.Copy).then_inc(osb_done, 1)

            def route_exp(r):
                act.wait_ge(rz_done, 4 * r + 3)
                nc.scalar.activation(re[:, :], rz[:, :], ACT.Exp, scale=1.0 / EPS_ROUTE, accum_out=rsum[:, :]).then_inc(re_done, 1)

            def route_ln(step, k):
                s, at = ring_at(step, ("R", k))
                act.wait_ge(full[s], at + 1)
                nc.scalar.activation(lns[:, :], psM[:, s, 0:1], ACT.Ln).then_inc(free[s], 1)

            def step(ring, where, i, u, late=True, load=True, value=True):
                r = 6 * i + 3 * u
                for item in timeline(ring, late, load):
                    if item[0] == "E":
                        exps(i, u, item[1])
                    elif item[0] == "OUT":
                        outputs(i if u else i - 1, 1 - u)
                    elif item[0] == "VALUES" and value:
                        values(i if u == 0 else i + 1, 1 - u)
                    elif item[0] == "CAST":
                        cast(i + 1, u)
                    elif item[0] == "RX":
                        route_exp(r + item[1])
                    elif item[0] == "R":
                        route_ln(where, item[1])

            nc.scalar.preload_act_table_set("natural_log_exp_and_others")
            act.wait_ge(smax_done, 1)
            step(ring_steady, (0, 0), 0, 0, late=False)
            step(ring_steady, (0, 1), 0, 1)
            with act.Fori(1, NQ // 2 - 1) as i:
                step(ring_steady, (i, 0), i, 0)
                step(ring_steady, (i, 1), i, 1)
            li = NQ // 2 - 1
            step(ring_steady, (li, 0), li, 0, load=False)
            step(ring_last, NQ - 1, li, 1, load=False, value=False)
            act.wait_ge(pv_done, NPV * NQ)
            s, at = ring_at(NQ - 1, ("OT", 1))
            act.wait_ge(full[s], at + 1)
            nc.scalar.activation(osb[:, :], psO[:, :, :].rearrange("p h n -> p (h n)"), ACT.Copy).then_inc(osb_done, 1)

            def hidden(i, u):
                act.wait_ge(h_ps, 2 * i + u + 1)
                if not (isinstance(i, int) and i == 0):
                    act.wait_ge(o_ps, 8 * (i - 1) + 4 * u + 4)
                nc.scalar.activation(hT[:, u, :], psO[:, u, :], ACT.Gelu, bias=b1l[:, 0:1]).then_inc(h_done, 1)

            def unit(i, u, more=True):
                for t in range(4):
                    n = 8 * i + 4 * u + t
                    act.wait_ge(saT_ps, n + 1)
                    if not (isinstance(i, int) and n < 2):
                        act.wait_ge(o_ps, n - 1)
                    nc.scalar.activation(saT[:, t % 2, :], psM[:, t % 2, 0:KE * P], ACT.Copy).then_inc(saT_done, 1)
                    if t == 1 and more:
                        hidden(i if u == 0 else i + 1, 1 - u)

            hidden(0, 0)
            unit(0, 0)
            unit(0, 1)
            with act.Fori(1, B - 1) as i:
                unit(i, 0)
                unit(i, 1)
            unit(B - 1, 0)
            unit(B - 1, 1, more=False)

            act.wait_ge(ob_done, NT)
            for h in range(2):
                for t in range(4):
                    st = 4 * h + t
                    act.wait_ge(gT_ps, st + 1)
                    nc.scalar.activation(xgT[:, :, st * P:(st + 1) * P], psM[:, st % 2, 0:KE * P].rearrange(
                        "p (k n) -> p k n", k=KE), ACT.Copy).then_inc(gT_done, 1)
                for c in range(NHC):
                    m = NHC * h + c
                    act.wait_ge(hh_ps, m + 1)
                    nc.scalar.activation(hidT[:, c, h * 512:(h + 1) * 512], psO[:, m % 2, :], ACT.Gelu,
                                         bias=b1h[:, c:c + 1]).then_inc(hh_done, 1)
                if h == 0:
                    act.wait_ge(gu_done, 2 * NSLOT + 2)
                    nc.scalar.activation(gscore[:, :], gu[:, :], ACT.Exp, scale=1.0 / EPS_ROUTE).then_inc(gs_done, 1)

        @block.tensor
        def _(pe):
            pe.wait_ge(consts, 2)

            def transposes_a(i, u):
                t = 2 * i + u
                pe.wait_ge(xr_done, t + 1)
                if not (isinstance(i, int) and i == 0):
                    pe.wait_ge(xT_done, t - 1)
                for k in range(KE):
                    mm = pe.transpose(psM[:, u, k * P:(k + 1) * P], xr[:, u, k * P:(k + 1) * P], ident[:, :])
                mm.then_inc(xT_ps, 1)

            def project(i, u):
                t = 2 * i + u
                pe.wait_ge(xT_done, t + 1)
                if isinstance(i, int) and t == 0:
                    pe.wait_ge(wa_in, 48)
                if not (isinstance(i, int) and i == 0):
                    pe.wait_ge(qkv_done, t - 1)
                for h in range(2):
                    n = HW + h
                    for k in range(KE):
                        mm = pe.matmul(psA[u][:, h, 0:n], xT[:, u, k, :], w_qkv[:, k, HW * h:HW * h + n],
                                       start=(k == 0), stop=(k == KE - 1))
                mm.then_inc(qkv_ps, 1)

            def tile_a(i, u, more=True):
                if more:
                    transposes_a(i if u == 0 else i + 1, 1 - u)
                project(i, u)

            transposes_a(0, 0)
            tile_a(0, 0)
            tile_a(0, 1)
            with pe.Fori(1, NT // 2 - 1) as i:
                tile_a(i, 0)
                tile_a(i, 1)
            tile_a(NT // 2 - 1, 0)
            tile_a(NT // 2 - 1, 1, more=False)

            def ring_item(step, fi, fu, f, item, r=None):
                s, at = ring_at(step, ("OT", item[1]) if item[0] == "SKIP" else item)
                if not (isinstance(at, int) and at == 0):
                    pe.wait_ge(free[s], at)
                kind = item[0]
                if kind == "T":
                    _, c, h = item
                    if c == 0 and h == 0:
                        pe.wait_ge(split_done, 5 * f + 5)
                    for b in range(4):
                        n = 8 * c + 4 * h + b
                        mm = pe.transpose(psM[0:W, s, b * P:(b + 1) * P], parts[:, fu, n * W:(n + 1) * W], ident[:, :])
                elif kind == "C":
                    _, c, k = item
                    qb, k0, n, _d = CHUNKS[k]
                    if k in (0, 4):
                        ts, tat = ring_at(step, ("T", c, 0 if k == 0 else 1))
                        pe.wait_ge(free[ts], tat + 1)
                    mm = pe.matmul(psM[:, s, 0:n], QTb[0:W, fu, c * 1024 + qb * P:c * 1024 + (qb + 1) * P, 0],
                                   QTb[0:W, fu, c * 1024 + k0:c * 1024 + k0 + n, 1], start=True, stop=True)
                elif kind == "MT":
                    c = item[1]
                    pe.wait_ge(mw_done, 4 * (4 * (f - 1 if c == 3 else f) + c + 1))
                    mm = pe.transpose(psM[0:24, s, 0:P], mW[:, c, :], ident[:, :])
                elif kind == "OT":
                    h = item[1]
                    pe.wait_ge(osb_done, f - 1)
                    for b in range(4):
                        mm = pe.transpose(psM[:, s, b * P:(b + 1) * P], osb[:, (4 * h + b) * P:(4 * h + b + 1) * P], ident[:, :])
                elif kind == "R":
                    pe.wait_ge(re_done, r + 1)
                    mm = pe.matmul(psM[:, s, 0:1], blockones[:, :], rsum[:, :], start=True, stop=True)
                else:
                    mm = pe.transpose(psM[0:24, s, 0:P], ident[:, 0:24], ident[:, :])
                mm.then_inc(full[s], 1)

            def scores(i, u, j):
                q = 2 * i + u
                kb, heads, a, n = EXPS[j]
                if not (isinstance(i, int) and q == 0 and j < ES):
                    pe.wait_ge(exp_done, NE * q + j + 1 - ES)
                if kb == 0 and a == 0:
                    pe.wait_ge(m_in[heads[0]], 16 * (q + 1))
                for k, c in enumerate(heads):
                    q0 = c * 1024 + kb * P + a
                    mm = pe.matmul(psE[:, (NE * u + j) % ES, k * n:(k + 1) * n],
                                   QTb[0:W + 3, u, c * 1024 + kb * P:c * 1024 + (kb + 1) * P, 1],
                                   QTb[0:W + 3, u, q0:q0 + n, 0], start=True, stop=True)
                mm.then_inc(qk_ps, 1)

            def product(i, u, kb, h):
                q = 2 * i + u
                w = (8 - kb) * P
                pe.wait_ge(mask_done, 8 * q + kb + 1)
                if kb == 0 and h == 0:
                    pe.wait_ge(v_done, q + 1)
                    if not (isinstance(i, int) and q == 0):
                        pe.wait_ge(osb_done, q)
                q0 = max(kb * P, 512 * h)
                n = 512 * (h + 1) - q0
                for c in range(4):
                    mm = pe.matmul(psO[32 * c:32 * c + 32, h, q0 - 512 * h:512], vext[:, u, 8 * c + kb, :],
                                   strip_at[kb][:, c, q0 - kb * P:q0 - kb * P + n],
                                   start=(kb == 0), stop=(kb == 4 * h + 3), skip_group_check=True)
                mm.then_inc(pv_done, 1)

            pe.wait_ge(dconst, N_DCONST)
            for item in ring_first:
                ring_item(-1, 0, 0, 0, item)

            def step(ring, where, i, u, late=True, load=True):
                for item in timeline(ring, late, load):
                    if item[0] == "E":
                        scores(i, u, item[1])
                    elif item[0] == "PV" and item[3] == 0:
                        product(i, u, item[1], item[2])
                    elif item[0] == "PV":
                        product(i if u else i - 1, 1 - u, item[1], item[2])
                    elif item[0] in ("T", "C", "MT", "OT", "R", "SKIP", "NOP"):
                        ring_item(where, i if u == 0 else i + 1, 1 - u, 2 * i + u + 1, item,
                                  6 * i + 3 * u + item[1] if item[0] == "R" else None)

            step(ring_steady, (0, 0), 0, 0, late=False)
            step(ring_steady, (0, 1), 0, 1)
            with pe.Fori(1, NQ // 2 - 1) as i:
                step(ring_steady, (i, 0), i, 0)
                step(ring_steady, (i, 1), i, 1)
            li = NQ // 2 - 1
            step(ring_steady, (li, 0), li, 0, load=False)
            step(ring_last, NQ - 1, li, 1, load=False)
            product(li, 1, 6, 1)
            product(li, 1, 7, 1)

            def light_hidden(i, u):
                if isinstance(i, int) and i == 0:
                    pe.wait_ge(osb_done, NQ)
                    pe.wait_ge(fold_done, N_FOLD - 1)
                    pe.wait_ge(wd_in, 16 * 7)
                    pe.wait_ge(xc_st[0], 16 * (NT // 2))
                    pe.wait_ge(xc_st[1], 16 * (NT // 2))
                else:
                    pe.wait_ge(h_done, 2 * (i - 1) + u + 1)
                for k in range(KE):
                    mm = pe.matmul(psO[:, u, :], w1l[:, k, :], xrT[:, k, bass.ds(1024 * i + 512 * u, 512)],
                                   start=(k == 0), stop=(k == KE - 1))
                mm.then_inc(h_ps, 1)

            light_hidden(0, 0)
            for h in range(2):
                s, at = final_ot(h)
                pe.wait_ge(free[s], at)
                for b in range(4):
                    mm = pe.transpose(psM[:, s, b * P:(b + 1) * P], osb[:, (4 * h + b) * P:(4 * h + b + 1) * P], ident[:, :])
                mm.then_inc(full[s], 1)
            light_hidden(0, 1)

            def transposes_c(i, u, t):
                n = 8 * i + 4 * u + t
                if t == 0:
                    pe.wait_ge(c_in[u], 16 * (i + 1))
                if not (isinstance(i, int) and n < 2):
                    pe.wait_ge(saT_done, n - 1)
                elif n == 0:
                    for h in range(2):
                        s, at = final_ot(h)
                        pe.wait_ge(free[s], at + 1)
                for k in range(KE):
                    mm = pe.transpose(psM[:, t % 2, k * P:(k + 1) * P], sa_in[:, u, t, k * P:(k + 1) * P], ident[:, :])
                mm.then_inc(saT_ps, 1)

            def project_c(i, u, t):
                n = 8 * i + 4 * u + t
                o = psC[:, t, 0:E]
                if t == 0:
                    pe.wait_ge(h_done, 2 * i + u + 1)
                if not (isinstance(i, int) and n < 4):
                    pe.wait_ge(ob_done, n - 3)
                pe.matmul(o, hT[:, u, t * P:(t + 1) * P], w2l, start=True, stop=False)
                pe.wait_ge(saT_done, n + 1)
                for k in range(KE):
                    mm = pe.matmul(o, saT[:, t % 2, k * P:(k + 1) * P], wout[:, k, :], start=False, stop=(k == KE - 1))
                mm.then_inc(o_ps, 1)

            def unit(i, u, more=True):
                for t in range(4):
                    if t < 3:
                        transposes_c(i, u, t + 1)
                    elif more:
                        transposes_c(i if u == 0 else i + 1, 1 - u, 0)
                    project_c(i, u, t)
                    if t == 0 and more and not (isinstance(i, int) and i == 0 and u == 0):
                        light_hidden(i if u == 0 else i + 1, 1 - u)

            transposes_c(0, 0, 0)
            unit(0, 0)
            unit(0, 1)
            with pe.Fori(1, B - 1) as i:
                unit(i, 0)
                unit(i, 1)
            unit(B - 1, 0)
            unit(B - 1, 1, more=False)

            for st in range(NSLOT):
                b, hh = st // 2, st % 2
                if hh == 0:
                    pe.wait_ge(hot_done, 8 * (b + 1))
                if st == 0:
                    pe.wait_ge(saT_done, NT)
                    pe.wait_ge(consts, N_CONST)
                for k in range(8):
                    mm = pe.matmul(psM[:, 0, 2 * st:2 * st + 2], hotb[:, 8 * b + k, hh * P:(hh + 1) * P],
                                   tokid[:, :, 8 * b + k], start=(k == 0), stop=(k == 7))
            mm.then_inc(idx_ps, 1)

            for h in range(2):
                for t in range(4):
                    st = 4 * h + t
                    pe.wait_ge(gn_done, st + 1)
                    if st >= 2:
                        pe.wait_ge(gT_done, st - 1)
                    elif st == 0:
                        pe.wait_ge(idx_done, 2)
                    for k in range(KE):
                        mm = pe.transpose(psM[:, st % 2, k * P:(k + 1) * P], xgn[:, st, k * P:(k + 1) * P], ident[:, :])
                    mm.then_inc(gT_ps, 1)
                pe.wait_ge(gT_done, 4 * h + 4)
                for c in range(NHC):
                    m = NHC * h + c
                    if m >= 2:
                        pe.wait_ge(hh_done, m - 1)
                    for k in range(KE):
                        mm = pe.matmul(psO[:, m % 2, :], w1h[:, k, c * P:(c + 1) * P], xgT[:, k, h * 512:(h + 1) * 512],
                                       start=(k == 0), stop=(k == KE - 1))
                    mm.then_inc(hh_ps, 1)
                for t in range(4):
                    st = 4 * h + t
                    o = psC[:, t, 0:E]
                    if st >= 4:
                        pe.wait_ge(hv_half, st - 3)
                    else:
                        pe.wait_ge(ob_done, NT)
                    for c in range(NHC):
                        pe.wait_ge(hh_done, NHC * h + c + 1)
                        mm = pe.matmul(o, hidT[:, c, st * P:(st + 1) * P], w2h[:, c, :], start=(c == 0), stop=(c == NHC - 1))
                    mm.then_inc(ho_ps, 1)

        @block.vector
        def _(dve):
            def const(ins):
                ins.then_inc(dconst, 1)

            const(dve.memset(vext[:, :, :, :], 0.0))
            const(dve.memset(blockones[:, :], 0.0))
            const(dve.memset(mWb[:, :, :, :, 1], 1.0))
            const(dve.memset(mx[:, :, :, :], MASKED))
            const(dve.memset(rank3[:, :, :], 0.0))
            dve.wait_ge(dconst, 2)
            const(dve.memset(vext[:, :, :, D:D + 1], 1.0))
            for b in range(4):
                const(dve.memset(blockones[32 * b:32 * b + 32, 32 * b:32 * b + 32], 1.0))
            const(dve.memset(mWb[:, :, :, :, 0], 0.0))

            def stats(g, n):
                if n == GROUPS[g][0]:
                    dve.wait_ge(x_in[g], 16)
                nc.vector.bn_stats(bn6[:, n, :], xs[:, n, :]).then_inc(bn_done, 1)
                dve.wait_ge(bn_done, 2 * n + 1)
                nc.vector.bn_aggr(mv[:, n, :], bn6[:, n, :]).then_inc(bn_done, 1)

            def invert(g):
                dve.wait_ge(stat_done, ST * g + 5)
                c = slice(GROUPS[g][0], sum(GROUPS[g]))
                nc.vector.reciprocal(rnrm[:, c], nrm[:, c]).then_inc(nrm_inv, 1)

            def evacuate(i, u):
                t = 2 * i + u
                dve.wait_ge(qkv_ps, t + 1)
                if not (isinstance(i, int) and i == 0):
                    dve.wait_ge(qkv_st[u], 16 * i)
                nc.vector.tensor_scalar(s_tok[:, bass.ds(t, 1)], psA[u][:, 1, HW:HW + 1], unscale[:, bass.ds(t, 1)], None,
                                        ALU.mult)
                nc.vector.scalar_tensor_tensor(out=qkvs[:, u, :].rearrange("p (h n) -> p h n", h=2), in0=psA[u][:, :, 0:HW],
                                               scalar=unscale[:, bass.ds(t, 1)],
                                               in1=bias_qkv.rearrange("p (h n) -> p h n", h=2),
                                               op0=ALU.mult, op1=ALU.add).then_inc(qkv_done, 1)

            for g in range(2):
                for t in range(GROUPS[g][1]):
                    stats(g, GROUPS[g][0] + t)
                invert(g)
            dve.wait_ge(wa_in, 48)
            rest = [(g, n) for g in (2, 3) for n in range(GROUPS[g][0], sum(GROUPS[g]))]
            for t in range(8):
                if t in (0, GROUPS[1][0]):
                    dve.wait_ge(stat_done, ST * (1 if t == 0 else 2))
                evacuate(t // 2, t % 2)
                for g, n in rest[4 * t:4 * t + 4]:
                    stats(g, n)
                if t == 3:
                    invert(2)
                if t == 7:
                    invert(3)
            dve.wait_ge(stat_done, ST * 4)
            with dve.Fori(4, NT // 2) as i:
                evacuate(i, 0)
                evacuate(i, 1)

            def ring_item(step, fu, f, late_m, late_u, item):
                s, at = ring_at(step, ("OT", item[1]) if item[0] == "SKIP" else item)
                kind = item[0]
                if kind == "C" and CHUNKS[item[2]][3]:
                    wait_apart(dve, full[s], at + 1)
                else:
                    dve.wait_ge(full[s], at + 1)
                if kind == "T":
                    _, c, h = item
                    q0 = c * 1024 + h * 512
                    nc.vector.tensor_copy(QT[0:W, fu, q0:q0 + 512], psM[0:W, s, :]).then_inc(free[s], 1)
                elif kind == "C":
                    _, c, k = item
                    qb, k0, n, diag = CHUNKS[k]
                    if k == 0 and not (isinstance(f, int) and f == 0):
                        wait_apart(dve, nm_done, 4 * (f - 1) + c + 1)
                    acc = mx[:, c, qb, k0 // 512:k0 // 512 + 1]
                    if diag:
                        nc.vector.tensor_tensor_reduce(psM[:, s, 0:n], psM[:, s, 0:n], maskrow[:, 512 - n:512], 1.0, MASKED,
                                                       ALU.add, ALU.max, acc).then_inc(free[s], 1)
                    else:
                        nc.vector.tensor_reduce(acc, psM[:, s, 0:n], AX.X, ALU.max).then_inc(free[s], 1)
                    if k == 11:
                        for kk in (9, 10, 11):
                            ss, aa = ring_at(step, ("C", c, kk))
                            dve.wait_ge(free[ss], aa + 1)
                        nc.vector.tensor_reduce(nm[:, c, :], mx[:, c, :, :], AX.X, ALU.max, negate=True).then_inc(nm_done, 1)
                elif kind == "MT":
                    nc.vector.tensor_copy(mT[:, item[1], :], psM[0:24, s, 0:P]).then_inc(free[s], 1)
                elif kind == "OT":
                    normalise(late_m, late_u, item[1], s)
                else:
                    nc.vector.tensor_copy(skipped[:, s:s + 1], psM[0:24, s, 0:1]).then_inc(free[s], 1)

            def normalise(m, u, h, s):
                o = psM[:, s, :].rearrange("p (n c w) -> p n c w", n=4, c=4)
                nc.vector.reciprocal(rden[:, h], o[:, :, :, D]).then_inc(rden_done, 1)
                dve.wait_ge(rden_done, 4 * m + 2 * u + h + 1)
                if h == 0:
                    dve.wait_ge(sa_st[u], 16 * (m + 1))
                nc.vector.tensor_tensor(pmo[:, u, :, 4 * h:4 * h + 4, :].rearrange("p c n d -> p n c d"), o[:, :, :, 0:D],
                                        rden[:, h].unsqueeze(3).to_broadcast([P, 4, 4, D]), ALU.mult).then_inc(free[s], 1)

            for item in ring_first:
                ring_item(-1, 0, 0, None, None, item)
            dve.wait_ge(route_in, 16 * 5)
            nc.vector.tensor_reduce(smax[:, :], xs[:, 0:4, :].rearrange("p t e -> p (t e)"), AX.X, ALU.max).then_inc(smax_done, 1)

            def step(ring, where, i, u, late=True, load=True):
                for item in timeline(ring, late, load):
                    if item[0] in ("T", "C", "MT", "OT", "SKIP", "NOP"):
                        ring_item(where, 1 - u, 2 * i + u + 1, i if u else i - 1, 1 - u, item)

            step(ring_steady, (0, 0), 0, 0, late=False)
            step(ring_steady, (0, 1), 0, 1)
            with dve.Fori(1, NQ // 2 - 1) as i:
                step(ring_steady, (i, 0), i, 0)
                step(ring_steady, (i, 1), i, 1)
            li = NQ // 2 - 1
            step(ring_steady, (li, 0), li, 0, load=False)
            step(ring_last, NQ - 1, li, 1, load=False)
            for h in range(2):
                s, at = final_ot(h)
                dve.wait_ge(full[s], at + 1)
                normalise(NQ // 2 - 1, 1, h, s)

            dve.wait_ge(na_in, 16)
            nc.vector.tensor_scalar(nlo_all[:, :], na_all[:, :], EPS_ROUTE * EXP_FLOOR, None, ALU.add).then_inc(nlo_done, 1)
            dve.wait_ge(nlo_done, 1)

            def ranking(i, u, t):
                k = 4 * u + t
                at = RK * i + 2 + RK_AT[k]
                kp = keyc[:, k:k + 1]
                dve.wait_ge(rk, at)
                if k > 0:
                    nc.vector.tensor_scalar(junk[:, 0:k * P], keyr[:, 0:k * P], kp, 0.0, ALU.is_ge, ALU.add,
                                            accum_out=rank3[:, 0, k:k + 1]).then_inc(rk, 1)
                    at += 1
                    dve.wait_ge(rk, at)
                nc.vector.tensor_scalar(junk[:, k * P:S], keyr[:, k * P:S], kp, 0.0, ALU.is_gt, ALU.add,
                                        accum_out=rank3[:, 1, k:k + 1]).then_inc(rk, 1)
                dve.wait_ge(rk, at + 1)
                nc.vector.scalar_tensor_tensor(out=junk[:, k * P:(k + 1) * P], in0=keyr[:, k * P:(k + 1) * P], scalar=kp,
                                               in1=below[:, :], op0=ALU.is_equal, op1=ALU.mult,
                                               accum_out=rank3[:, 2, k:k + 1]).then_inc(rk, 1)

            def unit(i, u):
                for t in range(4):
                    n = 8 * i + 4 * u + t
                    if t == 0:
                        dve.wait_ge(c_x, 2 * i + u + 1)
                        if not (isinstance(i, int) and i == 0):
                            dve.wait_ge(out_st[u], 16 * i)
                    dve.wait_ge(o_ps, n + 1)
                    nc.vector.tensor_tensor(ob[:, u, t, :], psC[:, t, 0:E], x_in2[:, u, t, :], ALU.add
                                            ).then_inc(ob_done, 1)
                    if u == 0 and t == 0:
                        dve.wait_ge(key_in, 16 * (i + 1))
                        lo, hi = nlo_all[:, bass.ds(i, 1)], na_all[:, bass.ds(i, 1)]
                        nc.vector.tensor_scalar(keyr[:, :], keyr[:, :], hi, lo, ALU.min, ALU.max).then_inc(rk, 1)
                        nc.vector.tensor_scalar(keyc[:, :], s_tok[:, bass.ds(8 * i, 8)], hi, lo, ALU.min, ALU.max).then_inc(rk, 1)
                    ranking(i, u, t)
                if u == 1:
                    at = RK * i + 2 + RK_AT[8]
                    dve.wait_ge(rk, at)
                    nc.vector.tensor_tensor(rank[:, :], rank3[:, 0, :], rank3[:, 1, :], ALU.add).then_inc(rk, 1)
                    dve.wait_ge(rk, at + 1)
                    nc.vector.tensor_tensor(rank[:, :], rank[:, :], rank3[:, 2, :], ALU.add).then_inc(rk, 1)
                    dve.wait_ge(rk, at + 2)
                    for k in range(8):
                        nc.vector.tensor_scalar(hotb[:, bass.ds(8 * i + k, 1), :].rearrange("p a n -> p (a n)"), iota256[:, :],
                                                rank[:, k:k + 1], None, ALU.is_equal).then_inc(hot_done, 1)

            dve.wait_ge(consts, N_CONST)
            unit(0, 0)
            unit(0, 1)
            with dve.Fori(1, B) as i:
                unit(i, 0)
                unit(i, 1)

            dve.wait_ge(idx_ps, 1)
            ip = psM[:, 0, 0:2 * NSLOT].rearrange("p (s w) -> p s w", w=2)
            nc.vector.tensor_scalar(idxf[:, :], ip[:, :, 0], float(P), None, ALU.mult).then_inc(idx_done, 1)
            dve.wait_ge(idx_done, 1)
            nc.vector.tensor_tensor(idx[:, :], idxf[:, :], ip[:, :, 1], ALU.add).then_inc(idx_done, 1)

            for h in range(2):
                for t in range(4):
                    st = 4 * h + t
                    dve.wait_ge(g_in[st], 16)
                    nc.vector.bn_stats(bn6[:, st, :], xg[:, st, :]).then_inc(gx_done, 1)
                    dve.wait_ge(gx_done, 9 * h + 2 * t + 1)
                    nc.vector.bn_aggr(mv[:, st, :], bn6[:, st, :]).then_inc(gx_done, 1)
                dve.wait_ge(gp_done, ST * h + 5)
                nc.vector.reciprocal(rnrm[:, 4 * h:4 * h + 4], nrm[:, 4 * h:4 * h + 4]).then_inc(gx_done, 1)
                dve.wait_ge(gp_done, ST * (h + 1))
                for t in range(4):
                    st = 4 * h + t
                    nc.vector.tensor_scalar(xgn[:, st, :], xg[:, st, :], xscale[:, st:st + 1], xshift[:, st:st + 1],
                                            ALU.mult, ALU.add).then_inc(gn_done, 1)
            for st in range(NSLOT):
                dve.wait_ge(gn_done, st + 1)
                nc.vector.tensor_tensor_reduce(xg[:, st, :], xgn[:, st, :], rt_row, 1.0, 0.0, ALU.mult, ALU.add,
                                               gdot[:, st:st + 1]).then_inc(gu_done, 1)
            dve.wait_ge(gu_done, NSLOT)
            for st in range(NSLOT):
                nc.vector.tensor_scalar(gu[:, st:st + 1], gdot[:, st:st + 1], unscale[:, st:st + 1],
                                        na_all[:, st // 2:st // 2 + 1], ALU.mult, ALU.subtract).then_inc(gu_done, 1)
            dve.wait_ge(gu_done, 2 * NSLOT)
            nc.vector.tensor_scalar(gu[:, :], gu[:, :], 0.0, None, ALU.min).then_inc(gu_done, 1)
            dve.wait_ge(gu_done, 2 * NSLOT + 1)
            nc.vector.tensor_scalar(gu[:, :], gu[:, :], 1.0, None, ALU.mult).then_inc(gu_done, 1)
            dve.wait_ge(gs_done, 1)
            nc.vector.tensor_scalar(gw[:, :], gscore[:, :], -1.0, 1.0, ALU.mult, ALU.add).then_inc(gu_done, 1)
            dve.wait_ge(gu_done, 2 * NSLOT + 3)
            nc.vector.tensor_tensor(gw[:, :], gw[:, :], gscore[:, :], ALU.add).then_inc(gu_done, 1)
            dve.wait_ge(gu_done, 2 * NSLOT + 4)
            for st in range(NSLOT):
                t = st % 4
                dve.wait_ge(ho_ps, st + 1)
                nc.vector.tensor_tensor(hv[:, st, :], psC[:, t, 0:E], bias_h, ALU.add).then_inc(hv_half, 1)
                dve.wait_ge(hv_half, st + 1)
                nc.vector.tensor_scalar(hv[:, st, :], hv[:, st, :], gw[:, st:st + 1], None, ALU.mult).then_inc(hv_done, 1)

        @block.gpsimd
        def _(pool):
            def const(ins, n=[0]):
                ins.then_inc(consts, 1)
                n[0] += 1
                return n[0]

            const(pool.memset(ident[:, :], 1.0))
            pool.wait_ge(consts, 1)
            const(pool.affine_select(out=ident[:, :], in_=ident[:, :], pattern=[[-1, P]], compare_op=ALU.is_equal,
                                     fill=0.0, base=0, channel_multiplier=1))
            const(pool.memset(halfpow[:, 0, :], -0.5))
            const(pool.memset(halfpow[:, 1, :], 0.5))
            pool.wait_ge(consts, 4)

            def factors(a, n, base, done, size):
                var, mean = mv[:, a:a + n, 1], mv[:, a:a + n, 0]
                c = slice(a, a + n)

                def then(ins, k):
                    ins.then_inc(done, 1)
                    pool.wait_ge(done, base + k)

                pool.tensor_scalar(veps[:, 0, c], var, EPS_LN, None, ALU.add).then_inc(done, 1)
                then(pool.tensor_scalar(veps[:, 1, c], var, VAR_FLOOR, None, ALU.max), 2)
                then(pool.tensor_tensor(roots[:, :, c], veps[:, :, c], halfpow[:, :, c], ALU.pow), 3)
                then(pool.tensor_tensor(nrm[:, c], roots[:, 0, c], roots[:, 1, c], ALU.mult), 4)
                then(pool.tensor_scalar(nrm[:, c], nrm[:, c], float(E) ** 0.5, 1e-12, ALU.mult, ALU.max), 5)
                pool.tensor_scalar(unscale[:, c], nrm[:, c], float(E) ** -0.5, None, ALU.mult).then_inc(done, 1)
                pool.wait_ge(*size)
                then(pool.tensor_tensor(xscale[:, c], roots[:, 0, c], rnrm[:, c], ALU.mult), 7)
                then(pool.tensor_scalar(xscale[:, c], xscale[:, c], float(E) ** 0.5, None, ALU.mult), 8)
                then(pool.tensor_tensor(xshift[:, c], mean, xscale[:, c], ALU.mult), 9)
                then(pool.tensor_scalar(xshift[:, c], xshift[:, c], -1.0, None, ALU.mult), 10)

            for g, (a, n) in enumerate(GROUPS):
                pool.wait_ge(bn_done, 2 * (a + n))
                factors(a, n, ST * g, stat_done, (nrm_inv, g + 1))
                pool.sem_inc(group_of, n)

            const(pool.memset(maskrow[:, :], 0.0))
            const(pool.memset(below[:, :], 1.0))
            pool.wait_ge(consts, 6)
            const(pool.affine_select(out=maskrow[:, 512 - P:512], in_=maskrow[:, 512 - P:512], pattern=[[-1, P]],
                                     compare_op=ALU.is_ge, fill=MASKED, base=0, channel_multiplier=1))
            const(pool.affine_select(out=below[:, :], in_=below[:, :], pattern=[[-1, P]], compare_op=ALU.is_gt,
                                     fill=0.0, base=0, channel_multiplier=1))
            const(pool.iota(iota_i[:, :], pattern=[[1, NUM_HEAVY]], base=0, channel_multiplier=0))
            const(pool.iota(tokid_i[:, 0, :], pattern=[[1, NT]], base=0, channel_multiplier=0))
            const(pool.iota(tokid_i[:, 1, :], pattern=[[0, NT]], base=0, channel_multiplier=1))
            pool.wait_ge(consts, 11)
            const(pool.tensor_copy(iota256[:, :], iota_i[:, :]))
            const(pool.tensor_copy(tokid[:, :, :], tokid_i[:, :, :]))

            pool.wait_ge(wc_in, 16 * 6)
            for k in range(KE):
                pool.tensor_scalar(w1l[:, k, :], w1l[:, k, :], gl[:, k:k + 1], None, ALU.mult).then_inc(fold_done, 1)
                pool.tensor_scalar(w1h[:, k, :], w1h[:, k, :], gh[:, k:k + 1], None, ALU.mult).then_inc(fold_done, 1)

            def second(i, u, t):
                q = 2 * i + u
                pool.wait_ge(cast_done, 2 * q + 1 + t)
                x_ = pm[:, u, :, t * D:(t + 1) * D].unsqueeze(2).to_broadcast([P, 32, 2, D])
                p1 = partsb[:, u, :, 2:3, :, t].to_broadcast([P, 32, 2, D])
                dst = partsb[:, u, :, 3:6:2, :, t] if t == 0 else partsb[:, u, :, 1:6:4, :, t]
                pool.tensor_tensor(dst, x_, p1, ALU.subtract).then_inc(split_done, 1)

            def rest(i, u):
                pool.tensor_tensor(r1[:, :, :].rearrange("p n (t e) -> p n t e", t=2),
                                   pm[:, u, :, 0:2 * D].rearrange("p n (t e) -> p n t e", t=2),
                                   partsb[:, u, :, 2, :, :].rearrange("p n e t -> p n t e"), ALU.subtract).then_inc(split_done, 1)

            def third(i, u, t):
                pool.wait_ge(split_done, 5 * (2 * i + u) + 3)
                pool.tensor_tensor(partsb[:, u, :, 4 if t == 0 else 0, :, t], r1[:, :, t * D:(t + 1) * D],
                                   partsb[:, u, :, 5, :, t], ALU.subtract).then_inc(split_done, 1)

            for u in range(2):
                second(0, u, 0)
                second(0, u, 1)
                if u == 1:
                    pool.wait_ge(split_done, 5)
                rest(0, u)
                third(0, u, 0)
                third(0, u, 1)

            def maxima(f, c):
                wait_apart(pool, nm_done, 4 * f + c + 1)
                at = 4 * (4 * f + c)
                p = [mWb[:, c, k, :, 0] for k in range(3)]
                pool.tensor_copy(p[0], nm[:, c, :]).then_inc(mw_done, 1)
                pool.wait_ge(mw_done, at + 1)
                pool.tensor_tensor(p[1], nm[:, c, :], p[0], ALU.subtract).then_inc(mw_done, 1)
                pool.tensor_tensor(nmr[:, c, :], nm[:, c, :], p[0], ALU.subtract).then_inc(mw_done, 1)
                pool.wait_ge(mw_done, at + 3)
                pool.tensor_tensor(p[2], nmr[:, c, :], p[1], ALU.subtract).then_inc(mw_done, 1)

            pool.wait_ge(dconst, N_DCONST)
            for c in range(3):
                maxima(0, c)
            pool.wait_ge(smax_done, 1)
            pool.memset(na[:, :], 0.0).then_inc(rz_done, 1)

            def route_z(r):
                wait_apart(pool, rz_done, 4 * r + 1)
                pool.tensor_scalar(rm[:, 0:1], na[:, :], smax[:, :], None, ALU.min).then_inc(rz_done, 1)
                wait_apart(pool, rz_done, 4 * r + 2)
                pool.tensor_scalar(rz[:, :], rs[:, :], na[:, :], rm[:, 0:1], ALU.min, ALU.subtract).then_inc(rz_done, 1)
                pool.tensor_scalar(rm[:, 1:2], rm[:, 0:1], C_ROUTE, None, ALU.subtract).then_inc(rz_done, 1)

            def route_a(step_, k, r):
                s, at = ring_at(step_, ("R", k))
                pool.wait_ge(free[s], at + 1)
                wait_apart(pool, rz_done, 4 * r + 4)
                pool.tensor_scalar(na[:, :], lns[:, :], EPS_ROUTE, rm[:, 1:2], ALU.mult, ALU.add).then_inc(rz_done, 1)

            route_z(0)

            def causal(i, u, kb):
                wait_apart(pool, exp_done, NE * (2 * i + u) + EXPS_OF[kb])
                diag = strip_at[kb][:, :, 0:P]
                pool.affine_select(out=diag, in_=diag, pattern=[[0, 4], [1, P]], compare_op=ALU.is_ge, fill=0.0,
                                   base=0, channel_multiplier=-1).then_inc(mask_done, 1)

            def sub(i, u, k):
                if k < 2:
                    second(i, u, k)
                elif k == 2:
                    pool.wait_ge(split_done, 5 * (2 * i + u) + 2)
                    rest(i, u)
                else:
                    third(i, u, k - 3)

            def step(ring, where, i, u, late=True, load=True):
                f, r = 2 * i + u + 1, 6 * i + 3 * u
                for item in timeline(ring, late, load):
                    if item[0] == "MAX":
                        maxima(f - 1 if item[1] == 3 else f, item[1])
                    elif item[0] == "CAUSAL":
                        causal(i, u, item[1])
                    elif item[0] == "SUB":
                        sub(i + 1, u, item[1])
                    elif item[0] == "RA":
                        route_a(where, item[1], r + item[1])
                        if not (isinstance(i, int) and r + item[1] == N_ITERS - 1):
                            route_z(r + item[1] + 1)

            step(ring_steady, (0, 0), 0, 0, late=False)
            step(ring_steady, (0, 1), 0, 1)
            with pool.Fori(1, NQ // 2 - 1) as i:
                step(ring_steady, (i, 0), i, 0)
                step(ring_steady, (i, 1), i, 1)
            li = NQ // 2 - 1
            step(ring_steady, (li, 0), li, 0, load=False)
            step(ring_last, NQ - 1, li, 1, load=False)

            def unit(i, u):
                pool.wait_ge(c_x_in[u], 16 * (i + 1))
                pool.tensor_tensor(x_in2[:, u], x_in2[:, u], bias_o[:, 0:1, :].to_broadcast([P, 4, E]), ALU.add).then_inc(c_x, 1)

            pool.wait_ge(wd_in, 16 * 7)
            pool.tensor_tensor(bias_o[:, 0, :], bias_o[:, 0, :], bias_o[:, 1, :], ALU.add).then_inc(fold_done, 1)
            pool.wait_ge(fold_done, N_FOLD)
            with pool.Fori(0, B) as i:
                unit(i, 0)
                unit(i, 1)
            pool.wait_ge(idx_done, 2)
            for st in range(NSLOT):
                pool.indirect_dma_start(out=xg[:, st, :], out_offset=None, in_=xf,
                                        in_offset=bass.IndirectOffsetOnAxis(ap=idx[:, st:st + 1], axis=0)).then_inc(g_in[st], 16)
            for h in range(2):
                pool.wait_ge(gx_done, 9 * h + 8)
                factors(4 * h, 4, ST * h, gp_done, (gx_done, 9 * h + 9))
            pool.wait_ge(out_st[0], 16 * B)
            pool.wait_ge(out_st[1], 16 * B)
            for st in range(NSLOT):
                pool.wait_ge(hv_done, st + 1)
                pool.indirect_dma_start(out=of, out_offset=bass.IndirectOffsetOnAxis(ap=idx[:, st:st + 1], axis=0),
                                        in_=hv[:, st, :], in_offset=None, compute_op=ALU.add).then_inc(add_st[st], 16)
            for st in range(NSLOT):
                pool.wait_ge(add_st[st], 16)


_INS = ['L0_attn_inputs', 'L0_attn_W_qkv', 'L0_attn_b_qkv', 'L0_attn_W_out', 'L0_attn_b_out', 'L0_ffn_routing_token',
        'L0_ffn_gamma_light', 'L0_ffn_w1_light', 'L0_ffn_b1_light', 'L0_ffn_w2_light', 'L0_ffn_b2_light',
        'L0_ffn_gamma_heavy', 'L0_ffn_w1_heavy', 'L0_ffn_b1_heavy', 'L0_ffn_w2_heavy', 'L0_ffn_b2_heavy']
_OUTS = [((4, 1024, 256), 'float32')]


def kernel(**inputs):
    import numpy as _np
    import concourse.bacc as _bacc
    from concourse import mybir as _mybir
    from concourse.bass_utils import run_bass_kernel_spmd as _run

    nc = _bacc.Bacc("TRN2", target_bir_lowering=False, num_devices=1)
    arrays, args = {}, []
    for name in _INS:
        a = _np.ascontiguousarray(inputs[name])
        arrays[f"in_{name}"] = a
        args.append(nc.dram_tensor(f"in_{name}", a.shape, _mybir.dt.from_np(a.dtype), kind="ExternalInput").ap())
    for i, (shape, dtype) in enumerate(_OUTS):
        dt = _mybir.dt.from_np(_np.dtype(dtype))
        args.append(nc.dram_tensor(f"out_{i}", shape, dt, kind="ExternalOutput").ap())
    layer_kernel(nc, *args)
    r = _run(nc, [arrays], core_ids=[0])
    return r.results[0]["out_0"]
```

```python
from contextlib import ExitStack
import math

import concourse.bass as bass
from concourse import mybir

F32 = mybir.dt.float32
BF16 = mybir.dt.bfloat16
I32 = mybir.dt.int32
ALU = mybir.AluOpType
ACT = mybir.ActivationFunctionType
AX = mybir.AxisListType

P = 128
EPS_LN = 1e-5
EPS_ROUTE = 0.1
K_ROUTE = 8.0
N_ITERS = 50
NUM_HEAVY = 256
EXP_FLOOR = -87.33654
MASKED = -3.0e38
VAR_FLOOR = 1e-36


MS = 3
ES = 3
ROUNDS = 17


def ring_orders():
    C = lambda c, a, b: [("C", c, k) for k in range(a, b)]
    T = lambda c: [("T", c, 0), ("T", c, 1)]
    first = (T(0) + T(1) + C(0, 0, 12) + T(2) + C(1, 0, 6) + [("MT", 0)] + C(1, 6, 12) + T(3)
             + C(2, 0, 6) + [("MT", 1)] + C(2, 6, 12) + C(3, 0, 6) + [("MT", 2)] + C(3, 6, 12))
    steady = (T(0) + [("MT", 3)] + T(1) + C(0, 0, 8) + [("OT", 0), ("OT", 1)] + C(0, 8, 10) + [("R", 0)]
              + C(0, 10, 12) + T(2) + C(1, 0, 6) + [("MT", 0)] + C(1, 6, 10) + [("R", 1)] + C(1, 10, 12) + T(3)
              + C(2, 0, 6) + [("MT", 1)] + C(2, 6, 10) + [("R", 2)] + C(2, 10, 12)
              + C(3, 0, 6) + [("MT", 2)] + C(3, 6, 12))

    until = (5, 10, 13)

    def with_search(ring, rounds, at, apart):
        ring = list(ring)
        for k, n in enumerate(rounds):
            ring.insert(at + (apart + 1) * k, ("S", n))
        return ring

    first += [("NOP",)] * (len(first) % 2)
    second = [with_search(steady, range(until[0]), 17, 8), with_search(steady, range(until[0], until[1]), 4, 12)]
    before_last = with_search(steady, range(until[1], until[2]), 4, 20)
    steady += [("NOP",)] * (-len(steady) % MS)
    last = [("MT", 3), ("OT", 0), ("OT", 1)]
    routes, rounds = [("R", k) for k in range(5)], [("S", n) for n in range(until[2], ROUNDS)]
    while routes or rounds:
        last += routes[:1] + rounds[:1]
        routes, rounds = routes[1:], rounds[1:]
    return first, second, steady, before_last, last


CHUNKS = [(qb, k0, min(512, (qb + 1) * P - k0), k0 + 512 >= (qb + 1) * P)
          for qb in range(8) for k0 in range(0, (qb + 1) * P, 512)]
EXPS = ([(kb, (c,), h * 512, 512 - h * kb * P) for kb in range(2) for c in range(4) for h in range(2)]
        + [(2, (0,), 0, 512), (2, (1,), 0, 512), (2, (0, 1), 512, 256)]
        + [(2, (2,), 0, 512), (2, (3,), 0, 512), (2, (2, 3), 512, 256)]
        + [(3, (0,), 0, 512), (3, (1,), 0, 512), (3, (0, 1), 512, 128)]
        + [(3, (2,), 0, 512), (3, (3,), 0, 512), (3, (2, 3), 512, 128)]
        + [(kb, (c,), 0, (8 - kb) * P) for kb in (4, 5) for c in range(4)]
        + [(6, (0, 1), 0, 256), (6, (2, 3), 0, 256), (7, (0, 1, 2, 3), 0, 128)])
EXPS_OF = [sum(1 for task in EXPS if task[0] <= k) for k in range(8)]


SUB_AFTER = (11, 15, 19, 23, 27)
PVS = [(kb, h) for kb in range(8) for h in range(kb // 4, 2)]
PVS_OF = [sum(1 for kb, _ in PVS if kb <= k) for k in range(8)]
NPV = len(PVS)


TAKES = {0: (6, -1), 1: (7, -1), 2: (5, -1), 3: (0, 0), 4: (1, 0), 5: (2, 0), 6: (3, 0), 7: (4, 0)}

LAG = 0.3
PER_ROW, PER_ROW_FLOAT32 = 0.00045, 0.00185
CAST, OUTPUTS, VALUES = 3.2, 1.1, 0.6
EXP, EXP_PER_COLUMN = 0.2, 0.00083
ROUTE = {"ScalarE": 0.5, "Pool": 1.2}
MAXIMA, CAUSAL, SUB = 0.9, 0.7, 2.2
TENSOR_OF = {"T": 0.45, "MT": 0.1, "OT": 0.45, "R": 0.06, "S": 0.06, "NOP": 0.06}
VECTOR_OF = {"T": 0.6, "MT": 0.25, "OT": 0.75, "S": 0.2, "NOP": 0.1}
CHUNK, CHUNK_PER_COLUMN, NEGATED = 0.1, 0.00105, 0.3
LOAD_M = 2.2
PACE, PRODUCT_LATER = 3.0, 0.4


def merge(ring, late, load):
    pe = act = dve = pool = 0.0
    m_free, e_free = [0.0] * MS, [0.0] * ES
    copied, masked, used, parted, loaded = {}, {}, {}, {3: 1.5}, {}
    ring, exps = list(ring), list(range(len(EXPS)))
    products = [(6, 1, -1), (7, 1, -1)] if late else []
    for kb, _, of in products:
        masked[kb, of] = 1.5
    products += [(kb, h, 0) for kb, h in PVS if kb < 6]
    outputs_at = None if late else 0.0
    subs = 5 if load else 0
    if load:
        act = CAST
    total = (len(ring), len(exps), len(products))
    out, filled = [], 0
    while ring or exps or products:
        choice = []
        if products:
            kb, h, of = products[0]
            if (kb, of) in masked and not (kb == 0 and outputs_at is None):
                start = max(masked[kb, of], outputs_at + LAG if (kb, of) == (0, 0) else 0)
                choice.append((start, 2, ("PV",) + products[0], 1 - len(products) / total[2]))
        if exps:
            j = exps[0]
            kb, heads, _, _ = EXPS[j]
            if kb == 2 or not any((a, of) == TAKES[kb] for a, _, of in products):
                start = max(e_free[j % ES], loaded.get(3, 0) if (kb, heads) == (0, (3,)) else 0)
                choice.append((start, 0 if act < dve else 1, ("E", j), 1 - len(exps) / total[1]))
        if ring and not (ring[0][0] == "OT" and outputs_at is None):
            x = ring[0]
            start = m_free[filled % MS]
            if x[0] == "C" and x[2] in (0, 4):
                start = max(start, copied.get((x[1], x[2] // 4), 0))
            if x[0] == "MT":
                start = max(start, parted.get(x[1], 0))
            if x[0] == "OT" and late:
                start = max(start, outputs_at + LAG)
            choice.append((start, 0 if dve <= act else 1, x, 1 - len(ring) / total[0]))
        start, _, x, _ = min(choice, key=lambda c: (
            max(c[0], pe) + PACE * c[3] + (PRODUCT_LATER if c[2][0] == "PV" else 0), c[1]))
        out.append(x)
        pe = max(pe, start)
        if x[0] == "PV":
            products.pop(0)
            kb, h, of = x[1:]
            pe += PER_ROW_FLOAT32 * (512 * (h + 1) - max(kb * P, 512 * h))
            used[kb, of] = pe
            if x == ("PV", 7, 1, -1):
                outputs_at = max(act, pe + LAG) + OUTPUTS
                act = outputs_at + VALUES
        elif x[0] == "E":
            j = exps.pop(0)
            kb, heads, _, n = EXPS[j]
            pe += PER_ROW * len(heads) * n
            act = max(act, pe + LAG, used.get(TAKES[kb], 0) + LAG if kb != 2 else 0) + EXP + EXP_PER_COLUMN * len(heads) * n
            e_free[j % ES] = act + LAG
            if j + 1 in EXPS_OF:
                pool = max(pool, act + LAG) + CAUSAL
                masked[EXPS_OF.index(j + 1), 0] = pool + LAG
            if j + 1 in SUB_AFTER and subs:
                subs -= 1
                pool += SUB
        else:
            ring.pop(0)
            slot = filled % MS
            filled += 1
            width = CHUNKS[x[2]][2] if x[0] == "C" else 0
            pe += TENSOR_OF.get(x[0], PER_ROW * width)
            if x[0] == "R":
                act = max(act, pe + LAG) + ROUTE["ScalarE"]
                m_free[slot] = act + LAG
                pool += ROUTE["Pool"]
            else:
                dve = max(dve, pe + LAG) + VECTOR_OF.get(x[0], CHUNK + CHUNK_PER_COLUMN * width)
                m_free[slot] = dve + LAG
            if x[0] == "T":
                copied[x[1], x[2]] = dve + LAG
            if x[0] == "C" and x[2] == 11:
                dve += NEGATED
                pool = max(pool, dve + LAG) + MAXIMA
                parted[x[1]] = pool + LAG
            if x[0] == "MT":
                loaded[x[1]] = dve + LOAD_M
    return out


def timeline(ring, late, load):
    order = merge(ring, late, load)
    out = ([("CAST",)] if load else []) + [("MAX", 3)]
    exps = 0
    subs = [("SUB", k) for k in range(5)] if load else []
    for item in order:
        if item[0] == "OT" and not late:
            item = ("SKIP", item[1])
        if item[0] == "R":
            at = len(out)
            n = 0
            while n < 2 and at > 1 and out[at - 1][0] != "RA":
                at -= 1
                n += out[at][0] == "E"
            out.insert(at, ("RX", item[1]))
            out += [item, ("RA", item[1])]
            continue
        out.append(item)
        if item == ("C", 0, 5) and not late:
            out.append(("ROUTES",))
        if item == ("PV", 7, 1, -1):
            out += [("OUT",), ("VALUES",)]
        if item == ("E", 1) and not late:
            out += [("VALUES",)]
        if item[0] == "C" and item[2] == 11 and item[1] < 3:
            out.append(("MAX", item[1]))
        if item[0] == "E":
            exps += 1
            if exps in EXPS_OF:
                out.append(("CAUSAL", EXPS_OF.index(exps)))
            if exps in SUB_AFTER and subs:
                out.append(subs.pop(0))
    return out


def wait_apart(engine, semaphore, value):
    engine.wait_ge(semaphore, value)
    if not isinstance(value, int):
        engine.nop(nofuse=True)


def layer_kernel(nc, x, W_qkv, b_qkv, W_out, b_out, rtok, g_l, w1_l, b1_l, w2_l, b2_l, g_h, w1_h, b1_h, w2_h, b2_h, out):
    B, S, E = x.shape
    T = B * S
    NT = T // P
    QKV = W_qkv.shape[1]
    HEADS = 16
    D = QKV // HEADS // 3
    SLOTS = HEADS
    NQ = T // 256
    HID_L, HID_H = w1_l.shape[1], w1_h.shape[1]
    KE = E // P
    NHC = HID_H // P
    SCALE = float((2 * E) ** -0.5)
    C_ROUTE = EPS_ROUTE * math.log(K_ROUTE)
    NSLOT = B * NUM_HEAVY // P
    HW = QKV // 2
    W = 6 * D

    xf = x.rearrange("b s e -> (b s) e")
    of = out.rearrange("b s e -> (b s) e")

    ring_first, ring_second, ring_steady, ring_before, ring_last = ring_orders()
    L0, L = len(ring_second[0]) + len(ring_second[1]), len(ring_steady)

    before = [len(ring_first) // 2] * 2 + [0]

    def ring_at(step, item):
        if isinstance(step, int) and step == -1:
            at = ring_first.index(item)
            return at % 2, at // 2
        if isinstance(step, int):
            at = L0 + L * (NQ - 4) + len(ring_before) + ring_last.index(item)
            return at % MS, before[at % MS] + at // MS
        i, u = step
        if isinstance(i, int) and i == 0:
            at = len(ring_second[0]) * u + ring_second[u].index(item)
            return at % MS, before[at % MS] + at // MS
        if isinstance(i, int) and i == NQ // 2 - 1:
            at = L0 + L * (NQ - 4) + ring_before.index(item)
            return at % MS, before[at % MS] + at // MS
        at = L0 + L * u + ring_steady.index(item)
        return at % MS, 2 * L // MS * (i - 1) + before[at % MS] + at // MS

    NE = len(EXPS)
    ST = 10
    GROUPS = [(0, 2), (2, 2), (4, 10), (14, 18)]
    def search_steps(r):
        return N_SEARCH + 8 * r

    PIECES = 2
    FRONT_FROM = NT // 2
    cuts = [len(ring_first) * k // (NT - FRONT_FROM) for k in range(NT - FRONT_FROM + 1)]
    BESIDE = {FRONT_FROM + k: ring_first[cuts[k]:cuts[k + 1]] for k in range(NT - FRONT_FROM)}

    N_DCONST, N_CONST, N_FOLD = 10, 14, 5
    N_SEARCH = 3

    def final_ot(h):
        at = L0 + L * (NQ - 4) + len(ring_before) + len(ring_last) + h
        return at % MS, before[at % MS] + at // MS

    with ExitStack() as ctx:
        def sb(name, shape, dt=F32):
            return ctx.enter_context(nc.sbuf_tensor(name, shape, dt))

        def sem(name):
            return ctx.enter_context(nc.semaphore(name))

        qkv_d = nc.dram_tensor("qkv_d", [T, QKV], F32).ap()
        sa_d = nc.dram_tensor("sa_d", [T, E], F32).ap()
        s_d = nc.dram_tensor("s_d", [T], F32).ap()
        na_d = nc.dram_tensor("na_d", [P, 2], F32).ap()

        ps = ctx.enter_context(nc.psum_tensor("ps", [P, 8, 512], F32))
        psM = ps[:, 0:MS]
        psE = ps[:, MS:MS + ES]
        psO = ps[:, 6:8]
        psT = ps[:, 2:4]
        psA = [ps[:, 4 + 2 * u:6 + 2 * u] for u in range(2)]
        psC = ps[:, 4:6]
        psS = ps[:, 2]
        psH = ps[:, 2:6]

        ident = sb("ident", [P, P])
        blockones = sb("blockones", [P, P])
        maskrow = sb("maskrow", [P, 512])
        earlier = sb("earlier", [P, P])
        ones = sb("ones", [P, P])
        iota256 = sb("iota256", [P, NUM_HEAVY])
        iota_i = sb("iota_i", [P, NUM_HEAVY], I32)
        tokid_i = sb("tokid_i", [P, 2, NT], I32)
        tokid = sb("tokid", [P, 2, NT], BF16)
        shared = sb("shared", [P, KE * (QKV + 1) + 3 * QKV])
        a0, a1 = KE * (QKV + 1), KE * (QKV + 1) + QKV
        w_qkv = shared[:, 0:a0].rearrange("p (k n) -> p k n", k=KE)
        bias_qkv = shared[:, a0:a1]
        qkvs = shared[:, a1:a1 + 2 * QKV].rearrange("p (b n) -> p b n", b=2)
        w2h = shared[:, 0:NHC * E].rearrange("p (c n) -> p c n", n=E)
        a2 = NHC * E
        wout = shared[:, a2:a2 + KE * E].rearrange("p (k n) -> p k n", n=E)
        w2l = shared[:, a2 + 2 * E:a2 + 3 * E]
        bias_o = shared[:, a2 + 3 * E:a2 + 5 * E].rearrange("p (k n) -> p k n", n=E)
        bias_h = shared[:, a2 + 5 * E:a2 + 6 * E]
        rt_row = shared[:, a2 + 6 * E:a2 + 7 * E]
        xrT = sb("xrT", [P, KE, T])
        xT = sb("xT", [P, 2, KE, P])
        gdot = sb("gdot", [P, NSLOT])
        gu = sb("gu", [P, NSLOT])
        gw = sb("gw", [P, NSLOT])
        gscore = sb("gscore", [P, NSLOT])
        skipped = sb("skipped", [24, 3])
        xr = sb("xr", [P, 2, E])
        bn6 = sb("bn6", [P, NT, 6])
        mv = sb("mv", [P, NT, 2])
        veps = sb("veps", [P, 2, NT])
        halfpow = sb("halfpow", [P, 2, NT])
        roots = sb("roots", [P, 2, NT])
        nrm = sb("nrm", [P, NT])
        rnrm = sb("rnrm", [P, NT])
        xscale = sb("xscale", [P, NT])
        xshift = sb("xshift", [P, NT])
        unscale = sb("unscale", [P, NT])
        s_tok = sb("s_tok", [P, NT])
        strips = sb("strips", [P, 10752])
        QT = sb("QT", [P, 2, 4096])
        parts = sb("parts", [P, 2, 32 * W])
        pm = sb("pm", [P, 2, 32, 3 * D])
        r1 = sb("r1", [P, 32, 2 * D])
        vext = sb("vext", [P, 2, 32, 32])
        osb = sb("osb", [P, 1024])
        rden = sb("rden", [P, 2, 4, 4])
        pmo = sb("pmo", [P, 2, 4, 8, D])
        mx = sb("mx", [P, 4, 8, 2])
        nm = sb("nm", [P, 4, 8])
        nmr = sb("nmr", [P, 4, 8])
        mW = sb("mW", [P, 4, 24])
        mT = sb("mT", [24, 4, P])
        rs = sb("rs", [P, 32])
        smax = sb("smax", [P, 1])
        rz = sb("rz", [P, 32])
        re = sb("re", [P, 32])
        rsum = sb("rsum", [P, 1])
        reach = sb("reach", [P, 3, 32])
        lns = sb("lns", [P, 1])
        rm = sb("rm", [P, 2])
        route = sb("route", [P, 2])
        na = route[:, 0:1]
        signed = sb("signed", [P, 32])
        count = sb("count", [P, 3])
        found = sb("found", [P, 1], I32)
        candidate = sb("candidate", [P, 3], I32)
        bits = sb("bits", [P, ROUNDS, 3], I32)
        step_up = sb("step_up", [P, 3], I32)
        passed = sb("passed", [P, 1])
        sign = sb("sign", [P, 1])
        wanted = sb("wanted", [P, 1])
        na_all = sb("na_all", [P, B, 2])
        nlo_all = sb("nlo_all", [P, B])
        w1l = sb("w1l", [P, KE, HID_L])
        w1h = sb("w1h", [P, KE, HID_H])
        b1l = sb("b1l", [P, 1])
        b1h = sb("b1h", [P, NHC])
        gl = sb("gl", [P, KE])
        gh = sb("gh", [P, KE])
        key = sb("key", [P, NT])
        kth = sb("kth", [P, B])
        above = sb("above", [P, 2, NT])
        total_above = sb("total_above", [P, B])
        room = sb("room", [P, B])
        chosen = sb("chosen", [P, NT])
        slot = sb("slot", [P, NT])
        idxf = sb("idxf", [P, NSLOT])
        idx = sb("idx", [P, NSLOT], I32)

        xs = strips[:, 0:NT * E].rearrange("p (t e) -> p t e", e=E)
        partsb = parts[:, :, :].rearrange("p b w -> p (b w)").bitcast(BF16).rearrange(
            "p (b n g e t) -> p b n g e t", b=2, n=32, g=6, t=2)
        QTb = QT[:, :, :].rearrange("p b w -> p (b w)").bitcast(BF16).rearrange("p (b w t) -> p b w t", b=2, t=2)
        mWb = mW[:, :, :].rearrange("p c w -> p (c w)").bitcast(BF16).rearrange(
            "p (c i n t) -> p c i n t", c=4, i=3, t=2)
        strip_at = {}
        for region, kbs in ((0, (0, 3, 6)), (4096, (1, 4, 7)), (4096 + 3584, (2, 5))):
            for kb in kbs:
                w = (8 - kb) * P
                strip_at[kb] = strips[:, region:region + 4 * w].rearrange("p (c w) -> p c w", c=4)

        sa_in = QT[:, 0, 2048:4096].rearrange("p (b t e) -> p b t e", b=2, e=E)
        x_in2 = pm[:, :, :, :].rearrange("p b n w -> p (b n w)")[:, 0:2048].rearrange("p (b t e) -> p b t e", b=2, e=E)
        saT = strips[:, 8192:8704].rearrange("p (b e) -> p b e", b=2)
        ob = QT[:, 0, 0:2048].rearrange("p (b t e) -> p b t e", b=2, e=E)
        hT = parts[:, 0, 0:1024].rearrange("p (b n) -> p b n", b=2)
        hotb = parts[:, :, :].rearrange("p b w -> p (b w)")[:, 2048:6144].bitcast(BF16).rearrange(
            "p (t n) -> p t n", n=NUM_HEAVY)
        hidT = strips[:, 0:8192].rearrange("p (c n) -> p c n", n=NSLOT * P)
        xg = QT[:, 1, 0:2048].rearrange("p (t e) -> p t e", e=E)
        xgT = QT[:, 1, 2048:4096].rearrange("p (k n) -> p k n", k=KE)
        hv = vext[:, :, :, :].rearrange("p b n w -> p (b n w)").rearrange("p (t e) -> p t e", e=E)
        xgn = strips[:, 8704:10752].rearrange("p (t e) -> p t e", e=E)

        wd_in = sem("wd_in")
        x_in = [sem(f"x_in{g}") for g in range(len(GROUPS))]
        wa_in = sem("wa_in")
        wc_in = sem("wc_in")
        consts = sem("consts")
        dconst = sem("dconst")
        bn_done = sem("bn_done")
        stat_done = sem("stat_done")
        nrm_inv = sem("nrm_inv")
        xr_done = sem("xr_done")
        xT_ps = sem("xT_ps")
        xT_done = sem("xT_done")
        qkv_ps = sem("qkv_ps")
        qkv_done = sem("qkv_done")
        qkv_st = [sem(f"qkv_st{u}") for u in range(2)]
        s_st = sem("s_st")
        rs_in = sem("rs_in")
        route_in = sem("route_in")
        smax_done = sem("smax_done")
        pm_first = [sem(f"pm_first{u}") for u in range(2)]
        pm_in = [sem(f"pm_in{u}") for u in range(2)]
        cast_done = sem("cast_done")
        v_done = sem("v_done")
        split_done = sem("split_done")
        full = [sem(f"full{s}") for s in range(MS)]
        free = [sem(f"free{s}") for s in range(MS)]
        nm_done = sem("nm_done")
        mw_done = sem("mw_done")
        m_in = [sem(f"m_in{c}") for c in range(4)]
        qk_ps = sem("qk_ps")
        exp_done = sem("exp_done")
        mask_done = sem("mask_done")
        pv_done = sem("pv_done")
        osb_done = sem("osb_done")
        rden_done = sem("rden_done")
        sa_st = [sem(f"sa_st{u}") for u in range(2)]
        rz_done = sem("rz_done")
        re_done = sem("re_done")
        fold_done = sem("fold_done")
        na_st = sem("na_st")
        na_in = sem("na_in")
        c_in = [sem(f"c_in{u}") for u in range(2)]
        c_x = sem("c_x")
        h_ps = sem("h_ps")
        h_done = sem("h_done")
        saT_ps = sem("saT_ps")
        saT_done = sem("saT_done")
        o_ps = sem("o_ps")
        ob_done = sem("ob_done")
        out_st = [sem(f"out_st{u}") for u in range(2)]
        th = sem("th")
        sl = sem("sl")
        ties_ps = sem("ties_ps")
        slot_ps = sem("slot_ps")
        hot_done = sem("hot_done")
        idx_ps = sem("idx_ps")
        idx_done = sem("idx_done")
        g_in = [sem(f"g_in{t}") for t in range(NSLOT)]
        gx_done = sem("gx_done")
        gp_done = sem("gp_done")
        gs_done = sem("gs_done")
        gT_ps = sem("gT_ps")
        gT_done = sem("gT_done")
        hh_ps = sem("hh_ps")
        hh_done = sem("hh_done")
        ho_ps = sem("ho_ps")
        hv_half = sem("hv_half")
        hv_done = sem("hv_done")
        add_st = [sem(f"add_st{t}") for t in range(NSLOT)]
        group_of = sem("group_of")
        xc_st = [sem(f"xc_st{u}") for u in range(2)]
        c_x_in = [sem(f"c_x_in{u}") for u in range(2)]
        gn_done = sem("gn_done")
        gu_done = sem("gu_done")

        def transposed(t, u):
            if isinstance(t, int) and t >= FRONT_FROM:
                return xrT[:, :, t * P:(t + 1) * P]
            return xT[:, u]

        pm_rows = qkv_d.rearrange("(q n t) (j f) -> q (t j) n f", n=32, t=8, j=SLOTS)

        block = ctx.enter_context(nc.Block())

        @block.sync
        def _(sp):
            xt = xf.rearrange("(t p) e -> p t e", p=P)
            for g, (a, n) in enumerate(GROUPS):
                sp.dma_start(xs[:, a:a + n, :], xt[:, a:a + n, :]).then_inc(x_in[g], 16)
                if g == 0:
                    sp.dma_start(w_qkv[:, :, 0:QKV], W_qkv.rearrange("(k p) n -> p k n", p=P)).then_inc(wa_in, 16)
                    sp.dma_start(w_qkv[:, :, QKV:QKV + 1], rtok.rearrange("(k p o) -> p k o", p=P, o=1), allow_slow_non_contiguous=True).then_inc(wa_in, 16)
                    sp.dma_start(bias_qkv, b_qkv.partition_broadcast(P)).then_inc(wa_in, 16)
            for dst, src in ((w1l[:, :, :], w1_l.rearrange("(k p) n -> p k n", p=P)),
                             (w1h[:, :, :], w1_h.rearrange("(k p) n -> p k n", p=P)),
                             (b1l[:, :], b1_l.rearrange("(p o) -> p o", o=1)),
                             (b1h[:, :], b1_h.rearrange("(k p) -> p k", p=P)),
                             (gl[:, :], g_l.rearrange("(k p) -> p k", p=P)),
                             (gh[:, :], g_h.rearrange("(k p) -> p k", p=P))):
                sp.dma_start(dst, src, allow_slow_non_contiguous=True).then_inc(wc_in, 16)

            def store_qkv(i, u):
                if not (isinstance(i, int) and 2 * i + u >= FRONT_FROM):
                    wait_apart(sp, xT_done, 2 * i + u + 1)
                    sp.dma_start(xrT[:, :, bass.ds((2 * i + u) * P, P)], xT[:, u]).then_inc(xc_st[u], 16)
                wait_apart(sp, qkv_done, 2 * i + u + 1)
                sp.dma_start(qkv_d.rearrange("(t p) n -> p t n", p=P)[:, bass.ds(2 * i + u, 1), :],
                             qkvs[:, u:u + 1, :]).then_inc(qkv_st[u], 16)

            def load_pm(i, u):
                wait_apart(sp, qkv_st[0], 32 * i + 16 * u + 16)
                wait_apart(sp, qkv_st[1], 32 * i + 16 * u + 16)
                sp.dma_start(pm[:, u, :, :], pm_rows[bass.ds(2 * i + u, 1)].rearrange("a p n f -> (a p) n f")
                             ).then_inc(pm_in[u], 16)

            with sp.Fori(0, FRONT_FROM // 2) as i:
                for u in range(2):
                    store_qkv(i, u)

            def load_m(i, u, c):
                first = isinstance(i, int) and i == -1
                s, at = ring_at(-1 if first else (i, u), ("MT", c))
                wait_apart(sp, free[s], at + 1)
                fu = 0 if first else (u if c == 3 else 1 - u)
                sp.dma_start(QT[W:W + 3, fu, c * 1024:(c + 1) * 1024].rearrange("i (n p) -> i n p", p=P),
                             mT[:, c, :]).then_inc(m_in[c], 16)

            for t in range(FRONT_FROM, NT):
                store_qkv(t // 2, t % 2)
                if t == NT - 10:
                    wait_apart(sp, v_done, 1)
                    wait_apart(sp, split_done, 5)
                    load_pm(1, 0)
                if t in (NT - 6, NT - 4, NT - 2):
                    load_m(-1, 0, (t - NT + 6) // 2)
            wait_apart(sp, qkv_done, NT)
            sp.dma_start(s_d.rearrange("(t p o) -> p t o", p=P, o=1), s_tok[:, :].unsqueeze(2), allow_slow_non_contiguous=True).then_inc(s_st, 16)

            def store_sa(i, u, where):
                for h in range(2):
                    s, at = where(h)
                    wait_apart(sp, free[s], at + 1)
                dst = sa_d.rearrange("(q n t) (j f) -> q (t j) n f", n=32, t=8, j=SLOTS)
                sp.dma_start(dst[bass.ds(2 * i + u, 1)].rearrange("a p n f -> (a p) n f"),
                             pmo[:, u].rearrange("p c n f -> p (c n) f")).then_inc(sa_st[u], 16)


            def step(i, u, late=True, load=True):
                if late:
                    load_m(i, u, 3)
                    store_sa(i if u else i - 1, 1 - u, lambda h: ring_at((i, u), ("OT", h)))
                if load:
                    wait_apart(sp, v_done, 2 * i + u + 2)
                    wait_apart(sp, split_done, 5 * (2 * i + u + 2))
                    load_pm(i + 1 if u == 0 else i + 2, 1 - u)
                for c in range(3):
                    load_m(i, u, c)

            for u in range(2):
                sp.sem_inc(sa_st[u], 16)
            load_m(0, 0, 3)
            wait_apart(sp, s_st, 16)
            sp.dma_start(rs[:, :], s_d.rearrange("(p n) -> p n", n=32)).then_inc(rs_in, 16)
            for b in range(B):
                sp.dma_start(osb[32 * b:32 * b + 32, :],
                             s_d[b * S:(b + 1) * S].partition_broadcast(32)).then_inc(route_in, 16)
            step(0, 0, late=False)

            wait_apart(sp, qkv_st[0], 16 * (NT // 2))
            wait_apart(sp, qkv_st[1], 16 * (NT // 2))
            for dst, src in ((w2l, w2_l), (wout, W_out.rearrange("(k p) n -> p k n", p=P)),
                             (w2h, w2_h.rearrange("(k p) n -> p k n", p=P)),
                             (bias_o[:, 0, :], b_out.partition_broadcast(P)), (bias_o[:, 1, :], b2_l.partition_broadcast(P)),
                             (bias_h, b2_h.partition_broadcast(P)), (rt_row, rtok.partition_broadcast(P))):
                sp.dma_start(dst, src).then_inc(wd_in, 16)

            step(0, 1)
            with sp.Fori(1, NQ // 2 - 2) as i:
                step(i, 0)
                step(i, 1)
            step(NQ // 2 - 2, 0)
            step(NQ // 2 - 2, 1, load=False)
            step(NQ // 2 - 1, 0, load=False)
            s, at = ring_at(NQ - 1, ("MT", 3))
            wait_apart(sp, free[s], at + 1)
            sp.dma_start(QT[W:W + 3, 1, 3 * 1024:4096].rearrange("i (n p) -> i n p", p=P), mT[:, 3, :]).then_inc(m_in[3], 16)
            store_sa(NQ // 2 - 1, 0, lambda h: ring_at(NQ - 1, ("OT", h)))
            xb3 = xf.rearrange("(b t p) e -> b p t e", t=4, p=P)
            sb3 = sa_d.rearrange("(b t p) e -> b p t e", t=4, p=P)
            ob3 = of.rearrange("(b t p) e -> b p t e", t=4, p=P)

            def load_c(i, u):
                sp.dma_start(sa_in[:, u], sb3[bass.ds(2 * i + u, 1)].rearrange("a p t e -> (a p) t e")).then_inc(c_in[u], 16)
                sp.dma_start(x_in2[:, u], xb3[bass.ds(2 * i + u, 1)].rearrange("a p t e -> (a p) t e")).then_inc(c_x_in[u], 16)

            wait_apart(sp, pv_done, NPV * (NQ - 1))
            wait_apart(sp, v_done, NQ)
            wait_apart(sp, split_done, 5 * NQ)
            for u in range(2):
                wait_apart(sp, sa_st[u], 16 * 3)
                load_c(0, u)
            wait_apart(sp, rz_done, N_ITERS * 4 + 1)
            wait_apart(sp, th, search_steps(ROUNDS) - 4 + 1)
            sp.dma_start(na_d, route[:, :]).then_inc(na_st, 16)
            wait_apart(sp, na_st, 16)
            sp.dma_start(na_all[:, :, :], na_d.rearrange("(b g) w -> g b w", g=32)[0].partition_broadcast(P),
                         allow_slow_non_contiguous=True).then_inc(na_in, 16)
            store_sa(NQ // 2 - 1, 1, final_ot)
            for u in range(2):
                wait_apart(sp, sa_st[u], 16 * (NQ // 2 + 1))

            def unit(i, u, more=True):
                wait_apart(sp, ob_done, 8 * i + 4 * u + 4)
                sp.dma_start(ob3[bass.ds(2 * i + u, 1)].rearrange("a p t e -> (a p) t e"), ob[:, u]).then_inc(out_st[u], 16)
                if more:
                    wait_apart(sp, saT_ps, 8 * i + 4 * u + 4)
                    load_c(i + 1, u)

            with sp.Fori(0, B - 1) as i:
                unit(i, 0)
                unit(i, 1)
            unit(B - 1, 0, more=False)
            unit(B - 1, 1, more=False)
            wait_apart(sp, out_st[0], 16 * B)
            wait_apart(sp, out_st[1], 16 * B)

        @block.scalar
        def _(act):
            def normalise(t, u):
                return nc.scalar.activation(xr[:, u, :], xs[:, bass.ds(t, 1), :].rearrange("p a e -> p (a e)"),
                                            ACT.Identity, bias=xshift[:, bass.ds(t, 1)], scale=xscale[:, bass.ds(t, 1)])

            def tile_a(i, u, more=True):
                t = 2 * i + u
                if more:
                    act.wait_ge(group_of, t + 2)
                    if not (isinstance(i, int) and t == 0):
                        act.wait_ge(xT_ps, t)
                    normalise(t + 1, 1 - u).then_inc(xr_done, 1)
                act.wait_ge(xT_ps, t + 1)
                if not (isinstance(i, int) and (i == 0 or t >= FRONT_FROM)):
                    act.wait_ge(qkv_ps, t - 1)
                    act.wait_ge(xc_st[u], 16 * i)
                nc.scalar.activation(transposed(t, u), psT[:, u, 0:KE * P].rearrange("p (k n) -> p k n", k=KE), ACT.Copy
                                     ).then_inc(xT_done, 1)

            def pm_loaded(i, u):
                if isinstance(i, int) and i == 0:
                    act.wait_ge(pm_first[u], 16 * PIECES)
                else:
                    act.wait_ge(pm_in[u], 16 * i)

            def cast(i, u):
                pm_loaded(i, u)
                for t, g0 in ((0, 0), (1, 2)):
                    src = pm[:, u, :, t * D:(t + 1) * D].unsqueeze(2).to_broadcast([P, 32, 3, D])
                    nc.scalar.activation(partsb[:, u, :, g0:g0 + 3, :, t], src, ACT.Copy).then_inc(cast_done, 1)

            def values(i, u):
                pm_loaded(i, u)
                nc.scalar.activation(vext[:, u, :, 0:D], pm[:, u, :, 2 * D:3 * D], ACT.Copy).then_inc(v_done, 1)

            act.wait_ge(group_of, 1)
            normalise(0, 0).then_inc(xr_done, 1)
            tile_a(0, 0)
            tile_a(0, 1)
            with act.Fori(1, NT // 8) as i:
                tile_a(i, 0)
                tile_a(i, 1)
            def load_first_pm(u, k):
                act.wait_ge(qkv_st[0], 16 * (u + 1))
                act.wait_ge(qkv_st[1], 16 * (u + 1))
                n = slice(k * 32 // PIECES, (k + 1) * 32 // PIECES)
                act.dma_start(pm[:, u, n, :], pm_rows[u:u + 1, :, n, :].rearrange("a p n f -> (a p) n f")
                              ).then_inc(pm_first[u], 16)

            for k in range(PIECES):
                load_first_pm(0, k)
                tile_a(NT // 8 + k // 2, k % 2)
            for t in range(NT // 4 + PIECES, FRONT_FROM - 6):
                tile_a(t // 2, t % 2)
            act.wait_ge(dconst, N_DCONST)
            cast(0, 0)
            for t in range(FRONT_FROM - 6, NT):
                tile_a(t // 2, t % 2, more=t < NT - 1)
                if FRONT_FROM + 1 <= t <= FRONT_FROM + PIECES:
                    load_first_pm(1, t - FRONT_FROM - 1)
                if t == FRONT_FROM + 6:
                    values(0, 0)
                    cast(0, 1)

            def exps(i, u, j):
                q = 2 * i + u
                kb, heads, a, n = EXPS[j]
                act.wait_ge(qk_ps, NE * q + j + 1)
                if j == 0 or EXPS[j - 1][0] != kb:
                    if kb >= 3:
                        act.wait_ge(pv_done, NPV * q + PVS_OF[kb - 3])
                    elif not (isinstance(i, int) and q == 0):
                        act.wait_ge(pv_done, NPV * (q - 1) + PVS_OF[(6, 7, 5)[kb]])
                src = psE[:, (NE * u + j) % ES, 0:len(heads) * n].rearrange("p (c n) -> p c n", n=n)
                dst = strip_at[kb][:, heads[0]:heads[-1] + 1, a:a + n]
                nc.scalar.activation(dst, src, ACT.Exp, scale=SCALE).then_inc(exp_done, 1)

            def outputs(i, u):
                q = 2 * i + u
                act.wait_ge(pv_done, NPV * (q + 1))
                if not (isinstance(i, int) and q == 0):
                    s, at = ring_at((i, u), ("OT", 1))
                    act.wait_ge(full[s], at + 1)
                nc.scalar.activation(osb[:, :], psO[:, :, :].rearrange("p h n -> p (h n)"), ACT.Copy).then_inc(osb_done, 1)

            def route_exp(r):
                act.wait_ge(rz_done, 4 * r + 3)
                nc.scalar.activation(re[:, :], rz[:, :], ACT.Exp, scale=1.0 / EPS_ROUTE, accum_out=rsum[:, :]).then_inc(re_done, 1)

            def route_ln(step, k):
                s, at = ring_at(step, ("R", k))
                act.wait_ge(full[s], at + 1)
                nc.scalar.activation(lns[:, :], psM[:, s, 0:1], ACT.Ln).then_inc(free[s], 1)

            def step(ring, where, i, u, late=True, load=True, value=True):
                r = 6 * i + 3 * u
                for item in timeline(ring, late, load):
                    if item[0] == "E":
                        exps(i, u, item[1])
                    elif item[0] == "OUT":
                        outputs(i if u else i - 1, 1 - u)
                    elif item[0] == "VALUES" and value:
                        values(i if u == 0 else i + 1, 1 - u)
                    elif item[0] == "CAST":
                        cast(i + 1, u)
                    elif item[0] == "RX":
                        route_exp(r + item[1])
                    elif item[0] == "R":
                        route_ln(where, item[1])

            nc.scalar.preload_act_table_set("natural_log_exp_and_others")
            step(ring_second[0], (0, 0), 0, 0, late=False)
            step(ring_second[1], (0, 1), 0, 1)
            with act.Fori(1, NQ // 2 - 1) as i:
                step(ring_steady, (i, 0), i, 0)
                step(ring_steady, (i, 1), i, 1)
            li = NQ // 2 - 1
            step(ring_before, (li, 0), li, 0, load=False)
            step(ring_last, NQ - 1, li, 1, load=False, value=False)
            act.wait_ge(pv_done, NPV * NQ)
            s, at = ring_at(NQ - 1, ("OT", 1))
            act.wait_ge(full[s], at + 1)
            nc.scalar.activation(osb[:, :], psO[:, :, :].rearrange("p h n -> p (h n)"), ACT.Copy).then_inc(osb_done, 1)

            def hidden(i, u):
                act.wait_ge(h_ps, 2 * i + u + 1)
                if not (isinstance(i, int) and i == 0):
                    act.wait_ge(o_ps, 8 * (i - 1) + 4 * u + 4)
                nc.scalar.activation(hT[:, u, :], psO[:, u, :], ACT.Gelu, bias=b1l[:, 0:1]).then_inc(h_done, 1)

            def unit(i, u, more=True):
                for t in range(4):
                    n = 8 * i + 4 * u + t
                    act.wait_ge(saT_ps, n + 1)
                    if not (isinstance(i, int) and n < 2):
                        act.wait_ge(o_ps, n - 1)
                    nc.scalar.activation(saT[:, t % 2, :], psM[:, t % 2, 0:KE * P], ACT.Copy).then_inc(saT_done, 1)
                    if t == 1 and more:
                        hidden(i if u == 0 else i + 1, 1 - u)

            hidden(0, 0)
            unit(0, 0)
            unit(0, 1)
            with act.Fori(1, B - 1) as i:
                unit(i, 0)
                unit(i, 1)
            unit(B - 1, 0)
            unit(B - 1, 1, more=False)

            for h in range(2):
                for t in range(4):
                    st = 4 * h + t
                    act.wait_ge(gT_ps, st + 1)
                    nc.scalar.activation(xgT[:, :, st * P:(st + 1) * P], psM[:, st % 2, 0:KE * P].rearrange(
                        "p (k n) -> p k n", k=KE), ACT.Copy).then_inc(gT_done, 1)
                for c in range(NHC):
                    m = NHC * h + c
                    act.wait_ge(hh_ps, m + 1)
                    nc.scalar.activation(hidT[:, c, h * 512:(h + 1) * 512], psO[:, m % 2, :], ACT.Gelu,
                                         bias=b1h[:, c:c + 1]).then_inc(hh_done, 1)
                if h == 0:
                    act.wait_ge(gu_done, 2 * NSLOT + 1)
                    nc.scalar.activation(gscore[:, :], gu[:, :], ACT.Exp, scale=1.0 / EPS_ROUTE).then_inc(gs_done, 1)

        @block.tensor
        def _(pe):
            pe.wait_ge(consts, 2)

            def transposes_a(i, u):
                t = 2 * i + u
                pe.wait_ge(xr_done, t + 1)
                if not (isinstance(i, int) and i == 0):
                    pe.wait_ge(xT_done, t - 1)
                for k in range(KE):
                    mm = pe.transpose(psT[:, u, k * P:(k + 1) * P], xr[:, u, k * P:(k + 1) * P], ident[:, :])
                mm.then_inc(xT_ps, 1)

            def project(i, u, h):
                t = 2 * i + u
                if h == 0:
                    pe.wait_ge(xT_done, t + 1)
                    if isinstance(i, int) and t == 0:
                        pe.wait_ge(wa_in, 48)
                    if not (isinstance(i, int) and i == 0):
                        pe.wait_ge(qkv_done, t - 1)
                n = HW + h
                for k in range(KE):
                    mm = pe.matmul(psA[u][:, h, 0:n], transposed(t, u)[:, k, :], w_qkv[:, k, HW * h:HW * h + n],
                                   start=(k == 0), stop=(k == KE - 1))
                if h == 1:
                    mm.then_inc(qkv_ps, 1)

            def tile_a(i, u):
                transposes_a(i if u == 0 else i + 1, 1 - u)
                project(i, u, 0)
                project(i, u, 1)

            transposes_a(0, 0)
            tile_a(0, 0)
            tile_a(0, 1)
            with pe.Fori(1, FRONT_FROM // 2) as i:
                tile_a(i, 0)
                tile_a(i, 1)

            def ring_item(step, fi, fu, f, item, r=None):
                s, at = ring_at(step, ("OT", item[1]) if item[0] == "SKIP" else item)
                if not (isinstance(at, int) and at == 0):
                    pe.wait_ge(free[s], at)
                kind = item[0]
                if kind == "T":
                    _, c, h = item
                    if c == 0 and h == 0:
                        pe.wait_ge(split_done, 5 * f + 5)
                    for b in range(4):
                        n = 8 * c + 4 * h + b
                        mm = pe.transpose(psM[0:W, s, b * P:(b + 1) * P], parts[:, fu, n * W:(n + 1) * W], ident[:, :])
                elif kind == "C":
                    _, c, k = item
                    qb, k0, n, _d = CHUNKS[k]
                    if k in (0, 4):
                        ts, tat = ring_at(step, ("T", c, 0 if k == 0 else 1))
                        pe.wait_ge(free[ts], tat + 1)
                    mm = pe.matmul(psM[:, s, 0:n], QTb[0:W, fu, c * 1024 + qb * P:c * 1024 + (qb + 1) * P, 0],
                                   QTb[0:W, fu, c * 1024 + k0:c * 1024 + k0 + n, 1], start=True, stop=True)
                elif kind == "MT":
                    c = item[1]
                    pe.wait_ge(mw_done, 4 * (4 * (f - 1 if c == 3 else f) + c + 1))
                    mm = pe.transpose(psM[0:24, s, 0:P], mW[:, c, :], ident[:, :])
                elif kind == "OT":
                    h = item[1]
                    pe.wait_ge(osb_done, f - 1)
                    for b in range(4):
                        mm = pe.transpose(psM[:, s, b * P:(b + 1) * P], osb[:, (4 * h + b) * P:(4 * h + b + 1) * P], ident[:, :])
                elif kind == "R":
                    pe.wait_ge(re_done, r + 1)
                    mm = pe.matmul(psM[:, s, 0:1], blockones[:, :], rsum[:, :], start=True, stop=True)
                elif kind == "S":
                    pe.wait_ge(th, search_steps(item[1]))
                    mm = pe.matmul(psM[:, s, 0:96], blockones[:, :], reach[:, :, :].rearrange("p c n -> p (c n)"),
                                   start=True, stop=True)
                else:
                    mm = pe.transpose(psM[0:24, s, 0:P], ident[:, 0:24], ident[:, :])
                mm.then_inc(full[s], 1)

            def scores(i, u, j):
                q = 2 * i + u
                kb, heads, a, n = EXPS[j]
                if not (isinstance(i, int) and q == 0 and j < ES):
                    pe.wait_ge(exp_done, NE * q + j + 1 - ES)
                if kb == 0 and a == 0:
                    pe.wait_ge(m_in[heads[0]], 16 * (q + 1))
                for k, c in enumerate(heads):
                    q0 = c * 1024 + kb * P + a
                    mm = pe.matmul(psE[:, (NE * u + j) % ES, k * n:(k + 1) * n],
                                   QTb[0:W + 3, u, c * 1024 + kb * P:c * 1024 + (kb + 1) * P, 1],
                                   QTb[0:W + 3, u, q0:q0 + n, 0], start=True, stop=True)
                mm.then_inc(qk_ps, 1)

            def product(i, u, kb, h):
                q = 2 * i + u
                w = (8 - kb) * P
                pe.wait_ge(mask_done, 8 * q + kb + 1)
                if kb == 0 and h == 0:
                    pe.wait_ge(v_done, q + 1)
                    if not (isinstance(i, int) and q == 0):
                        pe.wait_ge(osb_done, q)
                q0 = max(kb * P, 512 * h)
                n = 512 * (h + 1) - q0
                for c in range(4):
                    mm = pe.matmul(psO[32 * c:32 * c + 32, h, q0 - 512 * h:512], vext[:, u, 8 * c + kb, :],
                                   strip_at[kb][:, c, q0 - kb * P:q0 - kb * P + n],
                                   start=(kb == 0), stop=(kb == 4 * h + 3), skip_group_check=True)
                mm.then_inc(pv_done, 1)

            pe.wait_ge(dconst, N_DCONST)
            for t in range(FRONT_FROM, NT):
                if t < NT - 1:
                    transposes_a((t + 1) // 2, (t + 1) % 2)
                items = BESIDE[t]
                for h in range(2):
                    ring_item(-1, 0, 0, 0, items[h])
                    project(t // 2, t % 2, h)
                for item in items[2:]:
                    ring_item(-1, 0, 0, 0, item)
            pe.wait_ge(qkv_done, NT)

            def step(ring, where, i, u, late=True, load=True):
                for item in timeline(ring, late, load):
                    if item[0] == "E":
                        scores(i, u, item[1])
                    elif item[0] == "PV" and item[3] == 0:
                        product(i, u, item[1], item[2])
                    elif item[0] == "PV":
                        product(i if u else i - 1, 1 - u, item[1], item[2])
                    elif item[0] in ("T", "C", "MT", "OT", "R", "S", "SKIP", "NOP"):
                        ring_item(where, i if u == 0 else i + 1, 1 - u, 2 * i + u + 1, item,
                                  6 * i + 3 * u + item[1] if item[0] == "R" else None)

            step(ring_second[0], (0, 0), 0, 0, late=False)
            step(ring_second[1], (0, 1), 0, 1)
            with pe.Fori(1, NQ // 2 - 1) as i:
                step(ring_steady, (i, 0), i, 0)
                step(ring_steady, (i, 1), i, 1)
            li = NQ // 2 - 1
            step(ring_before, (li, 0), li, 0, load=False)
            step(ring_last, NQ - 1, li, 1, load=False)
            product(li, 1, 6, 1)
            product(li, 1, 7, 1)

            def light_hidden(i, u):
                if isinstance(i, int) and i == 0:
                    pe.wait_ge(osb_done, NQ)
                    pe.wait_ge(fold_done, N_FOLD - 1)
                    pe.wait_ge(wd_in, 16 * 7)
                    pe.wait_ge(xc_st[0], 16 * (FRONT_FROM // 2))
                    pe.wait_ge(xc_st[1], 16 * (FRONT_FROM // 2))
                else:
                    pe.wait_ge(h_done, 2 * (i - 1) + u + 1)
                for k in range(KE):
                    mm = pe.matmul(psO[:, u, :], w1l[:, k, :], xrT[:, k, bass.ds(1024 * i + 512 * u, 512)],
                                   start=(k == 0), stop=(k == KE - 1))
                mm.then_inc(h_ps, 1)

            light_hidden(0, 0)
            for h in range(2):
                s, at = final_ot(h)
                pe.wait_ge(free[s], at)
                for b in range(4):
                    mm = pe.transpose(psM[:, s, b * P:(b + 1) * P], osb[:, (4 * h + b) * P:(4 * h + b + 1) * P], ident[:, :])
                mm.then_inc(full[s], 1)
            light_hidden(0, 1)

            def transposes_c(i, u, t):
                n = 8 * i + 4 * u + t
                if t == 0:
                    pe.wait_ge(c_in[u], 16 * (i + 1))
                if not (isinstance(i, int) and n < 2):
                    pe.wait_ge(saT_done, n - 1)
                elif n == 0:
                    for h in range(2):
                        s, at = final_ot(h)
                        pe.wait_ge(free[s], at + 1)
                for k in range(KE):
                    mm = pe.transpose(psM[:, t % 2, k * P:(k + 1) * P], sa_in[:, u, t, k * P:(k + 1) * P], ident[:, :])
                mm.then_inc(saT_ps, 1)

            def project_c(i, u, t):
                n = 8 * i + 4 * u + t
                o = psC[:, t % 2, 0:E]
                if t == 0:
                    pe.wait_ge(h_done, 2 * i + u + 1)
                if not (isinstance(i, int) and n < 2):
                    pe.wait_ge(ob_done, n - 1)
                pe.matmul(o, hT[:, u, t * P:(t + 1) * P], w2l, start=True, stop=False)
                pe.wait_ge(saT_done, n + 1)
                for k in range(KE):
                    mm = pe.matmul(o, saT[:, t % 2, k * P:(k + 1) * P], wout[:, k, :], start=False, stop=(k == KE - 1))
                mm.then_inc(o_ps, 1)

            def unit(i, u, more=True):
                for t in range(4):
                    if t < 3:
                        transposes_c(i, u, t + 1)
                    elif more:
                        transposes_c(i if u == 0 else i + 1, 1 - u, 0)
                    project_c(i, u, t)
                    if t == 0 and more and not (isinstance(i, int) and i == 0 and u == 0):
                        light_hidden(i if u == 0 else i + 1, 1 - u)

            def prefix(out_, flags):
                pe.matmul(out_, earlier[:, :], flags, start=True, stop=False)
                o, f = (y.rearrange("p (b k) -> p b k", k=8) for y in (out_, flags))
                for d in range(1, 8):
                    mm = pe.matmul(o[:, :, d:8], ones[:, :], f[:, :, 0:8 - d], start=False, stop=(d == 7))
                return mm

            def number_slots():
                pe.wait_ge(hot_done, NT)
                for st in range(NSLOT):
                    b, hh = st // 2, st % 2
                    for k in range(8):
                        mm = pe.matmul(psS[:, 384 + 2 * st:386 + 2 * st], hotb[:, 8 * b + k, hh * P:(hh + 1) * P],
                                       tokid[:, :, 8 * b + k], start=(k == 0), stop=(k == 7))
                mm.then_inc(idx_ps, 1)

            transposes_c(0, 0, 0)
            unit(0, 0)
            pe.wait_ge(sl, 7)
            pe.wait_ge(consts, N_CONST)
            pe.matmul(psS[:, 256:256 + 2 * NT], ones[:, :], above[:, :, :].rearrange("p w n -> p (w n)"),
                      start=True, stop=True)
            prefix(psS[:, 320:320 + NT], above[:, 1, :]).then_inc(ties_ps, 1)
            unit(0, 1)
            pe.wait_ge(sl, 12)
            prefix(psS[:, 352:352 + NT], chosen[:, :]).then_inc(slot_ps, 1)
            with pe.Fori(1, B - 1) as i:
                unit(i, 0)
                unit(i, 1)
            number_slots()
            unit(B - 1, 0)
            unit(B - 1, 1, more=False)

            for h in range(2):
                for t in range(4):
                    st = 4 * h + t
                    pe.wait_ge(gn_done, st + 1)
                    if st >= 2:
                        pe.wait_ge(gT_done, st - 1)
                    elif st == 0:
                        pe.wait_ge(saT_done, NT)
                    for k in range(KE):
                        mm = pe.transpose(psM[:, st % 2, k * P:(k + 1) * P], xgn[:, st, k * P:(k + 1) * P], ident[:, :])
                    mm.then_inc(gT_ps, 1)
                pe.wait_ge(gT_done, 4 * h + 4)
                for c in range(NHC):
                    m = NHC * h + c
                    if m >= 2:
                        pe.wait_ge(hh_done, m - 1)
                    for k in range(KE):
                        mm = pe.matmul(psO[:, m % 2, :], w1h[:, k, c * P:(c + 1) * P], xgT[:, k, h * 512:(h + 1) * 512],
                                       start=(k == 0), stop=(k == KE - 1))
                    mm.then_inc(hh_ps, 1)
                for t in range(4):
                    st = 4 * h + t
                    o = psH[:, t, 0:E]
                    if st >= 4:
                        pe.wait_ge(hv_half, st - 3)
                    else:
                        pe.wait_ge(ob_done, NT)
                    for c in range(NHC):
                        pe.wait_ge(hh_done, NHC * h + c + 1)
                        mm = pe.matmul(o, hidT[:, c, st * P:(st + 1) * P], w2h[:, c, :], start=(c == 0), stop=(c == NHC - 1))
                    mm.then_inc(ho_ps, 1)

        @block.vector
        def _(dve):
            def const(ins):
                ins.then_inc(dconst, 1)

            const(dve.memset(vext[:, :, :, :], 0.0))
            const(dve.memset(blockones[:, :], 0.0))
            const(dve.memset(mWb[:, :, :, :, 1], 1.0))
            const(dve.memset(mx[:, :, :, :], MASKED))
            dve.wait_ge(dconst, 2)
            const(dve.memset(vext[:, :, :, D:D + 1], 1.0))
            for b in range(4):
                const(dve.memset(blockones[32 * b:32 * b + 32, 32 * b:32 * b + 32], 1.0))
            const(dve.memset(mWb[:, :, :, :, 0], 0.0))

            def stats(g, n):
                if n == GROUPS[g][0]:
                    dve.wait_ge(x_in[g], 16)
                nc.vector.bn_stats(bn6[:, n, :], xs[:, n, :]).then_inc(bn_done, 1)
                dve.wait_ge(bn_done, 2 * n + 1)
                nc.vector.bn_aggr(mv[:, n, :], bn6[:, n, :]).then_inc(bn_done, 1)

            def invert(g):
                dve.wait_ge(stat_done, ST * g + 5)
                c = slice(GROUPS[g][0], sum(GROUPS[g]))
                nc.vector.reciprocal(rnrm[:, c], nrm[:, c]).then_inc(nrm_inv, 1)

            def evacuate(i, u):
                t = 2 * i + u
                dve.wait_ge(qkv_ps, t + 1)
                if not (isinstance(i, int) and i == 0):
                    dve.wait_ge(qkv_st[u], 16 * i)
                nc.vector.tensor_scalar(s_tok[:, bass.ds(t, 1)], psA[u][:, 1, HW:HW + 1], unscale[:, bass.ds(t, 1)], None,
                                        ALU.mult)
                nc.vector.scalar_tensor_tensor(out=qkvs[:, u, :].rearrange("p (h n) -> p h n", h=2), in0=psA[u][:, :, 0:HW],
                                               scalar=unscale[:, bass.ds(t, 1)],
                                               in1=bias_qkv.rearrange("p (h n) -> p h n", h=2),
                                               op0=ALU.mult, op1=ALU.add).then_inc(qkv_done, 1)

            for g in range(2):
                for t in range(GROUPS[g][1]):
                    stats(g, GROUPS[g][0] + t)
                invert(g)
            dve.wait_ge(wa_in, 48)
            rest = [(g, n) for g in (2, 3) for n in range(GROUPS[g][0], sum(GROUPS[g]))]
            for n in range(GROUPS[2][0], GROUPS[2][0] + 4):
                stats(*rest.pop(0))
            for t in range(8):
                for g, (a, _) in enumerate(GROUPS):
                    if t == a:
                        dve.wait_ge(stat_done, ST * (g + 1))
                evacuate(t // 2, t % 2)
                for g, n in rest[4 * t:4 * t + 4]:
                    stats(g, n)
                if t == 1:
                    invert(2)
            invert(3)
            dve.wait_ge(stat_done, ST * 4)
            with dve.Fori(4, FRONT_FROM // 2 - 1) as i:
                evacuate(i, 0)
                evacuate(i, 1)
            evacuate(FRONT_FROM // 2 - 1, 0)

            def ring_item(step, fu, f, late_m, late_u, item):
                s, at = ring_at(step, ("OT", item[1]) if item[0] == "SKIP" else item)
                kind = item[0]
                if kind == "C" and CHUNKS[item[2]][3]:
                    wait_apart(dve, full[s], at + 1)
                else:
                    dve.wait_ge(full[s], at + 1)
                if kind == "T":
                    _, c, h = item
                    q0 = c * 1024 + h * 512
                    nc.vector.tensor_copy(QT[0:W, fu, q0:q0 + 512], psM[0:W, s, :]).then_inc(free[s], 1)
                elif kind == "C":
                    _, c, k = item
                    qb, k0, n, diag = CHUNKS[k]
                    if k == 0 and not (isinstance(f, int) and f == 0):
                        wait_apart(dve, nm_done, 4 * (f - 1) + c + 1)
                    acc = mx[:, c, qb, k0 // 512:k0 // 512 + 1]
                    if diag:
                        nc.vector.tensor_tensor_reduce(psM[:, s, 0:n], psM[:, s, 0:n], maskrow[:, 512 - n:512], 1.0, MASKED,
                                                       ALU.add, ALU.max, acc).then_inc(free[s], 1)
                    else:
                        nc.vector.tensor_reduce(acc, psM[:, s, 0:n], AX.X, ALU.max).then_inc(free[s], 1)
                    if k == 11:
                        for kk in (9, 10, 11):
                            ss, aa = ring_at(step, ("C", c, kk))
                            dve.wait_ge(free[ss], aa + 1)
                        nc.vector.tensor_reduce(nm[:, c, :], mx[:, c, :, :], AX.X, ALU.max, negate=True).then_inc(nm_done, 1)
                elif kind == "MT":
                    nc.vector.tensor_copy(mT[:, item[1], :], psM[0:24, s, 0:P]).then_inc(free[s], 1)
                elif kind == "S":
                    nc.vector.tensor_reduce(count[:, :], psM[:, s, 0:96].rearrange("p (c n) -> p c n", c=3), AX.X, ALU.add
                                            ).then_inc(free[s], 1)
                elif kind == "OT":
                    normalise(late_m, late_u, item[1], s)
                else:
                    nc.vector.tensor_copy(skipped[:, s:s + 1], psM[0:24, s, 0:1]).then_inc(free[s], 1)

            def normalise(m, u, h, s):
                o = psM[:, s, :].rearrange("p (n c w) -> p n c w", n=4, c=4)
                nc.vector.reciprocal(rden[:, h], o[:, :, :, D]).then_inc(rden_done, 1)
                dve.wait_ge(rden_done, 4 * m + 2 * u + h + 1)
                if h == 0:
                    dve.wait_ge(sa_st[u], 16 * (m + 1))
                nc.vector.tensor_tensor(pmo[:, u, :, 4 * h:4 * h + 4, :].rearrange("p c n d -> p n c d"), o[:, :, :, 0:D],
                                        rden[:, h].unsqueeze(3).to_broadcast([P, 4, 4, D]), ALU.mult).then_inc(free[s], 1)

            for t in range(FRONT_FROM, NT):
                for k, item in enumerate(BESIDE[t]):
                    if k == 2:
                        evacuate((t - 1) // 2, (t - 1) % 2)
                    ring_item(-1, 0, 0, None, None, item)
            evacuate(NT // 2 - 1, 1)

            def step(ring, where, i, u, late=True, load=True):
                for item in timeline(ring, late, load):
                    if item[0] == "ROUTES":
                        dve.wait_ge(route_in, 16 * B)
                        nc.vector.tensor_reduce(smax[:, :], osb[:, :], AX.X, ALU.max).then_inc(smax_done, 1)
                    if item[0] in ("T", "C", "MT", "OT", "S", "SKIP", "NOP"):
                        ring_item(where, 1 - u, 2 * i + u + 1, i if u else i - 1, 1 - u, item)

            step(ring_second[0], (0, 0), 0, 0, late=False)
            step(ring_second[1], (0, 1), 0, 1)
            with dve.Fori(1, NQ // 2 - 1) as i:
                step(ring_steady, (i, 0), i, 0)
                step(ring_steady, (i, 1), i, 1)
            li = NQ // 2 - 1
            step(ring_before, (li, 0), li, 0, load=False)
            step(ring_last, NQ - 1, li, 1, load=False)
            for h in range(2):
                s, at = final_ot(h)
                dve.wait_ge(full[s], at + 1)
                normalise(NQ // 2 - 1, 1, h, s)

            dve.wait_ge(na_in, 16)
            hi, lo, score = na_all[:, :, 0], nlo_all[:, :], s_tok[:, :].rearrange("p (b k) -> p b k", k=8)
            by_batch = lambda y: y.rearrange("p (b k) -> p b k", k=8)
            wide = lambda y: y.unsqueeze(2).to_broadcast([P, B, 8])

            def then(ins, n):
                ins.then_inc(sl, 1)
                dve.wait_ge(sl, n)

            nc.vector.tensor_tensor(kth[:, :], na_all[:, :, 1], hi, ALU.min).then_inc(sl, 1)
            nc.vector.tensor_tensor(by_batch(key[:, :]), score, wide(hi), ALU.min).then_inc(sl, 1)
            then(nc.vector.tensor_scalar(nlo_all[:, :], hi, EPS_ROUTE * EXP_FLOOR, None, ALU.add), 3)
            nc.vector.tensor_tensor(kth[:, :], kth[:, :], lo, ALU.max).then_inc(sl, 1)
            then(nc.vector.tensor_tensor(by_batch(key[:, :]), by_batch(key[:, :]), wide(lo), ALU.max), 5)
            nc.vector.tensor_tensor(by_batch(above[:, 0, :]), by_batch(key[:, :]), wide(kth[:, :]), ALU.is_gt).then_inc(sl, 1)
            nc.vector.tensor_tensor(by_batch(above[:, 1, :]), by_batch(key[:, :]), wide(kth[:, :]), ALU.is_equal).then_inc(sl, 1)

            def choose():
                dve.wait_ge(ties_ps, 1)
                then(nc.vector.tensor_reduce(total_above[:, :], by_batch(psS[:, 256:256 + NT]), AX.X, ALU.add), 8)
                then(nc.vector.tensor_scalar(room[:, :], total_above[:, :], -1.0, float(NUM_HEAVY), ALU.mult, ALU.add), 9)
                then(nc.vector.tensor_tensor(by_batch(chosen[:, :]), by_batch(psS[:, 320:320 + NT]), wide(room[:, :]),
                                             ALU.is_lt), 10)
                then(nc.vector.tensor_tensor(chosen[:, :], chosen[:, :], above[:, 1, :], ALU.mult), 11)
                nc.vector.tensor_tensor(chosen[:, :], chosen[:, :], above[:, 0, :], ALU.add).then_inc(sl, 1)

            def number():
                dve.wait_ge(slot_ps, 1)
                then(nc.vector.scalar_tensor_tensor(out=slot[:, :], in0=psS[:, 352:352 + NT], scalar=1.0, in1=chosen[:, :],
                                                    op0=ALU.add, op1=ALU.mult), 13)
                then(nc.vector.tensor_scalar(slot[:, :], slot[:, :], -1.0, None, ALU.add), 14)

            def unit(i, u, tiles=range(4)):
                for t in tiles:
                    n = 8 * i + 4 * u + t
                    if t == 0:
                        dve.wait_ge(c_x, 2 * i + u + 1)
                        if not (isinstance(i, int) and i == 0):
                            dve.wait_ge(out_st[u], 16 * i)
                    dve.wait_ge(o_ps, n + 1)
                    nc.vector.tensor_tensor(ob[:, u, t, :], psC[:, t % 2, 0:E], x_in2[:, u, t, :], ALU.add
                                            ).then_inc(ob_done, 1)

            def one_hots(b):
                for k in range(8):
                    nc.vector.tensor_scalar(hotb[:, bass.ds(8 * b + k, 1), :].rearrange("p a n -> p (a n)"), iota256[:, :],
                                            slot[:, bass.ds(8 * b + k, 1)], None, ALU.is_equal).then_inc(hot_done, 1)

            unit(0, 0)
            choose()
            unit(0, 1)
            dve.wait_ge(consts, N_CONST)
            number()
            with dve.Fori(1, B - 1) as i:
                for u in range(2):
                    unit(i, u)
                    one_hots(2 * (i - 1) + u)
            dve.wait_ge(idx_ps, 1)
            ip = psS[:, 384:384 + 2 * NSLOT].rearrange("p (s w) -> p s w", w=2)
            nc.vector.tensor_scalar(idxf[:, :], ip[:, :, 0], float(P), None, ALU.mult).then_inc(idx_done, 1)
            dve.wait_ge(idx_done, 1)
            nc.vector.tensor_tensor(idx[:, :], idxf[:, :], ip[:, :, 1], ALU.add).then_inc(idx_done, 1)
            unit(B - 1, 0)

            def gathered_stats(h):
                for t in range(4):
                    st = 4 * h + t
                    dve.wait_ge(g_in[st], 16)
                    nc.vector.bn_stats(bn6[:, st, :], xg[:, st, :]).then_inc(gx_done, 1)
                    dve.wait_ge(gx_done, 9 * h + 2 * t + 1)
                    nc.vector.bn_aggr(mv[:, st, :], bn6[:, st, :]).then_inc(gx_done, 1)

            def gathered_invert(h):
                dve.wait_ge(gp_done, ST * h + 5)
                nc.vector.reciprocal(rnrm[:, 4 * h:4 * h + 4], nrm[:, 4 * h:4 * h + 4]).then_inc(gx_done, 1)

            def gathered_normalise(h):
                dve.wait_ge(gp_done, ST * (h + 1))
                for t in range(4):
                    st = 4 * h + t
                    nc.vector.tensor_scalar(xgn[:, st, :], xg[:, st, :], xscale[:, st:st + 1], xshift[:, st:st + 1],
                                            ALU.mult, ALU.add).then_inc(gn_done, 1)

            gathered_stats(0)
            unit(B - 1, 1, range(2))
            gathered_invert(0)
            unit(B - 1, 1, range(2, 4))
            gathered_normalise(0)
            gathered_stats(1)
            gathered_invert(1)
            gathered_normalise(1)
            for st in range(NSLOT):
                dve.wait_ge(gn_done, st + 1)
                nc.vector.tensor_tensor_reduce(xg[:, st, :], xgn[:, st, :], rt_row, 1.0, 0.0, ALU.mult, ALU.add,
                                               gdot[:, st:st + 1]).then_inc(gu_done, 1)
            dve.wait_ge(gu_done, NSLOT)
            for st in range(NSLOT):
                nc.vector.tensor_scalar(gu[:, st:st + 1], gdot[:, st:st + 1], unscale[:, st:st + 1],
                                        na_all[:, st // 2, 0:1], ALU.mult, ALU.subtract).then_inc(gu_done, 1)
            dve.wait_ge(gu_done, 2 * NSLOT)
            nc.vector.tensor_scalar(gu[:, :], gu[:, :], 0.0, None, ALU.min).then_inc(gu_done, 1)
            dve.wait_ge(gs_done, 1)
            nc.vector.tensor_scalar(gw[:, :], gscore[:, :], -1.0, 1.0, ALU.mult, ALU.add).then_inc(gu_done, 1)
            dve.wait_ge(gu_done, 2 * NSLOT + 2)
            nc.vector.tensor_tensor(gw[:, :], gw[:, :], gscore[:, :], ALU.add).then_inc(gu_done, 1)
            dve.wait_ge(gu_done, 2 * NSLOT + 3)
            for st in range(NSLOT):
                t = st % 4
                dve.wait_ge(ho_ps, st + 1)
                nc.vector.tensor_tensor(hv[:, st, :], psH[:, t, 0:E], bias_h, ALU.add).then_inc(hv_half, 1)
                dve.wait_ge(hv_half, st + 1)
                nc.vector.tensor_scalar(hv[:, st, :], hv[:, st, :], gw[:, st:st + 1], None, ALU.mult).then_inc(hv_done, 1)

        @block.gpsimd
        def _(pool):
            def const(ins):
                ins.then_inc(consts, 1)

            const(pool.memset(ident[:, :], 1.0))
            pool.wait_ge(consts, 1)
            const(pool.affine_select(out=ident[:, :], in_=ident[:, :], pattern=[[-1, P]], compare_op=ALU.is_equal,
                                     fill=0.0, base=0, channel_multiplier=1))
            const(pool.memset(halfpow[:, 0, :], -0.5))
            const(pool.memset(halfpow[:, 1, :], 0.5))
            pool.wait_ge(consts, 4)

            def factors(a, n, base, done, size):
                var, mean = mv[:, a:a + n, 1], mv[:, a:a + n, 0]
                c = slice(a, a + n)

                def then(ins, k):
                    ins.then_inc(done, 1)
                    pool.wait_ge(done, base + k)

                pool.tensor_scalar(veps[:, 0, c], var, EPS_LN, None, ALU.add).then_inc(done, 1)
                then(pool.tensor_scalar(veps[:, 1, c], var, VAR_FLOOR, None, ALU.max), 2)
                then(pool.tensor_tensor(roots[:, :, c], veps[:, :, c], halfpow[:, :, c], ALU.pow), 3)
                then(pool.tensor_tensor(nrm[:, c], roots[:, 0, c], roots[:, 1, c], ALU.mult), 4)
                then(pool.tensor_scalar(nrm[:, c], nrm[:, c], float(E) ** 0.5, 1e-12, ALU.mult, ALU.max), 5)
                pool.tensor_scalar(unscale[:, c], nrm[:, c], float(E) ** -0.5, None, ALU.mult).then_inc(done, 1)
                pool.wait_ge(*size)
                then(pool.tensor_tensor(xscale[:, c], roots[:, 0, c], rnrm[:, c], ALU.mult), 7)
                then(pool.tensor_scalar(xscale[:, c], xscale[:, c], float(E) ** 0.5, None, ALU.mult), 8)
                then(pool.tensor_tensor(xshift[:, c], mean, xscale[:, c], ALU.mult), 9)
                then(pool.tensor_scalar(xshift[:, c], xshift[:, c], -1.0, None, ALU.mult), 10)

            for g, (a, n) in enumerate(GROUPS):
                pool.wait_ge(bn_done, 2 * (a + n))
                factors(a, n, ST * g, stat_done, (nrm_inv, g + 1))
                pool.sem_inc(group_of, n)

            const(pool.memset(maskrow[:, :], 0.0))
            const(pool.memset(earlier[:, :], 1.0))
            const(pool.memset(ones[:, :], 1.0))
            pool.wait_ge(consts, 7)
            const(pool.affine_select(out=maskrow[:, 512 - P:512], in_=maskrow[:, 512 - P:512], pattern=[[-1, P]],
                                     compare_op=ALU.is_ge, fill=MASKED, base=0, channel_multiplier=1))
            const(pool.affine_select(out=earlier[:, :], in_=earlier[:, :], pattern=[[1, P]], compare_op=ALU.is_gt,
                                     fill=0.0, base=0, channel_multiplier=-1))
            const(pool.iota(iota_i[:, :], pattern=[[1, NUM_HEAVY]], base=0, channel_multiplier=0))
            const(pool.iota(tokid_i[:, 0, :], pattern=[[1, NT]], base=0, channel_multiplier=0))
            const(pool.iota(tokid_i[:, 1, :], pattern=[[0, NT]], base=0, channel_multiplier=1))
            pool.wait_ge(consts, 12)
            const(pool.tensor_copy(iota256[:, :], iota_i[:, :]))
            const(pool.tensor_copy(tokid[:, :, :], tokid_i[:, :, :]))

            def second(i, u, t):
                q = 2 * i + u
                pool.wait_ge(cast_done, 2 * q + 1 + t)
                x_ = pm[:, u, :, t * D:(t + 1) * D].unsqueeze(2).to_broadcast([P, 32, 2, D])
                p1 = partsb[:, u, :, 2:3, :, t].to_broadcast([P, 32, 2, D])
                dst = partsb[:, u, :, 3:6:2, :, t] if t == 0 else partsb[:, u, :, 1:6:4, :, t]
                pool.tensor_tensor(dst, x_, p1, ALU.subtract).then_inc(split_done, 1)

            def rest(i, u):
                pool.tensor_tensor(r1[:, :, :].rearrange("p n (t e) -> p n t e", t=2),
                                   pm[:, u, :, 0:2 * D].rearrange("p n (t e) -> p n t e", t=2),
                                   partsb[:, u, :, 2, :, :].rearrange("p n e t -> p n t e"), ALU.subtract).then_inc(split_done, 1)

            def third(i, u, t):
                pool.wait_ge(split_done, 5 * (2 * i + u) + 3)
                pool.tensor_tensor(partsb[:, u, :, 4 if t == 0 else 0, :, t], r1[:, :, t * D:(t + 1) * D],
                                   partsb[:, u, :, 5, :, t], ALU.subtract).then_inc(split_done, 1)

            def split(u):
                second(0, u, 0)
                second(0, u, 1)
                if u == 1:
                    pool.wait_ge(split_done, 5)
                rest(0, u)
                third(0, u, 0)
                third(0, u, 1)

            def maxima(f, c):
                wait_apart(pool, nm_done, 4 * f + c + 1)
                at = 4 * (4 * f + c)
                p = [mWb[:, c, k, :, 0] for k in range(3)]
                pool.tensor_copy(p[0], nm[:, c, :]).then_inc(mw_done, 1)
                pool.wait_ge(mw_done, at + 1)
                pool.tensor_tensor(p[1], nm[:, c, :], p[0], ALU.subtract).then_inc(mw_done, 1)
                pool.tensor_tensor(nmr[:, c, :], nm[:, c, :], p[0], ALU.subtract).then_inc(mw_done, 1)
                pool.wait_ge(mw_done, at + 3)
                pool.tensor_tensor(p[2], nmr[:, c, :], p[1], ALU.subtract).then_inc(mw_done, 1)

            def search(step_, r):
                s, at = ring_at(step_, ("S", r))
                pool.wait_ge(free[s], at + 1)

                def then(ins, n):
                    ins.then_inc(th, 1)
                    pool.wait_ge(th, search_steps(r) + n)

                if r == 0:
                    then(pool.tensor_scalar(passed[:, :], count[:, 0:1], NUM_HEAVY - 0.5, None, ALU.is_ge), 1)
                    pool.tensor_scalar(sign[:, :], passed[:, :], 2.0, -1.0, ALU.mult, ALU.add).then_inc(th, 1)
                    then(pool.tensor_scalar(wanted[:, :], passed[:, :], float(2 * NUM_HEAVY - S - 1), S - NUM_HEAVY + 0.5,
                                            ALU.mult, ALU.add), 3)
                    then(pool.tensor_scalar(signed[:, :], rs[:, :], sign[:, :], None, ALU.mult), 4)
                else:
                    then(pool.tensor_scalar(step_up[:, :], count[:, :], wanted[:, :], float(1 << (32 - 2 * r)),
                                            ALU.is_ge, ALU.mult), 1)
                    for n in range(3):
                        then(pool.tensor_tensor(found[:, :], found[:, :], step_up[:, n:n + 1], ALU.add), 2 + n)
                if r < ROUNDS - 1:
                    then(pool.tensor_tensor(candidate[:, :], bits[:, r + 1, :], found[:, :].to_broadcast([P, 3]), ALU.add), 5)
                    for n in range(3):
                        pool.tensor_scalar(reach[:, n, :], signed[:, :], candidate[:, n:n + 1].bitcast(F32), None, ALU.is_ge
                                           ).then_inc(th, 1)

            split(0)
            for n in range(1, ROUNDS):
                for k in range(3):
                    b = (k + 1) << (32 - 2 * n) if n > 1 or k == 0 else 0x7F7FFFFF
                    ins = pool.memset(bits[:, n, k:k + 1], b)
            ins.then_inc(th, 1)
            pool.memset(found[:, :], 0).then_inc(th, 1)
            pool.wait_ge(wc_in, 16 * 6)
            for k in range(KE):
                pool.tensor_scalar(w1l[:, k, :], w1l[:, k, :], gl[:, k:k + 1], None, ALU.mult).then_inc(fold_done, 1)
                pool.tensor_scalar(w1h[:, k, :], w1h[:, k, :], gh[:, k:k + 1], None, ALU.mult).then_inc(fold_done, 1)
            pool.wait_ge(dconst, N_DCONST)
            maxima(0, 0)
            split(1)
            maxima(0, 1)
            maxima(0, 2)

            def route_z(r):
                wait_apart(pool, rz_done, 4 * r + 1)
                pool.tensor_scalar(rm[:, 0:1], na[:, :], smax[:, :], None, ALU.min).then_inc(rz_done, 1)
                wait_apart(pool, rz_done, 4 * r + 2)
                pool.tensor_scalar(rz[:, :], rs[:, :], na[:, :], rm[:, 0:1], ALU.min, ALU.subtract).then_inc(rz_done, 1)
                pool.tensor_scalar(rm[:, 1:2], rm[:, 0:1], C_ROUTE, None, ALU.subtract).then_inc(rz_done, 1)

            def route_a(step_, k, r):
                s, at = ring_at(step_, ("R", k))
                pool.wait_ge(free[s], at + 1)
                wait_apart(pool, rz_done, 4 * r + 4)
                pool.tensor_scalar(na[:, :], lns[:, :], EPS_ROUTE, rm[:, 1:2], ALU.mult, ALU.add).then_inc(rz_done, 1)

            def routes():
                pool.wait_ge(smax_done, 1)
                pool.memset(na[:, :], 0.0).then_inc(rz_done, 1)
                route_z(0)
                pool.wait_ge(rs_in, 16)
                pool.tensor_scalar(reach[:, :, :], rs[:, :].unsqueeze(1).to_broadcast([P, 3, 32]), 0.0, None, ALU.is_ge
                                   ).then_inc(th, 1)

            def causal(i, u, kb):
                wait_apart(pool, exp_done, NE * (2 * i + u) + EXPS_OF[kb])
                diag = strip_at[kb][:, :, 0:P]
                pool.affine_select(out=diag, in_=diag, pattern=[[0, 4], [1, P]], compare_op=ALU.is_ge, fill=0.0,
                                   base=0, channel_multiplier=-1).then_inc(mask_done, 1)

            def sub(i, u, k):
                if k < 2:
                    second(i, u, k)
                elif k == 2:
                    pool.wait_ge(split_done, 5 * (2 * i + u) + 2)
                    rest(i, u)
                else:
                    third(i, u, k - 3)

            def step(ring, where, i, u, late=True, load=True):
                f, r = 2 * i + u + 1, 6 * i + 3 * u
                for item in timeline(ring, late, load):
                    if item[0] == "MAX":
                        maxima(f - 1 if item[1] == 3 else f, item[1])
                    elif item[0] == "CAUSAL":
                        causal(i, u, item[1])
                    elif item[0] == "SUB":
                        sub(i + 1, u, item[1])
                    elif item[0] == "RA":
                        route_a(where, item[1], r + item[1])
                        if not (isinstance(i, int) and r + item[1] == N_ITERS - 1):
                            route_z(r + item[1] + 1)
                    elif item[0] == "ROUTES":
                        routes()
                    elif item[0] == "S":
                        search(where, item[1])

            step(ring_second[0], (0, 0), 0, 0, late=False)
            step(ring_second[1], (0, 1), 0, 1)
            with pool.Fori(1, NQ // 2 - 1) as i:
                step(ring_steady, (i, 0), i, 0)
                step(ring_steady, (i, 1), i, 1)
            li = NQ // 2 - 1
            step(ring_before, (li, 0), li, 0, load=False)
            step(ring_last, NQ - 1, li, 1, load=False)
            pool.wait_ge(th, search_steps(ROUNDS) - 4)
            pool.tensor_scalar(route[:, 1:2], found[:, :].bitcast(F32), sign[:, :], None, ALU.mult).then_inc(th, 1)

            def unit(i, u):
                pool.wait_ge(c_x_in[u], 16 * (i + 1))
                pool.tensor_tensor(x_in2[:, u], x_in2[:, u], bias_o[:, 0:1, :].to_broadcast([P, 4, E]), ALU.add).then_inc(c_x, 1)

            pool.wait_ge(wd_in, 16 * 7)
            pool.tensor_tensor(bias_o[:, 0, :], bias_o[:, 0, :], bias_o[:, 1, :], ALU.add).then_inc(fold_done, 1)
            pool.wait_ge(fold_done, N_FOLD)
            with pool.Fori(0, B - 1) as i:
                unit(i, 0)
                unit(i, 1)
            unit(B - 1, 0)

            def gather(h):
                for st in range(4 * h, 4 * h + 4):
                    pool.indirect_dma_start(out=xg[:, st, :], out_offset=None, in_=xf,
                                            in_offset=bass.IndirectOffsetOnAxis(ap=idx[:, st:st + 1], axis=0)).then_inc(g_in[st], 16)

            def gathered_factors(h):
                pool.wait_ge(gx_done, 9 * h + 8)
                factors(4 * h, 4, ST * h, gp_done, (gx_done, 9 * h + 9))

            pool.wait_ge(idx_done, 2)
            gather(0)
            unit(B - 1, 1)
            gathered_factors(0)
            gather(1)
            gathered_factors(1)
            pool.wait_ge(out_st[0], 16 * B)
            pool.wait_ge(out_st[1], 16 * B)
            for st in range(NSLOT):
                pool.wait_ge(hv_done, st + 1)
                pool.indirect_dma_start(out=of, out_offset=bass.IndirectOffsetOnAxis(ap=idx[:, st:st + 1], axis=0),
                                        in_=hv[:, st, :], in_offset=None, compute_op=ALU.add).then_inc(add_st[st], 16)
            for st in range(NSLOT):
                pool.wait_ge(add_st[st], 16)


_INS = ['L0_attn_inputs', 'L0_attn_W_qkv', 'L0_attn_b_qkv', 'L0_attn_W_out', 'L0_attn_b_out', 'L0_ffn_routing_token',
        'L0_ffn_gamma_light', 'L0_ffn_w1_light', 'L0_ffn_b1_light', 'L0_ffn_w2_light', 'L0_ffn_b2_light',
        'L0_ffn_gamma_heavy', 'L0_ffn_w1_heavy', 'L0_ffn_b1_heavy', 'L0_ffn_w2_heavy', 'L0_ffn_b2_heavy']
_OUTS = [((4, 1024, 256), 'float32')]


def kernel(**inputs):
    import numpy as _np
    import concourse.bacc as _bacc
    from concourse import mybir as _mybir
    from concourse.bass_utils import run_bass_kernel_spmd as _run

    nc = _bacc.Bacc("TRN2", target_bir_lowering=False, num_devices=1)
    arrays, args = {}, []
    for name in _INS:
        a = _np.ascontiguousarray(inputs[name])
        arrays[f"in_{name}"] = a
        args.append(nc.dram_tensor(f"in_{name}", a.shape, _mybir.dt.from_np(a.dtype), kind="ExternalInput").ap())
    for i, (shape, dtype) in enumerate(_OUTS):
        dt = _mybir.dt.from_np(_np.dtype(dtype))
        args.append(nc.dram_tensor(f"out_{i}", shape, dt, kind="ExternalOutput").ap())
    layer_kernel(nc, *args)
    r = _run(nc, [arrays], core_ids=[0])
    return r.results[0]["out_0"]
```
